# Optimizing a Trainium2 kernel written in Bass

```python
import numpy as np
import jax
import jax.numpy as jnp

def _softmax(x, axis=-1):
    return jax.nn.softmax(x, axis=axis)

def _gelu(x):
    return jax.nn.gelu(x, approximate=True)

def _silu(x):
    return jax.nn.silu(x)

def _sigmoid(x):
    return jax.nn.sigmoid(x)

def _layernorm(x, axis=-1, eps=1e-05):
    m = jnp.mean(x, axis=axis, keepdims=True)
    v = jnp.var(x, axis=axis, keepdims=True)
    return (x - m) / jnp.sqrt(v + eps)

def _scatter_add(tgt, idx, src, axis=0):
    return tgt.at[idx].add(src)

def _segment_sum(src, seg, n):
    return jax.ops.segment_sum(src, seg, n)
kernel_name = 'mk_gnn_preln_d4_gnn_r32_5544d8'

def setup_inputs(seed: int=0):
    np.random.seed(seed)
    _w = jnp.asarray

    def _rec_inputs():
        import jax
        import jax.numpy as jnp
        _gk = jax.random.key(seed)
        x = 0.0007147 + 1 * jax.random.normal(jax.random.fold_in(_gk, 1), (50000, 64), jnp.float32)
        src = jax.random.randint(jax.random.fold_in(_gk, 2), (50000,), 0, 50000, jnp.int32)
        dst = jax.random.randint(jax.random.fold_in(_gk, 3), (50000,), 0, 50000, jnp.int32)
        _o = jnp.argsort(dst, stable=True)
        src = src[_o]
        dst = dst[_o]
        edge_attr_32 = 0.000196303 + 1.00016 * jax.random.normal(jax.random.fold_in(_gk, 13), (50000, 32), jnp.float32)
        edge_type_2 = jax.random.randint(jax.random.fold_in(_gk, 15), (50000,), 0, 2, jnp.int32)
        edge_type_9 = jax.random.randint(jax.random.fold_in(_gk, 16), (50000,), 0, 9, jnp.int32)
        node_type_2 = jax.random.randint(jax.random.fold_in(_gk, 17), (50000,), 0, 2, jnp.int32)
        return (x, src, dst, edge_attr_32, edge_type_2, edge_type_9, node_type_2)
    x, src, dst, edge_attr_32, edge_type_2, edge_type_9, node_type_2 = _rec_inputs()

    def _L0_gnn_setup():
        import jax, jax.numpy as jnp
        import numpy as np
        N = 50000
        R = 9
        E = 64
        L = 3
        G = 2 * R
        N_EDGES = 25000
        key = jax.random.key(seed)
        k0, k1, k2, k3, k4 = jax.random.split(key, 5)
        edge_index = jax.random.randint(k0, (2, N_EDGES), 0, N, dtype=jnp.int32)
        edge_type = jax.random.randint(k1, (N_EDGES,), 0, R, dtype=jnp.int32)
        emb = jax.random.normal(k2, (N, E), dtype=jnp.float32)
        weights = jax.random.normal(k3, (L, G, E, E), dtype=jnp.float32) / np.sqrt(E)
        biases = jax.random.normal(k4, (L, G, E), dtype=jnp.float32) * 0.1
        return {'emb': emb, 'weights': weights, 'biases': biases, 'edge_index': edge_index, 'edge_type': edge_type}
    _L0_gnn_all = _L0_gnn_setup()
    _L0_gnn_in = {k: v for k, v in _L0_gnn_all.items() if k in ('weights', 'biases')}
    del _L0_gnn_all

    def _L1_gnn_setup():
        import jax, jax.numpy as jnp
        import numpy as np
        N_NODES = 50000
        N_EDGES = 25000
        IN_CH = 64
        HID = 128
        EPS_BN = 1e-05
        LEAKY_SLOPE = 0.01

        def _gcn_conv(x, src, dst, dinv, W, b, n_nodes):
            h = x @ W
            norm = dinv[src] * dinv[dst]
            msg = h[src] * norm[:, None]
            out = jax.ops.segment_sum(msg, dst, num_segments=n_nodes)
            return out + b

        def _batchnorm(x, gamma, beta):
            mean = jnp.mean(x, axis=0)
            var = jnp.mean(jnp.square(x - mean), axis=0)
            return (x - mean) * jax.lax.rsqrt(var + EPS_BN) * gamma + beta

        def _leaky_relu(x):
            return jnp.where(x > 0, x, LEAKY_SLOPE * x)
        key = jax.random.key(seed)
        ks = jax.random.split(key, 8)
        x = jax.random.normal(ks[0], (N_NODES, IN_CH), dtype=jnp.float32)
        edge_index = jax.random.randint(ks[1], (2, N_EDGES), 0, N_NODES, dtype=jnp.int32)
        W1 = jax.random.normal(ks[2], (IN_CH, HID), dtype=jnp.float32) / np.sqrt(IN_CH)
        W2 = jax.random.normal(ks[3], (HID, HID // 2), dtype=jnp.float32) / np.sqrt(HID)
        W3 = jax.random.normal(ks[4], (HID // 2, IN_CH), dtype=jnp.float32) / np.sqrt(HID // 2)
        return {'x': x, 'edge_index': edge_index, 'W1': W1, 'b1': jnp.zeros((HID,), jnp.float32), 'g1': jnp.ones((HID,), jnp.float32), 'be1': jnp.zeros((HID,), jnp.float32), 'W2': W2, 'b2': jnp.zeros((HID // 2,), jnp.float32), 'g2': jnp.ones((HID // 2,), jnp.float32), 'be2': jnp.zeros((HID // 2,), jnp.float32), 'W3': W3, 'b3': jnp.zeros((IN_CH,), jnp.float32)}
    _L1_gnn_all = _L1_gnn_setup()
    _L1_gnn_in = {k: v for k, v in _L1_gnn_all.items() if k in ('W1', 'b1', 'g1', 'be1', 'W2', 'b2', 'g2', 'be2', 'W3', 'b3')}
    del _L1_gnn_all

    def _L2_gnn_setup():
        import jax, jax.numpy as jnp
        import numpy as np
        N, E = (50000, 25000)
        IN, H, D = (64, 4, 16)
        NT, ET = (2, 2)

        def _typed_linear(x, W, types):
            y_all = jnp.einsum('ni,tio->tno', x, W)
            return y_all[types, jnp.arange(x.shape[0])]
        key = jax.random.key(seed)
        ks = jax.random.split(key, 13)
        s = 0.05
        return {'x': jax.random.normal(ks[0], (N, IN), jnp.float32), 'Wk': jax.random.normal(ks[1], (NT, IN, H * D), jnp.float32) * s, 'Wq': jax.random.normal(ks[2], (NT, IN, H * D), jnp.float32) * s, 'Wv': jax.random.normal(ks[3], (NT, IN, H * D), jnp.float32) * s, 'Wa': jax.random.normal(ks[4], (NT, H * D, H * D), jnp.float32) * s, 'Ratt': jax.random.normal(ks[5], (H, ET, D, D), jnp.float32) * s, 'Rmsg': jax.random.normal(ks[6], (H, ET, D, D), jnp.float32) * s, 'pri': jnp.ones((H, ET), jnp.float32), 'skip': jnp.ones((NT,), jnp.float32), 'ntype': jax.random.randint(ks[7], (N,), 0, NT), 'etype': jax.random.randint(ks[8], (E,), 0, ET), 'src': jax.random.randint(ks[9], (E,), 0, N), 'dst': jax.random.randint(ks[10], (E,), 0, N)}
    _L2_gnn_all = _L2_gnn_setup()
    _L2_gnn_in = {k: v for k, v in _L2_gnn_all.items() if k in ('Wk', 'Wq', 'Wv', 'Wa', 'Ratt', 'Rmsg', 'pri', 'skip')}
    del _L2_gnn_all

    def _L3_gnn_setup():
        import jax, jax.numpy as jnp
        import numpy as np
        N, E, G = (50000, 25000, 16)
        F_X, F_E, F_U = (64, 32, 64)
        H1, H2, H3 = (128, 64, 64)

        def _lin_init(key, fan_in, fan_out):
            kw, kb = jax.random.split(key)
            bound = 1.0 / np.sqrt(fan_in)
            W = jax.random.uniform(kw, (fan_in, fan_out), jnp.float32, -bound, bound)
            b = jax.random.uniform(kb, (fan_out,), jnp.float32, -bound, bound)
            return (W, b)
        key = jax.random.key(seed)
        ks = jax.random.split(key, 9)
        x = jax.random.normal(ks[0], (N, F_X), jnp.float32)
        edge_index = jax.random.randint(ks[1], (2, E), 0, N, jnp.int32)
        edge_attr = jax.random.normal(ks[2], (E, F_E), jnp.float32)
        u = jax.random.normal(ks[3], (G, F_U), jnp.float32)
        batch = jnp.sort(jax.random.randint(ks[4], (N,), 0, G, jnp.int32))
        W1, b1 = _lin_init(ks[5], F_X + F_E, H1)
        W2, b2 = _lin_init(ks[6], H1, H2)
        W3, b3 = _lin_init(ks[7], H2 + F_X + F_U, H2)
        W4, b4 = _lin_init(ks[8], H2, H3)
        return {'x': x, 'edge_index': edge_index, 'edge_attr': edge_attr, 'u': u, 'batch': batch, 'W1': W1, 'b1': b1, 'W2': W2, 'b2': b2, 'W3': W3, 'b3': b3, 'W4': W4, 'b4': b4}
    _L3_gnn_all = _L3_gnn_setup()
    _L3_gnn_in = {k: v for k, v in _L3_gnn_all.items() if k in ('u', 'W1', 'b1', 'W2', 'b2', 'W3', 'b3', 'W4', 'b4')}
    del _L3_gnn_all
    return {'x': x, 'src': src, 'dst': dst, 'edge_attr_32': edge_attr_32, 'edge_type_2': edge_type_2, 'edge_type_9': edge_type_9, 'node_type_2': node_type_2, 'L0_gnn_weights': _L0_gnn_in['weights'], 'L0_gnn_biases': _L0_gnn_in['biases'], 'L1_gnn_W1': _L1_gnn_in['W1'], 'L1_gnn_b1': _L1_gnn_in['b1'], 'L1_gnn_g1': _L1_gnn_in['g1'], 'L1_gnn_be1': _L1_gnn_in['be1'], 'L1_gnn_W2': _L1_gnn_in['W2'], 'L1_gnn_b2': _L1_gnn_in['b2'], 'L1_gnn_g2': _L1_gnn_in['g2'], 'L1_gnn_be2': _L1_gnn_in['be2'], 'L1_gnn_W3': _L1_gnn_in['W3'], 'L1_gnn_b3': _L1_gnn_in['b3'], 'L2_gnn_Wk': _L2_gnn_in['Wk'], 'L2_gnn_Wq': _L2_gnn_in['Wq'], 'L2_gnn_Wv': _L2_gnn_in['Wv'], 'L2_gnn_Wa': _L2_gnn_in['Wa'], 'L2_gnn_Ratt': _L2_gnn_in['Ratt'], 'L2_gnn_Rmsg': _L2_gnn_in['Rmsg'], 'L2_gnn_pri': _L2_gnn_in['pri'], 'L2_gnn_skip': _L2_gnn_in['skip'], 'L3_gnn_u': _L3_gnn_in['u'], 'L3_gnn_W1': _L3_gnn_in['W1'], 'L3_gnn_b1': _L3_gnn_in['b1'], 'L3_gnn_W2': _L3_gnn_in['W2'], 'L3_gnn_b2': _L3_gnn_in['b2'], 'L3_gnn_W3': _L3_gnn_in['W3'], 'L3_gnn_b3': _L3_gnn_in['b3'], 'L3_gnn_W4': _L3_gnn_in['W4'], 'L3_gnn_b4': _L3_gnn_in['b4']}

def reference(x, src, dst, edge_attr_32, edge_type_2, edge_type_9, node_type_2, L0_gnn_weights, L0_gnn_biases, L1_gnn_W1, L1_gnn_b1, L1_gnn_g1, L1_gnn_be1, L1_gnn_W2, L1_gnn_b2, L1_gnn_g2, L1_gnn_be2, L1_gnn_W3, L1_gnn_b3, L2_gnn_Wk, L2_gnn_Wq, L2_gnn_Wv, L2_gnn_Wa, L2_gnn_Ratt, L2_gnn_Rmsg, L2_gnn_pri, L2_gnn_skip, L3_gnn_u, L3_gnn_W1, L3_gnn_b1, L3_gnn_W2, L3_gnn_b2, L3_gnn_W3, L3_gnn_b3, L3_gnn_W4, L3_gnn_b4):
    import jax
    import jax.numpy as jnp

    def _L0_gnn_ref(emb, weights, biases, edge_index, edge_type):
        import jax, jax.numpy as jnp
        import numpy as np
        N = 50000
        R = 9
        E = 64
        L = 3
        G = 2 * R
        N_EDGES = 25000
        dst = jnp.concatenate([edge_index[0], edge_index[1]])
        src = jnp.concatenate([edge_index[1], edge_index[0]])
        grp = jnp.concatenate([edge_type, edge_type + R])
        seg = dst * G + grp
        cnt = jax.ops.segment_sum(jnp.ones(src.shape[0], emb.dtype), seg, num_segments=N * G).reshape(N, G)
        x = emb
        for l in range(L):
            xs = x[src]
            A = jax.ops.segment_sum(xs, seg, num_segments=N * G).reshape(N, G, E)
            h = jnp.einsum('nge,gef->nf', A, weights[l]) + cnt @ biases[l]
            x = jax.nn.relu(h) if l + 1 < L else h
        return x

    def _L1_gnn_ref(x, edge_index, W1, b1, g1, be1, W2, b2, g2, be2, W3, b3):
        import jax, jax.numpy as jnp
        import numpy as np
        N_NODES = 50000
        N_EDGES = 25000
        IN_CH = 64
        HID = 128
        EPS_BN = 1e-05
        LEAKY_SLOPE = 0.01

        def _gcn_conv(x, src, dst, dinv, W, b, n_nodes):
            h = x @ W
            norm = dinv[src] * dinv[dst]
            msg = h[src] * norm[:, None]
            out = jax.ops.segment_sum(msg, dst, num_segments=n_nodes)
            return out + b

        def _batchnorm(x, gamma, beta):
            mean = jnp.mean(x, axis=0)
            var = jnp.mean(jnp.square(x - mean), axis=0)
            return (x - mean) * jax.lax.rsqrt(var + EPS_BN) * gamma + beta

        def _leaky_relu(x):
            return jnp.where(x > 0, x, LEAKY_SLOPE * x)
        n = x.shape[0]
        loops = jnp.arange(n, dtype=edge_index.dtype)
        src = jnp.concatenate([edge_index[0], loops])
        dst = jnp.concatenate([edge_index[1], loops])
        deg = jax.ops.segment_sum(jnp.ones_like(src, dtype=x.dtype), dst, num_segments=n)
        dinv = jax.lax.rsqrt(deg)
        h = _gcn_conv(x, src, dst, dinv, W1, b1, n)
        h = _leaky_relu(_batchnorm(h, g1, be1))
        h = _gcn_conv(h, src, dst, dinv, W2, b2, n)
        z = _leaky_relu(_batchnorm(h, g2, be2))
        out = _gcn_conv(z, src, dst, dinv, W3, b3, n)
        return out

    def _L2_gnn_ref(x, Wk, Wq, Wv, Wa, Ratt, Rmsg, pri, skip, ntype, etype, src, dst):
        import jax, jax.numpy as jnp
        import numpy as np
        N, E = (50000, 25000)
        IN, H, D = (64, 4, 16)
        NT, ET = (2, 2)

        def _typed_linear(x, W, types):
            y_all = jnp.einsum('ni,tio->tno', x, W)
            return y_all[types, jnp.arange(x.shape[0])]
        n = x.shape[0]
        k = _typed_linear(x, Wk, ntype).reshape(n, H, D)
        q = _typed_linear(x, Wq, ntype).reshape(n, H, D)
        v = _typed_linear(x, Wv, ntype).reshape(n, H, D)
        katt = jnp.einsum('nhd,htdf->thnf', k, Ratt)
        vmsg = jnp.einsum('nhd,htdf->thnf', v, Rmsg)
        kw = katt[etype, :, src]
        m = vmsg[etype, :, src]
        qd = q[dst]
        a = (kw * qd).sum(-1) * pri[:, etype].T / jnp.sqrt(jnp.float32(D))
        amax = jax.ops.segment_max(a, dst, num_segments=n)
        ae = jnp.exp(a - amax[dst])
        asum = jax.ops.segment_sum(ae, dst, num_segments=n)
        attn = ae / asum[dst]
        h = jax.ops.segment_sum(m * attn[:, :, None], dst, num_segments=n)
        h = _typed_linear(h.reshape(n, H * D), Wa, ntype)
        alpha = jax.nn.sigmoid(skip)[ntype][:, None]
        return h * alpha + x * (1.0 - alpha)

    def _L3_gnn_ref(x, edge_index, edge_attr, u, batch, W1, b1, W2, b2, W3, b3, W4, b4):
        import jax, jax.numpy as jnp
        import numpy as np
        N, E, G = (50000, 25000, 16)
        F_X, F_E, F_U = (64, 32, 64)
        H1, H2, H3 = (128, 64, 64)

        def _lin_init(key, fan_in, fan_out):
            kw, kb = jax.random.split(key)
            bound = 1.0 / np.sqrt(fan_in)
            W = jax.random.uniform(kw, (fan_in, fan_out), jnp.float32, -bound, bound)
            b = jax.random.uniform(kb, (fan_out,), jnp.float32, -bound, bound)
            return (W, b)
        row, col = (edge_index[0], edge_index[1])
        e = jnp.concatenate([x[row], edge_attr], axis=1)
        e = jax.nn.relu(e @ W1 + b1) @ W2 + b2
        s = jax.ops.segment_sum(e, col, num_segments=x.shape[0])
        cnt = jax.ops.segment_sum(jnp.ones((e.shape[0],), e.dtype), col, num_segments=x.shape[0])
        agg = s / jnp.maximum(cnt, 1.0)[:, None]
        h = jnp.concatenate([x, agg, u[batch]], axis=1)
        return jax.nn.relu(h @ W3 + b3) @ W4 + b4
    edge_index = jnp.stack([src, dst])
    batch0 = jnp.zeros((50000,), jnp.int32)
    h = jnp.maximum(_layernorm(x, axis=-1), 0.0)
    x = x + _L0_gnn_ref(h, L0_gnn_weights, L0_gnn_biases, edge_index, edge_type_9)
    h = jnp.maximum(_layernorm(x, axis=-1), 0.0)
    x = x + _L1_gnn_ref(h, edge_index, L1_gnn_W1, L1_gnn_b1, L1_gnn_g1, L1_gnn_be1, L1_gnn_W2, L1_gnn_b2, L1_gnn_g2, L1_gnn_be2, L1_gnn_W3, L1_gnn_b3)
    h = jnp.maximum(_layernorm(x, axis=-1), 0.0)
    x = x + _L2_gnn_ref(h, L2_gnn_Wk, L2_gnn_Wq, L2_gnn_Wv, L2_gnn_Wa, L2_gnn_Ratt, L2_gnn_Rmsg, L2_gnn_pri, L2_gnn_skip, node_type_2, edge_type_2, src, dst)
    h = jnp.maximum(_layernorm(x, axis=-1), 0.0)
    x = x + _L3_gnn_ref(h, edge_index, edge_attr_32, L3_gnn_u, batch0, L3_gnn_W1, L3_gnn_b1, L3_gnn_W2, L3_gnn_b2, L3_gnn_W3, L3_gnn_b3, L3_gnn_W4, L3_gnn_b4)
    return x

_drawn_inputs = setup_inputs


def setup_inputs(seed=0):
    import zlib

    import numpy as np

    out = dict(_drawn_inputs(seed))
    spreads = {'L1_gnn_b1': (0.0, 2.0),
     'L1_gnn_g1': (1.0, 0.2),
     'L1_gnn_be1': (0.0, 0.314),
     'L1_gnn_b2': (0.0, 2.0),
     'L1_gnn_g2': (1.0, 0.2),
     'L1_gnn_be2': (0.0, 0.1),
     'L1_gnn_b3': (0.0, 0.1),
     'L2_gnn_pri': (1.0, 0.6),
     'L2_gnn_skip': (1.0, 0.6)}
    factors = {'edge_attr_32': 8.0,
     'L2_gnn_Wk': 8.0,
     'L2_gnn_Wq': 8.0,
     'L2_gnn_Wv': 8.0,
     'L2_gnn_Wa': 8.0,
     'L2_gnn_Ratt': 8.0,
     'L2_gnn_Rmsg': 8.0,
     'L3_gnn_W1': 8.0,
     'L3_gnn_b1': 28.622,
     'L3_gnn_W2': 7.666,
     'L3_gnn_b2': 64.0,
     'L3_gnn_b3': 30.674,
     'L3_gnn_u': 4.609,
     'L3_gnn_b4': 6.732}
    for name, (base, spread) in spreads.items():
        noise = np.random.default_rng([zlib.crc32(name.encode()), seed]).standard_normal(out[name].shape)
        drawn = base * np.exp(spread * noise) if base else spread * noise
        out[name] = jnp.asarray(drawn.astype(out[name].dtype))
    for name, factor in factors.items():
        out[name] = (out[name] * factor).astype(out[name].dtype)
    return out
```

```python
from contextlib import ExitStack

import concourse.bass as bass
from concourse import mybir

ALU = mybir.AluOpType
ACT = mybir.ActivationFunctionType
F32 = mybir.dt.float32
I32 = mybir.dt.int32
AX = mybir.AxisListType.X

P = 128
N = 50000
D = 64
G7 = 7
SN = G7 * P
NJ = -(-N // SN)
NP = NJ * SN
NT = NP // P
ET = NP // P
EP = ET * P
NR = NP + P
R9 = 9
NPAIR = 5
VALID_LAST = N - (NJ - 1) * SN
HEADS, HD = 4, 16
FE = 32
EPS = 1e-5
LEAK = 0.01
LOWEST = -3.0e38


class Signal:

    def __init__(self, nc, ctx, name):
        self.sem = ctx.enter_context(nc.semaphore(name))
        self.base = 0

    def at(self, n):
        return n + self.base if self.base else n

    def close(self, n):
        self.base += n


class Chain:

    def __init__(self, steps):
        self.steps, self.per, self.n, self.loops = steps, 0, 0, 0

    def turn(self, i):
        if isinstance(i, int) and i == 0:
            self.first = True
        else:
            if self.first:
                self.per, self.first = self.n, False
        self.i, self.n = i, 0

    def link(self, eng, ins):
        self.n += 1
        ins.then_inc(self.steps.sem, 1)
        eng.wait_ge(self.steps.sem, self.steps.at(self.i * self.per + self.n))

    def close(self, turns):
        per = self.n if self.first else self.per
        assert self.first or self.n == self.per
        self.steps.close(per * turns)


def turns(eng, count, body):
    body(0)
    if count > 1:
        with eng.Fori(1, count) as i:
            body(i)
class Env:
    pass


def node_view(table, j, width=None):
    return table[bass.ts(j, SN), :].rearrange("(q p) d -> p q d", p=P)


def bc(ap, n=D):
    return ap.unsqueeze(2).to_broadcast([ap.shape[0], ap.shape[1], n])


def layernorm_relu(nc, g, dve, chain, n, x, xc, sq, st, out):
    s = g.ns
    total, mean, ssq, std, rstd = (st[:, k] for k in range(5))
    chain.link(dve, nc.vector.tensor_reduce(total, x, AX, ALU.add))
    chain.link(dve, nc.vector.tensor_scalar(mean, total, 1.0 / D, None, ALU.mult))
    chain.link(dve, nc.vector.tensor_tensor(xc, x, bc(mean), ALU.subtract))
    chain.link(dve, nc.vector.tensor_tensor(sq, xc, xc, ALU.mult))
    nc.vector.tensor_reduce(ssq, sq, AX, ALU.add).then_inc(s.squares.sem, 1)
    dve.wait_ge(s.root.sem, s.root.at(n + 1))
    chain.link(dve, nc.vector.reciprocal(rstd, std))
    chain.link(dve, nc.vector.tensor_tensor(sq, xc, bc(rstd), ALU.mult))
    return nc.vector.tensor_scalar(out, sq, 0.0, None, ALU.max)


def deviation(nc, g, act, n, st):
    s = g.ns
    act.wait_ge(s.squares.sem, s.squares.at(n + 1))
    nc.scalar.activation(st[:, 3], st[:, 2], ACT.Sqrt, scale=1.0 / D, bias=g.eps[:, 0:1]).then_inc(s.root.sem, 1)


def node_programs(nc, g, block, loads, stores, nl, ns):
    s = g.ns

    @block.sync
    def _(sp):
        def pair(i):
            for h in range(2):
                if not isinstance(i, int):
                    sp.wait_ge(s.stored[h].sem, s.stored[h].at(16 * ns * i)).then_inc(g.sp_gate, 1)
                for dst, src in loads(2 * i + h, h):
                    sp.dma_start(dst, src).then_inc(s.loaded[h].sem, 16)
        turns(sp, NJ // 2, pair)
        for h in range(2):
            sp.wait_ge(s.stored[h].sem, s.stored[h].at(16 * ns * (NJ // 2)))


def node_close(s, nl, ns):
    for h in range(2):
        s.loaded[h].close(16 * nl * (NJ // 2))
        s.stored[h].close(16 * ns * (NJ // 2))


def stage_norm(nc, g, name, first, acc_in, relu_only=False):
    s = g.ns
    with ExitStack() as ctx:
        sb = lambda n, sh, d=F32: ctx.enter_context(nc.sbuf_tensor(f"{name}_{n}", sh, d))
        inp = [sb(f"inp{h}", [P, max(1, len(acc_in)), G7, D]) for h in range(2)]
        out = [sb(f"out{h}", [P, G7, D]) for h in range(2)]
        xc, sq, st = sb("xc", [P, G7, D]), sb("sq", [P, G7, D]), sb("st", [P, 5, G7])
        chain = Chain(s.chain)
        zeroed = acc_in or g.acc
        nl, ns = (len(acc_in) or 1), 1 + len(zeroed) + (3 if first else 0)

        def loads(j, h):
            if first:
                return [(inp[h][:, 0], node_view(g.x, j))]
            return [(inp[h][:, k], node_view(a, j)) for k, a in enumerate(acc_in)]
        block = ctx.enter_context(nc.Block())
        node_programs(nc, g, block, loads, None, nl, ns)

        @block.vector
        def _(dve):
            def pair(i):
                chain.turn(i)
                for h in range(2):
                    dve.wait_ge(s.loaded[h].sem, s.loaded[h].at(16 * nl * (i + 1)))
                    if not isinstance(i, int):
                        dve.wait_ge(s.stored[h].sem, s.stored[h].at(16 * ns * i))
                    if first:
                        last = layernorm_relu(nc, g, dve, chain, 2 * i + h, inp[h][:, 0], xc[:], sq[:], st, out[h][:])
                    else:
                        cur = inp[h][:, 0]
                        for k in range(1, len(acc_in)):
                            chain.link(dve, nc.vector.tensor_tensor(xc[:], cur, inp[h][:, k], ALU.add))
                            cur = xc[:]
                        last = nc.vector.tensor_scalar(out[h][:], cur, 0.0, None, ALU.max)
                    last.then_inc(s.ready.sem, 1)
                    dve.wait_ge(s.ready.sem, s.ready.at(2 * i + h + 1))
            turns(dve, NJ // 2, pair)

        @block.scalar
        def _(act):
            def pair(i):
                for h in range(2):
                    j = 2 * i + h
                    if first:
                        deviation(nc, g, act, j, st)
                    act.wait_ge(s.ready.sem, s.ready.at(j + 1))
                    act.dma_start(node_view(g.T0, j), out[h][:]).then_inc(s.stored[h].sem, 16)
                    for a in zeroed:
                        act.dma_start(node_view(a, j), g.zeros[:, 0:G7 * D].rearrange("p (q d) -> p q d", q=G7)).then_inc(s.stored[h].sem, 16)
                    if first:
                        act.dma_start(g.acc68[bass.ts(j, SN), :].rearrange("(p q) d -> p (q d)", p=P), g.zeros[:, 0:G7 * (D + HEADS)]).then_inc(s.stored[h].sem, 16)
                        act.dma_start(g.count[bass.ts(j, SN), :].rearrange("(p q) d -> p (q d)", p=P), g.zeros[:, 0:G7]).then_inc(s.stored[h].sem, 16)
                        act.dma_start(g.high[bass.ts(j, SN), :].rearrange("(p q) d -> p (q d)", p=P), g.lowest[:, 0:G7 * HEADS]).then_inc(s.stored[h].sem, 16)
            turns(act, NJ // 2, pair)
    chain.close(NJ // 2)
    node_close(s, nl, ns)
    s.ready.close(NJ)
    if first:
        s.squares.close(NJ)
        s.root.close(NJ)


def stage_first_residual(nc, g):
    s = g.ns
    name = "n2"
    with ExitStack() as ctx:
        sb = lambda n, sh, d=F32: ctx.enter_context(nc.sbuf_tensor(f"{name}_{n}", sh, d))
        na = len(g.acc)
        inp = [sb(f"inp{h}", [P, 1 + na, G7, D]) for h in range(2)]
        x1 = [sb(f"x1{h}", [P, G7, D]) for h in range(2)]
        out = [sb(f"out{h}", [P, G7, D]) for h in range(2)]
        xc, sq, st, y = sb("xc", [P, G7, D]), sb("sq", [P, G7, D]), sb("st", [P, 5, G7]), sb("y", [P, G7, D])
        chain = Chain(s.chain)
        nl, ns = 1 + na, 2 + na
        block = ctx.enter_context(nc.Block())
        node_programs(nc, g, block, lambda j, h: [(inp[h][:, 0], node_view(g.x, j))] + [
            (inp[h][:, 1 + k], node_view(a, j)) for k, a in enumerate(g.acc)], None, nl, ns)

        @block.vector
        def _(dve):
            def pair(i):
                chain.turn(i)
                for h in range(2):
                    dve.wait_ge(s.loaded[h].sem, s.loaded[h].at(16 * nl * (i + 1)))
                    if not isinstance(i, int):
                        dve.wait_ge(s.stored[h].sem, s.stored[h].at(16 * ns * i))
                    cur = inp[h][:, 1]
                    for k in range(1, na):
                        chain.link(dve, nc.vector.tensor_tensor(y[:], cur, inp[h][:, 1 + k], ALU.add))
                        cur = y[:]
                    chain.link(dve, nc.vector.tensor_tensor(x1[h][:], cur, inp[h][:, 0], ALU.add))
                    chain.link(dve, layernorm_relu(nc, g, dve, chain, 2 * i + h, x1[h][:], xc[:], sq[:], st, y[:]))
                    nc.vector.tensor_tensor(out[h][:], y[:], bc(g.dinv[:, bass.ts(2 * i + h, G7)]), ALU.mult).then_inc(s.ready.sem, 1)
                    dve.wait_ge(s.ready.sem, s.ready.at(2 * i + h + 1))
            turns(dve, NJ // 2, pair)

        @block.scalar
        def _(act):
            def pair(i):
                for h in range(2):
                    j = 2 * i + h
                    deviation(nc, g, act, j, st)
                    act.wait_ge(s.ready.sem, s.ready.at(2 * i + h + 1))
                    act.dma_start(node_view(g.X, j), x1[h][:]).then_inc(s.stored[h].sem, 16)
                    act.dma_start(node_view(g.T0, j), out[h][:]).then_inc(s.stored[h].sem, 16)
                    for a in g.acc:
                        act.dma_start(node_view(a, j), g.zeros[:, 0:G7 * D].rearrange("p (q d) -> p q d", q=G7)).then_inc(s.stored[h].sem, 16)
            turns(act, NJ // 2, pair)
    chain.close(NJ // 2)
    node_close(s, nl, ns)
    for sig in (s.ready, s.squares, s.root):
        sig.close(NJ)


def stage_conv_stats(nc, g, name, channels):
    s = g.ns
    HALF = SN // 2
    with ExitStack() as ctx:
        sb = lambda n, sh, d=F32: ctx.enter_context(nc.sbuf_tensor(f"{name}_{n}", sh, d))
        pb = lambda n, sh: ctx.enter_context(nc.psum_tensor(f"{name}_{n}", sh, F32))
        inp = [sb(f"inp{h}", [P, 3, G7, D]) for h in range(2)]
        y, agg = sb("y", [P, G7, D]), sb("agg", [P, G7, D])
        agg_t = sb("agg_t", [D, SN])
        ut = [sb(f"ut{h}", [channels, SN]) for h in range(2)]
        stats = sb("stats", [channels, 2 * NJ, 6])
        agg_ps = [pb(f"agg_ps{k}", [D, 4 * P]) for k in range(2)]
        u_ps = [pb(f"u_ps{k}", [channels, HALF]) for k in range(2)]
        chain = Chain(s.chain)
        accs = g.acc[0:2]
        nl, ns = 3, 1 + 2
        block = ctx.enter_context(nc.Block())
        node_programs(nc, g, block, lambda j, h: [(inp[h][:, 0], node_view(g.T0, j)), (inp[h][:, 1], node_view(accs[0], j)),
                                                  (inp[h][:, 2], node_view(accs[1], j))], None, nl, ns)

        @block.vector
        def _(dve):
            def pair(i):
                chain.turn(i)
                for h in range(2):
                    dve.wait_ge(s.loaded[h].sem, s.loaded[h].at(16 * nl * (i + 1)))
                    chain.link(dve, nc.vector.tensor_tensor(y[:], inp[h][:, 0], inp[h][:, 1], ALU.add))
                    chain.link(dve, nc.vector.tensor_tensor(y[:], y[:], inp[h][:, 2], ALU.add))
                    if h or not isinstance(i, int):
                        dve.wait_ge(s.turned.sem, s.turned.at(2 * i + h))
                    nc.vector.tensor_tensor(agg[:], y[:], bc(g.dinv[:, bass.ts(2 * i + h, G7)]), ALU.mult).then_inc(s.ready.sem, 1)
                    dve.wait_ge(s.out.sem, s.out.at(2 * i + h + 1))
                    for k in range(2):
                        col = bass.ds(4 * i + 2 * h + k, 1)
                        last = nc.vector.bn_stats(stats[:, col, :].rearrange("c a s -> c (a s)"), ut[h][:, k * HALF:(k + 1) * HALF])
                    last.then_inc(s.stat.sem, 1)
            turns(dve, NJ // 2, pair)
            h = 1
            assert VALID_LAST > HALF
            dve.wait_ge(s.stat.sem, s.stat.at(NJ))
            nc.vector.bn_stats(stats[:, 2 * NJ - 1, :], ut[h][:, HALF:VALID_LAST]).then_inc(s.stat.sem, 1)
            dve.wait_ge(s.stat.sem, s.stat.at(NJ + 1))
            nc.vector.bn_aggr(g.mv[0:channels, :], stats[:].rearrange("c a s -> c (a s)")).then_inc(s.stat.sem, 1)
            mv, gb = g.mv, g.gb1 if channels == P else g.gb2
            step = lambda n, ins: (ins.then_inc(s.stat.sem, 1), dve.wait_ge(s.stat.sem, s.stat.at(NJ + 2 + n)))
            dve.wait_ge(s.root.sem, s.root.at(1))
            step(1, nc.vector.reciprocal(g.bn[0:channels, 2:3], g.bn[0:channels, 3:4]))
            step(2, nc.vector.tensor_tensor(g.bn[0:channels, 0:1], g.bn[0:channels, 2:3], gb[0:channels, 0:1], ALU.mult))
            step(3, nc.vector.tensor_tensor(g.bn[0:channels, 3:4], mv[0:channels, 0:1], g.bn[0:channels, 0:1], ALU.mult))
            step(4, nc.vector.tensor_tensor(g.bn[0:channels, 1:2], gb[0:channels, 1:2], g.bn[0:channels, 3:4], ALU.subtract))

        @block.tensor
        def _(pe):
            def pair(i):
                for h in range(2):
                    n = 2 * i + h
                    pe.wait_ge(s.ready.sem, s.ready.at(n + 1))
                    if h or not isinstance(i, int):
                        pe.wait_ge(s.half.sem, s.half.at(n))
                        pe.wait_ge(s.out.sem, s.out.at(n))
                    for q in range(G7):
                        mm = nc.tensor.matmul(agg_ps[q // 4][:, bass.ts(q % 4, P)], agg[:, q], g.ident[:], start=True, stop=True)
                    mm.then_inc(s.turned.sem, 1)
                    if channels == P:
                        pe.wait_ge(s.half.sem, s.half.at(n + 1))
                        for k in range(2):
                            mm = nc.tensor.matmul(u_ps[k][:], g.w1[:], agg_t[:, k * HALF:(k + 1) * HALF], start=True, stop=True)
                        mm.then_inc(s.product.sem, 1)
            turns(pe, NJ // 2, pair)

        @block.scalar
        def _(act):
            def pair(i):
                for h in range(2):
                    n = 2 * i + h
                    act.wait_ge(s.turned.sem, s.turned.at(n + 1))
                    if not isinstance(i, int):
                        act.wait_ge(s.stored[h].sem, s.stored[h].at(16 * ns * i))
                        act.wait_ge(s.stat.sem, s.stat.at(n - 1))
                    if channels == P:
                        nc.scalar.activation(agg_t[:, 0:4 * P], agg_ps[0][:], ACT.Copy)
                        nc.scalar.activation(agg_t[:, 4 * P:SN], agg_ps[1][:, 0:3 * P], ACT.Copy).then_inc(s.half.sem, 1)
                        act.wait_ge(s.product.sem, s.product.at(n + 1))
                        for k in range(2):
                            last = nc.scalar.activation(ut[h][:, k * HALF:(k + 1) * HALF], u_ps[k][:], ACT.Identity, bias=g.cb1[:, 0:1])
                    else:
                        nc.scalar.activation(ut[h][:, 0:4 * P], agg_ps[0][:], ACT.Identity, bias=g.cb2[0:D, 0:1])
                        last = nc.scalar.activation(ut[h][:, 4 * P:SN], agg_ps[1][:, 0:3 * P], ACT.Identity, bias=g.cb2[0:D, 0:1])
                        last.then_inc(s.half.sem, 1)
                    if channels == P:
                        last.then_inc(s.out.sem, 1)
                    else:
                        act.wait_ge(s.half.sem, s.half.at(n + 1)).then_inc(s.out.sem, 1)
                    act.wait_ge(s.out.sem, s.out.at(n + 1))
                    act.dma_start(g.UT[0:channels, bass.ts(n, SN)], ut[h][:]).then_inc(s.stored[h].sem, 16)
                    for a in accs:
                        act.dma_start(node_view(a, n), g.zeros[:, 0:G7 * D].rearrange("p (q d) -> p q d", q=G7)).then_inc(s.stored[h].sem, 16)
            turns(act, NJ // 2, pair)
            act.wait_ge(s.stat.sem, s.stat.at(NJ + 2))
            nc.scalar.activation(g.bn[0:channels, 3:4], g.mv[0:channels, 1:2], ACT.Sqrt, bias=g.eps[0:channels, 0:1]).then_inc(s.root.sem, 1)
    chain.close(NJ // 2)
    node_close(s, nl, ns)
    s.root.close(1)
    for sig in (s.ready, s.turned, s.half, s.out):
        sig.close(NJ)
    if channels == P:
        s.product.close(NJ)
    s.stat.close(NJ + 6)


def stage_conv_next(nc, g, name, channels, weight):
    s = g.ns
    with ExitStack() as ctx:
        sb = lambda n, sh, d=F32: ctx.enter_context(nc.sbuf_tensor(f"{name}_{n}", sh, d))
        pb = lambda n, sh: ctx.enter_context(nc.psum_tensor(f"{name}_{n}", sh, F32))
        ut = [sb(f"ut{h}", [channels, SN]) for h in range(2)]
        lin, z = sb("lin", [channels, SN]), sb("z", [channels, SN])
        out = [sb(f"out{h}", [P, G7, D]) for h in range(2)]
        v_ps = pb("v_ps", [P, G7, D])
        chain = Chain(s.chain)
        nl, ns = 1, 1
        block = ctx.enter_context(nc.Block())
        node_programs(nc, g, block, lambda j, h: [(ut[h][:], g.UT[0:channels, bass.ts(j, SN)])], None, nl, ns)

        @block.scalar
        def _(act):
            def pair(i):
                for h in range(2):
                    n = 2 * i + h
                    act.wait_ge(s.loaded[h].sem, s.loaded[h].at(16 * nl * (i + 1)))
                    if h or not isinstance(i, int):
                        act.wait_ge(s.half.sem, s.half.at(n))
                    nc.scalar.activation(lin[:], ut[h][:], ACT.Identity, bias=g.bn[0:channels, 1:2], scale=g.bn[0:channels, 0:1]).then_inc(s.ready.sem, 1)
                    act.wait_ge(s.out.sem, s.out.at(n + 1))
                    act.dma_start(node_view(g.T0, n), out[h][:]).then_inc(s.stored[h].sem, 16)
            turns(act, NJ // 2, pair)

        @block.vector
        def _(dve):
            def pair(i):
                for h in range(2):
                    n = 2 * i + h
                    dve.wait_ge(s.ready.sem, s.ready.at(n + 1))
                    if h or not isinstance(i, int):
                        dve.wait_ge(s.product.sem, s.product.at(n))
                    nc.vector.scalar_tensor_tensor(z[:], lin[:], LEAK, lin[:], ALU.mult, ALU.max).then_inc(s.half.sem, 1)
                    dve.wait_ge(s.product.sem, s.product.at(n + 1))
                    if not isinstance(i, int):
                        dve.wait_ge(s.stored[h].sem, s.stored[h].at(16 * ns * i))
                    nc.vector.tensor_tensor(out[h][:], v_ps[:], bc(g.dinv[:, bass.ts(n, G7)]), ALU.mult).then_inc(s.out.sem, 1)
            turns(dve, NJ // 2, pair)

        @block.tensor
        def _(pe):
            def pair(i):
                for h in range(2):
                    n = 2 * i + h
                    pe.wait_ge(s.half.sem, s.half.at(n + 1))
                    if h or not isinstance(i, int):
                        pe.wait_ge(s.out.sem, s.out.at(n))
                    for q in range(G7):
                        mm = nc.tensor.matmul(v_ps[:, q], z[:, bass.ts(q, P)], weight, start=True, stop=True)
                    mm.then_inc(s.product.sem, 1)
            turns(pe, NJ // 2, pair)
    node_close(s, nl, ns)
    for sig in (s.ready, s.half, s.out, s.product):
        sig.close(NJ)


def stage_typed(nc, g):
    s = g.ns
    name = "n7"
    with ExitStack() as ctx:
        sb = lambda n, sh, d=F32: ctx.enter_context(nc.sbuf_tensor(f"{name}_{n}", sh, d))
        pb = lambda n, sh: ctx.enter_context(nc.psum_tensor(f"{name}_{n}", sh, F32))
        inp = [sb(f"inp{h}", [P, 4, G7, D]) for h in range(2)]
        xo = [sb(f"xo{h}", [P, G7, D]) for h in range(2)]
        q_out = [sb(f"q_out{h}", [P, G7, D]) for h in range(2)]
        kv_out = [sb(f"kv_out{h}", [P, G7, 4 * D]) for h in range(2)]
        xc, sq, st, y, hh = sb("xc", [P, G7, D]), sb("sq", [P, G7, D]), sb("st", [P, 5, G7]), sb("y", [P, G7, D]), sb("hh", [P, G7, D])
        typed, typed_t = sb("typed", [P, G7, 2, D]), sb("typed_t", [P, G7, P])
        t_ps = [pb(f"t_ps{k}", [P, 4, P]) for k in range(2)]
        o_ps = [pb(f"o_ps{k}", [P, 5 * D]) for k in range(4)]
        chain = Chain(s.chain)
        nl, ns = 4, 5
        block = ctx.enter_context(nc.Block())
        node_programs(nc, g, block, lambda j, h: [(inp[h][:, 0], node_view(g.X, j)), (inp[h][:, 1], node_view(g.T0, j)),
                                                  (inp[h][:, 2], node_view(g.acc[0], j)), (inp[h][:, 3], node_view(g.acc[1], j))], None, nl, ns)

        @block.vector
        def _(dve):
            def pair(i):
                chain.turn(i)
                for h in range(2):
                    n = 2 * i + h
                    dve.wait_ge(s.loaded[h].sem, s.loaded[h].at(16 * nl * (i + 1)))
                    if not isinstance(i, int):
                        dve.wait_ge(s.stored[h].sem, s.stored[h].at(16 * ns * i))
                    L = lambda ins: chain.link(dve, ins)
                    cols = bass.ts(n, G7)
                    L(nc.vector.tensor_tensor(y[:], inp[h][:, 1], inp[h][:, 2], ALU.add))
                    L(nc.vector.tensor_tensor(y[:], y[:], inp[h][:, 3], ALU.add))
                    L(nc.vector.tensor_tensor(y[:], y[:], bc(g.dinv[:, cols]), ALU.mult))
                    L(nc.vector.tensor_tensor(y[:], y[:], g.cb3[:].unsqueeze(1).to_broadcast([P, G7, D]), ALU.add))
                    L(nc.vector.tensor_tensor(y[:], y[:], inp[h][:, 0], ALU.add))
                    L(layernorm_relu(nc, g, dve, chain, n, y[:], xc[:], sq[:], st, hh[:]))
                    if h or not isinstance(i, int):
                        dve.wait_ge(s.turned.sem, s.turned.at(2 * n))
                    L(nc.vector.tensor_tensor(typed[:, :, 1], hh[:], bc(g.type1[:, cols]), ALU.mult))
                    nc.vector.tensor_tensor(typed[:, :, 0], hh[:], typed[:, :, 1], ALU.subtract).then_inc(s.ready.sem, 1)
                    L(nc.vector.tensor_tensor(sq[:], hh[:], bc(g.beta[:, cols]), ALU.mult))
                    nc.vector.tensor_tensor(xo[h][:], y[:], sq[:], ALU.add).then_inc(s.out.sem, 1)
                    dve.wait_ge(s.out.sem, s.out.at(n + 1))
                    dve.wait_ge(s.product.sem, s.product.at(G7 * n + 1))
            turns(dve, NJ // 2, pair)

        @block.tensor
        def _(pe):
            def pair(i):
                for h in range(2):
                    n = 2 * i + h
                    pe.wait_ge(s.ready.sem, s.ready.at(n + 1))
                    if h or not isinstance(i, int):
                        pe.wait_ge(s.half.sem, s.half.at(2 * n))
                    for k in range(2):
                        for q in range(4 * k, min(G7, 4 * k + 4)):
                            mm = nc.tensor.matmul(t_ps[k][:, q % 4], typed[:, q].rearrange("p t d -> p (t d)"), g.ident[:], start=True, stop=True)
                        mm.then_inc(s.turned.sem, 1)
                    for q in range(G7):
                        pe.wait_ge(s.half.sem, s.half.at(2 * n + q // 4 + 1))
                        if q >= 4:
                            pe.wait_ge(s.out2.sem, s.out2.at(G7 * n + q - 3))
                        elif h or not isinstance(i, int):
                            pe.wait_ge(s.out2.sem, s.out2.at(G7 * n))
                        nc.tensor.matmul(o_ps[q % 4][:], typed_t[:, q], g.wqkv[:], start=True, stop=True).then_inc(s.product.sem, 1)
            turns(pe, NJ // 2, pair)

        @block.scalar
        def _(act):
            def pair(i):
                for h in range(2):
                    n = 2 * i + h
                    deviation(nc, g, act, n, st)
                    for k in range(2):
                        act.wait_ge(s.turned.sem, s.turned.at(2 * n + k + 1))
                        if k == 0 and (h or not isinstance(i, int)):
                            act.wait_ge(s.product.sem, s.product.at(G7 * n))
                        m = min(G7, 4 * k + 4) - 4 * k
                        nc.scalar.activation(typed_t[:, 4 * k:4 * k + m], t_ps[k][:, 0:m], ACT.Copy).then_inc(s.half.sem, 1)
                    if not isinstance(i, int):
                        act.wait_ge(s.stored[h].sem, s.stored[h].at(16 * ns * i))
                    for q in range(G7):
                        act.wait_ge(s.product.sem, s.product.at(G7 * n + q + 1))
                        nc.scalar.activation(q_out[h][:, q], o_ps[q % 4][:, 0:D], ACT.Copy)
                        nc.scalar.activation(kv_out[h][:, q], o_ps[q % 4][:, D:5 * D], ACT.Copy).then_inc(s.out2.sem, 1)
                    act.wait_ge(s.out2.sem, s.out2.at(G7 * n + G7))
                    act.wait_ge(s.out.sem, s.out.at(n + 1))
                    act.dma_start(node_view(g.X, n), xo[h][:]).then_inc(s.stored[h].sem, 16)
                    act.dma_start(node_view(g.Q, n), q_out[h][:]).then_inc(s.stored[h].sem, 16)
                    act.dma_start(node_view(g.KV, n), kv_out[h][:]).then_inc(s.stored[h].sem, 16)
                    for a in g.acc[0:2]:
                        act.dma_start(node_view(a, n), g.zeros[:, 0:G7 * D].rearrange("p (q d) -> p q d", q=G7)).then_inc(s.stored[h].sem, 16)
            turns(act, NJ // 2, pair)
    chain.close(NJ // 2)
    node_close(s, nl, ns)
    s.ready.close(NJ)
    s.out.close(NJ)
    s.turned.close(2 * NJ)
    s.half.close(2 * NJ)
    s.squares.close(NJ)
    s.root.close(NJ)
    for sig in (s.product, s.out2):
        sig.close(G7 * NJ)


def stage_attended(nc, g):
    s = g.ns
    name = "n8"
    with ExitStack() as ctx:
        sb = lambda n, sh, d=F32: ctx.enter_context(nc.sbuf_tensor(f"{name}_{n}", sh, d))
        pb = lambda n, sh: ctx.enter_context(nc.psum_tensor(f"{name}_{n}", sh, F32))
        acc = [sb(f"acc{h}", [P, G7, D + HEADS]) for h in range(2)]
        x_in = [sb(f"x_in{h}", [P, G7, D]) for h in range(2)]
        xo, out = ([sb(f"{m}{h}", [P, G7, D]) for h in range(2)] for m in ("xo", "out"))
        xc, sq, st, y = sb("xc", [P, G7, D]), sb("sq", [P, G7, D]), sb("st", [P, 5, G7]), sb("y", [P, G7, D])
        den, rden = sb("den", [P, G7, HEADS]), sb("rden", [P, G7, HEADS])
        typed, typed_t = sb("typed", [P, G7, 2, D]), sb("typed_t", [P, G7, P])
        t_ps = [pb(f"t_ps{k}", [P, 4, P]) for k in range(2)]
        o_ps = pb("o_ps", [P, G7, D])
        chain = Chain(s.chain)
        nl, ns = 2, 2
        block = ctx.enter_context(nc.Block())
        node_programs(nc, g, block, lambda j, h: [(acc[h][:], node_view(g.acc68, j)), (x_in[h][:], node_view(g.X, j))], None, nl, ns)

        @block.vector
        def _(dve):
            def pair(i):
                chain.turn(i)
                for h in range(2):
                    n = 2 * i + h
                    L = lambda ins: chain.link(dve, ins)
                    cols = bass.ts(n, G7)
                    dve.wait_ge(s.loaded[h].sem, s.loaded[h].at(16 * nl * (i + 1)))
                    L(nc.vector.tensor_scalar(den[:], acc[h][:, :, D:D + HEADS], 1e-30, None, ALU.max))
                    L(nc.vector.reciprocal(rden[:], den[:]))
                    for hd in range(HEADS):
                        r = slice(HD * hd, HD * hd + HD)
                        last = nc.vector.tensor_tensor(y[:, :, r], acc[h][:, :, r], rden[:, :, hd:hd + 1].to_broadcast([P, G7, HD]), ALU.mult)
                    L(last)
                    L(nc.vector.tensor_tensor(typed[:, :, 1], y[:], bc(g.type1[:, cols]), ALU.mult))
                    nc.vector.tensor_tensor(typed[:, :, 0], y[:], typed[:, :, 1], ALU.subtract).then_inc(s.ready.sem, 1)
                    dve.wait_ge(s.product.sem, s.product.at(n + 1))
                    L(nc.vector.tensor_tensor(xc[:], o_ps[:], bc(g.alpha[:, cols]), ALU.mult))
                    if not isinstance(i, int):
                        dve.wait_ge(s.stored[h].sem, s.stored[h].at(16 * ns * i))
                    L(nc.vector.tensor_tensor(xo[h][:], xc[:], x_in[h][:], ALU.add))
                    layernorm_relu(nc, g, dve, chain, n, xo[h][:], xc[:], sq[:], st, out[h][:]).then_inc(s.out.sem, 1)
                    dve.wait_ge(s.out.sem, s.out.at(n + 1))
            turns(dve, NJ // 2, pair)

        @block.tensor
        def _(pe):
            def pair(i):
                for h in range(2):
                    n = 2 * i + h
                    pe.wait_ge(s.ready.sem, s.ready.at(n + 1))
                    for k in range(2):
                        for q in range(4 * k, min(G7, 4 * k + 4)):
                            mm = nc.tensor.matmul(t_ps[k][:, q % 4], typed[:, q].rearrange("p t d -> p (t d)"), g.ident[:], start=True, stop=True)
                        mm.then_inc(s.turned.sem, 1)
                    for q in range(G7):
                        pe.wait_ge(s.half.sem, s.half.at(2 * n + q // 4 + 1))
                        mm = nc.tensor.matmul(o_ps[:, q], typed_t[:, q], g.wa[:], start=True, stop=True)
                    mm.then_inc(s.product.sem, 1)
            turns(pe, NJ // 2, pair)

        @block.scalar
        def _(act):
            def pair(i):
                for h in range(2):
                    n = 2 * i + h
                    for k in range(2):
                        act.wait_ge(s.turned.sem, s.turned.at(2 * n + k + 1))
                        m = min(G7, 4 * k + 4) - 4 * k
                        nc.scalar.activation(typed_t[:, 4 * k:4 * k + m], t_ps[k][:, 0:m], ACT.Copy).then_inc(s.half.sem, 1)
                    deviation(nc, g, act, n, st)
                    act.wait_ge(s.out.sem, s.out.at(n + 1))
                    act.dma_start(node_view(g.X, n), xo[h][:]).then_inc(s.stored[h].sem, 16)
                    act.dma_start(node_view(g.T0, n), out[h][:]).then_inc(s.stored[h].sem, 16)
            turns(act, NJ // 2, pair)
    chain.close(NJ // 2)
    node_close(s, nl, ns)
    for sig in (s.ready, s.product, s.out, s.squares, s.root):
        sig.close(NJ)
    s.turned.close(2 * NJ)
    s.half.close(2 * NJ)


def stage_last(nc, g):
    s = g.ns
    name = "n9"
    HALF = SN // 2
    with ExitStack() as ctx:
        sb = lambda n, sh, d=F32: ctx.enter_context(nc.sbuf_tensor(f"{name}_{n}", sh, d))
        pb = lambda n, sh: ctx.enter_context(nc.psum_tensor(f"{name}_{n}", sh, F32))
        inp = [sb(f"inp{h}", [P, 2, G7, D]) for h in range(2)]
        both = [sb(f"both{h}", [P, G7, 2, D]) for h in range(2)]
        x_in = [sb(f"x_in{h}", [P, G7, D]) for h in range(2)]
        out = [sb(f"out{h}", [P, G7, D]) for h in range(2)]
        y, both_t, hid = sb("y", [P, G7, D]), sb("both_t", [P, SN]), sb("hid", [D, SN])
        t_ps = [pb(f"t_ps{k}", [P, 4 * P]) for k in range(2)]
        h_ps = [pb(f"h_ps{k}", [D, HALF]) for k in range(2)]
        o_ps = pb("o_ps", [P, G7, D])
        chain = Chain(s.chain)
        nl, ns = 4, 1
        block = ctx.enter_context(nc.Block())
        node_programs(nc, g, block, lambda j, h: [(both[h][:, :, 0], node_view(g.T0, j)), (inp[h][:, 0], node_view(g.acc[0], j)),
                                                  (inp[h][:, 1], node_view(g.acc[1], j)), (x_in[h][:], node_view(g.X, j))], None, nl, ns)

        @block.vector
        def _(dve):
            def pair(i):
                chain.turn(i)
                for h in range(2):
                    n = 2 * i + h
                    L = lambda ins: chain.link(dve, ins)
                    dve.wait_ge(s.loaded[h].sem, s.loaded[h].at(16 * nl * (i + 1)))
                    L(nc.vector.tensor_tensor(y[:], inp[h][:, 0], inp[h][:, 1], ALU.add))
                    nc.vector.tensor_tensor(both[h][:, :, 1], y[:], bc(g.rcount[:, bass.ts(n, G7)]), ALU.mult).then_inc(s.ready.sem, 1)
                    dve.wait_ge(s.product.sem, s.product.at(2 * n + 2))
                    L(nc.vector.tensor_tensor(y[:], o_ps[:], g.b34[:].unsqueeze(1).to_broadcast([P, G7, D]), ALU.add))
                    if not isinstance(i, int):
                        dve.wait_ge(s.stored[h].sem, s.stored[h].at(16 * ns * i))
                    nc.vector.tensor_tensor(out[h][:], y[:], x_in[h][:], ALU.add).then_inc(s.out.sem, 1)
                    dve.wait_ge(s.out.sem, s.out.at(n + 1))
            turns(dve, NJ // 2, pair)

        @block.tensor
        def _(pe):
            def pair(i):
                for h in range(2):
                    n = 2 * i + h
                    pe.wait_ge(s.ready.sem, s.ready.at(n + 1))
                    for q in range(G7):
                        mm = nc.tensor.matmul(t_ps[q // 4][:, bass.ts(q % 4, P)], both[h][:, q].rearrange("p t d -> p (t d)"), g.ident[:], start=True, stop=True)
                    mm.then_inc(s.turned.sem, 1)
                    pe.wait_ge(s.half.sem, s.half.at(2 * n + 1))
                    for k in range(2):
                        mm = nc.tensor.matmul(h_ps[k][:], g.w33[:], both_t[:, k * HALF:(k + 1) * HALF], start=True, stop=True)
                    mm.then_inc(s.product.sem, 1)
                    pe.wait_ge(s.half.sem, s.half.at(2 * n + 2))
                    for q in range(G7):
                        mm = nc.tensor.matmul(o_ps[:, q], hid[:, bass.ts(q, P)], g.w34[:], start=True, stop=True)
                    mm.then_inc(s.product.sem, 1)
            turns(pe, NJ // 2, pair)

        @block.scalar
        def _(act):
            def pair(i):
                for h in range(2):
                    n = 2 * i + h
                    act.wait_ge(s.turned.sem, s.turned.at(n + 1))
                    nc.scalar.activation(both_t[:, 0:4 * P], t_ps[0][:], ACT.Copy)
                    nc.scalar.activation(both_t[:, 4 * P:SN], t_ps[1][:, 0:3 * P], ACT.Copy).then_inc(s.half.sem, 1)
                    act.wait_ge(s.product.sem, s.product.at(2 * n + 1))
                    for k in range(2):
                        last = nc.scalar.activation(hid[:, k * HALF:(k + 1) * HALF], h_ps[k][:], ACT.Relu, bias=g.c3[0:D, 0:1])
                    last.then_inc(s.half.sem, 1)
                    act.wait_ge(s.out.sem, s.out.at(n + 1))
                    act.dma_start(node_view(g.out, n), out[h][:]).then_inc(s.stored[h].sem, 16)
            turns(act, NJ // 2, pair)
    chain.close(NJ // 2)
    node_close(s, nl, ns)
    s.ready.close(NJ)
    s.turned.close(NJ)
    s.out.close(NJ)
    s.product.close(2 * NJ)
    s.half.close(2 * NJ)
def general_transform_edges(nc, env, layer):
    g = env
    with ExitStack() as ctx:
        sb = lambda n, s, d=F32: ctx.enter_context(nc.sbuf_tensor(f"ge{layer}_{n}", s, d))
        pb = lambda n, s: ctx.enter_context(nc.psum_tensor(f"ge{layer}_{n}", s, F32))
        edge_i, lead, rows, cols = sb("edge_i", [P, 3], I32), sb("lead", [P, 2], I32), sb("rows", [P, 3, P]), sb("cols", [P, 4])
        far = sb("far", [P, 2, D])
        masked, onehot, same = sb("masked", [P, NPAIR, P]), sb("onehot", [R9, P]), sb("same", [P, P])
        msg, total = sb("msg", [P, D]), sb("total", [P, 2, D])
        far_t, msg_ps, total_ps = pb("far_t", [P, P]), pb("msg_ps", [P, D]), pb("total_ps", [P, D])
        s = g.gs
        block = ctx.enter_context(nc.Block())

        @block.sync
        def _(sp):
            def tile(i):
                if not isinstance(i, int):
                    sp.wait_ge(s.scattered[0].sem, s.scattered[0].at(16 * i)).then_inc(g.sp_gate, 1)
                    sp.wait_ge(s.scattered[1].sem, s.scattered[1].at(16 * i)).then_inc(g.sp_gate, 1)
                e = bass.ts(i, P)
                sp.dma_start(edge_i[:], g.edge_i[e, :]).then_inc(s.loaded.sem, 16)
                sp.dma_start(lead[:], g.lead[e, :]).then_inc(s.loaded.sem, 16)
                sp.dma_start(rows[:], g.edge_rows[:, e].partition_broadcast(P)).then_inc(s.loaded.sem, 16)
                sp.dma_start(cols[:], g.edge_cols[e, :]).then_inc(s.loaded.sem, 16)
            turns(sp, ET, tile)
            for d in range(2):
                sp.wait_ge(s.scattered[d].sem, s.scattered[d].at(16 * ET))

        @block.gpsimd
        def _(pool):
            def tile(i):
                pool.wait_ge(s.loaded.sem, s.loaded.at(64 * i + 64)).then_inc(s.gate.sem, 1)
                for d in range(2):
                    pool.indirect_dma_start(out=far[:, d], out_offset=None, in_=g.T0[:], in_offset=bass.IndirectOffsetOnAxis(
                        ap=edge_i[:, d:d + 1], axis=0)).then_inc(s.gathered[d].sem, 16)
                for d in range(2):
                    pool.wait_ge(s.summed.sem, s.summed.at(2 * i + d + 1)).then_inc(s.gate.sem, 1)
                    pool.indirect_dma_start(out=g.acc[d][:], out_offset=bass.IndirectOffsetOnAxis(ap=lead[:, d:d + 1], axis=0),
                                            in_=total[:, d], in_offset=None, compute_op=ALU.add).then_inc(s.scattered[d].sem, 16)
            turns(pool, ET, tile)

        @block.tensor
        def _(pe):
            def tile(i):
                for d in range(2):
                    pe.wait_ge(s.gathered[d].sem, s.gathered[d].at(16 * i + 16))
                    for half in range(2):
                        mm = nc.tensor.matmul(far_t[64 * half:64 * half + 64, :], far[:, d], g.ident[:], start=True, stop=True)
                    mm.then_inc(s.turned.sem, 1)
                    pe.wait_ge(s.masked.sem, s.masked.at(2 * i + d + 1))
                    for j in range(NPAIR):
                        nc.tensor.matmul(msg_ps[:], masked[:, j], g.w0[:, layer, d, j], start=(j == 0), stop=False)
                    nc.tensor.matmul(msg_ps[:], onehot[:], g.b0[:, layer, d], start=False, stop=True).then_inc(s.product.sem, 1)
                    pe.wait_ge(s.msg.sem, s.msg.at(2 * i + d + 1))
                    nc.tensor.matmul(total_ps[:], same[:], msg[:], start=True, stop=True).then_inc(s.joined.sem, 1)
            turns(pe, ET, tile)

        @block.vector
        def _(dve):
            def tile(i):
                for d in range(2):
                    dve.wait_ge(s.turned.sem, s.turned.at(2 * i + d + 1))
                    dve.wait_ge(s.loaded.sem, s.loaded.at(64 * i + 64))
                    if d or not isinstance(i, int):
                        dve.wait_ge(s.joined.sem, s.joined.at(2 * i + d))
                    nc.vector.tensor_scalar(same[:], rows[:, 1 - d], cols[:, 1 - d:2 - d], None, ALU.is_equal)
                    nc.vector.tensor_scalar(onehot[:], rows[0:R9, 2], g.pid[0:R9, :], None, ALU.is_equal)
                    for j in range(NPAIR):
                        last = nc.vector.scalar_tensor_tensor(masked[:, j], rows[:, 2], g.type_of_row[:, j:j + 1], far_t[:],
                                                              ALU.is_equal, ALU.mult)
                    last.then_inc(s.masked.sem, 1)
            turns(dve, ET, tile)

        @block.scalar
        def _(act):
            def tile(i):
                for d in range(2):
                    act.wait_ge(s.product.sem, s.product.at(2 * i + d + 1))
                    nc.scalar.activation(msg[:], msg_ps[:], ACT.Copy).then_inc(s.msg.sem, 1)
                    act.wait_ge(s.joined.sem, s.joined.at(2 * i + d + 1))
                    nc.scalar.activation(total[:, d], total_ps[:], ACT.Copy).then_inc(s.summed.sem, 1)
            turns(act, ET, tile)
    for d in range(2):
        s.scattered[d].close(16 * ET)
        s.gathered[d].close(16 * ET)
    s.loaded.close(64 * ET)
    for sig in (s.summed, s.turned, s.masked, s.product, s.msg, s.joined):
        sig.close(2 * ET)


def general_sum_edges(nc, env, name, table, out, width, mlp=False, count=False):
    g = env
    with ExitStack() as ctx:
        sb = lambda n, s, d=F32: ctx.enter_context(nc.sbuf_tensor(f"{name}_{n}", s, d))
        pb = lambda n, s: ctx.enter_context(nc.psum_tensor(f"{name}_{n}", s, F32))
        edge_i, lead, rows, cols = sb("edge_i", [P, 3], I32), sb("lead", [P, 2], I32), sb("rows", [P, 3, P]), sb("cols", [P, 4])
        far, same, total = sb("far", [P, D]), sb("same", [P, P]), sb("total", [P, width])
        total_ps = pb("total_ps", [P, width])
        if mlp:
            feat, far_sb, hid, msg = sb("feat", [FE, P]), sb("far_sb", [D, P]), sb("hid", [P, P]), sb("msg", [P, D])
            far_t, hid_ps, msg_ps = pb("far_t", [D, P]), pb("hid_ps", [P, P]), pb("msg_ps", [P, D])
        s = g.gs
        loads = 5 if mlp else 4
        block = ctx.enter_context(nc.Block())

        @block.sync
        def _(sp):
            def tile(i):
                if not isinstance(i, int):
                    sp.wait_ge(s.scattered[0].sem, s.scattered[0].at(16 * i)).then_inc(g.sp_gate, 1)
                e = bass.ts(i, P)
                sp.dma_start(edge_i[:], g.edge_i[e, :]).then_inc(s.loaded.sem, 16)
                sp.dma_start(lead[:], g.lead[e, :]).then_inc(s.loaded.sem, 16)
                sp.dma_start(rows[:], g.edge_rows[:, e].partition_broadcast(P)).then_inc(s.loaded.sem, 16)
                sp.dma_start(cols[:], g.edge_cols[e, :]).then_inc(s.loaded.sem, 16)
                if mlp:
                    sp.dma_start(feat[:], g.feat_t[:, e]).then_inc(s.loaded.sem, 16)
            turns(sp, ET, tile)
            sp.wait_ge(s.scattered[0].sem, s.scattered[0].at(16 * ET))

        @block.gpsimd
        def _(pool):
            def tile(i):
                pool.wait_ge(s.loaded.sem, s.loaded.at(16 * loads * (i + 1))).then_inc(s.gate.sem, 1)
                if not count:
                    pool.indirect_dma_start(out=far[:], out_offset=None, in_=table[:], in_offset=bass.IndirectOffsetOnAxis(
                        ap=edge_i[:, 0:1], axis=0)).then_inc(s.gathered[0].sem, 16)
                pool.wait_ge(s.summed.sem, s.summed.at(i + 1)).then_inc(s.gate.sem, 1)
                pool.indirect_dma_start(out=out[:], out_offset=bass.IndirectOffsetOnAxis(ap=lead[:, 0:1], axis=0),
                                        in_=total[:], in_offset=None, compute_op=ALU.add).then_inc(s.scattered[0].sem, 16)
            turns(pool, ET, tile)

        @block.tensor
        def _(pe):
            def tile(i):
                if not count:
                    pe.wait_ge(s.gathered[0].sem, s.gathered[0].at(16 * i + 16))
                if mlp:
                    nc.tensor.matmul(far_t[:], far[:], g.ident[:], start=True, stop=True).then_inc(s.turned.sem, 1)
                    pe.wait_ge(s.msg.sem, s.msg.at(3 * i + 1))
                    nc.tensor.matmul(hid_ps[:], g.w31x[:], far_sb[:], start=True, stop=False)
                    nc.tensor.matmul(hid_ps[:], g.w31e[:], feat[:], start=False, stop=True).then_inc(s.turned.sem, 1)
                    pe.wait_ge(s.msg.sem, s.msg.at(3 * i + 2))
                    nc.tensor.matmul(msg_ps[:], hid[:], g.w32[:], start=True, stop=True).then_inc(s.turned.sem, 1)
                    pe.wait_ge(s.msg.sem, s.msg.at(3 * i + 3))
                pe.wait_ge(s.masked.sem, s.masked.at(i + 1))
                rhs = g.ones[:, 0:1] if count else msg[:] if mlp else far[:]
                nc.tensor.matmul(total_ps[:], same[:], rhs, start=True, stop=True).then_inc(s.joined.sem, 1)
            turns(pe, ET, tile)

        @block.vector
        def _(dve):
            def tile(i):
                dve.wait_ge(s.loaded.sem, s.loaded.at(16 * loads * (i + 1)))
                nc.vector.tensor_scalar(same[:], rows[:, 1], cols[:, 1:2], None, ALU.is_equal).then_inc(s.masked.sem, 1)
                if mlp:
                    dve.wait_ge(s.turned.sem, s.turned.at(3 * i + 3))
                    nc.vector.tensor_tensor(msg[:], msg_ps[:], g.b32[:], ALU.add).then_inc(s.msg.sem, 1)
            turns(dve, ET, tile)

        @block.scalar
        def _(act):
            def tile(i):
                if mlp:
                    act.wait_ge(s.loaded.sem, s.loaded.at(16 * loads * (i + 1)))
                    act.wait_ge(s.turned.sem, s.turned.at(3 * i + 1))
                    nc.scalar.activation(far_sb[:], far_t[:], ACT.Copy).then_inc(s.msg.sem, 1)
                    act.wait_ge(s.turned.sem, s.turned.at(3 * i + 2))
                    nc.scalar.activation(hid[:], hid_ps[:], ACT.Relu, bias=g.b31[:, 0:1]).then_inc(s.msg.sem, 1)
                act.wait_ge(s.joined.sem, s.joined.at(i + 1))
                nc.scalar.activation(total[:], total_ps[:], ACT.Copy).then_inc(s.summed.sem, 1)
            turns(act, ET, tile)
    s.scattered[0].close(16 * ET)
    if not count:
        s.gathered[0].close(16 * ET)
    s.loaded.close(16 * loads * ET)
    for sig in (s.summed, s.masked, s.joined):
        sig.close(ET)
    if mlp:
        s.turned.close(3 * ET)
        s.msg.close(3 * ET)


def general_scores(nc, env):
    g = env
    with ExitStack() as ctx:
        sb = lambda n, s, d=F32: ctx.enter_context(nc.sbuf_tensor(f"gs_{n}", s, d))
        pb = lambda n, s: ctx.enter_context(nc.psum_tensor(f"gs_{n}", s, F32))
        edge_i, lead, rows, cols = sb("edge_i", [P, 3], I32), sb("lead", [P, 2], I32), sb("rows", [P, 3, P]), sb("cols", [P, 4])
        kv, q, prod, score = sb("kv", [P, 2 * D]), sb("q", [P, D]), sb("prod", [P, D]), sb("score", [P, HEADS])
        diag, away, junk = sb("diag", [P, HEADS, P]), sb("away", [P, P]), sb("junk", [P, P])
        best, so_far, high = sb("best", [P, HEADS]), sb("so_far", [P, HEADS]), sb("high", [P, HEADS])
        spread = pb("spread", [P, HEADS, P])
        s = g.gs
        chain = Chain(s.chain)
        block = ctx.enter_context(nc.Block())

        @block.sync
        def _(sp):
            def tile(i):
                if not isinstance(i, int):
                    sp.wait_ge(s.scattered[0].sem, s.scattered[0].at(16 * i)).then_inc(g.sp_gate, 1)
                e = bass.ts(i, P)
                sp.dma_start(edge_i[:], g.edge_i[e, :]).then_inc(s.loaded.sem, 16)
                sp.dma_start(lead[:], g.lead[e, :]).then_inc(s.loaded.sem, 16)
                sp.dma_start(rows[:], g.edge_rows[:, e].partition_broadcast(P)).then_inc(s.loaded.sem, 16)
                sp.dma_start(cols[:], g.edge_cols[e, :]).then_inc(s.loaded.sem, 16)
            turns(sp, ET, tile)
            sp.wait_ge(s.scattered[0].sem, s.scattered[0].at(16 * ET))

        @block.gpsimd
        def _(pool):
            def tile(i):
                if not isinstance(i, int):
                    pool.wait_ge(s.scattered[0].sem, s.scattered[0].at(16 * i)).then_inc(s.gate.sem, 1)
                pool.wait_ge(s.loaded.sem, s.loaded.at(64 * i + 64)).then_inc(s.gate.sem, 1)
                pool.indirect_dma_start(out=kv[:], out_offset=None, in_=g.KV2, in_offset=bass.IndirectOffsetOnAxis(
                    ap=edge_i[:, 2:3], axis=0)).then_inc(s.gathered[0].sem, 16)
                pool.indirect_dma_start(out=q[:], out_offset=None, in_=g.Q[:], in_offset=bass.IndirectOffsetOnAxis(
                    ap=edge_i[:, 1:2], axis=0)).then_inc(s.gathered[1].sem, 16)
                pool.indirect_dma_start(out=so_far[:], out_offset=None, in_=g.high[:], in_offset=bass.IndirectOffsetOnAxis(
                    ap=edge_i[:, 1:2], axis=0)).then_inc(s.gathered[2].sem, 16)
                pool.wait_ge(s.summed.sem, s.summed.at(i + 1)).then_inc(s.gate.sem, 1)
                pool.indirect_dma_start(out=g.high[:], out_offset=bass.IndirectOffsetOnAxis(ap=lead[:, 0:1], axis=0),
                                        in_=high[:], in_offset=None).then_inc(s.scattered[0].sem, 16)
            turns(pool, ET, tile)

        @block.tensor
        def _(pe):
            def tile(i):
                pe.wait_ge(s.masked.sem, s.masked.at(i + 1))
                nc.tensor.matmul(spread[:], g.ones[:], diag[:], start=True, stop=True).then_inc(s.turned.sem, 1)
            turns(pe, ET, tile)

        @block.vector
        def _(dve):
            def tile(i):
                chain.turn(i)
                dve.wait_ge(s.loaded.sem, s.loaded.at(64 * i + 64))
                dve.wait_ge(s.gathered[0].sem, s.gathered[0].at(16 * i + 16))
                dve.wait_ge(s.gathered[1].sem, s.gathered[1].at(16 * i + 16))
                chain.link(dve, nc.vector.tensor_tensor(prod[:], kv[:, 0:D], q[:], ALU.mult))
                chain.link(dve, nc.vector.tensor_reduce(score[:], prod[:].rearrange("p (h d) -> p h d", h=HEADS), AX, ALU.add))
                for h in range(HEADS):
                    last = nc.vector.tensor_scalar(diag[:, h], g.ident[:], score[:, h:h + 1], None, ALU.mult)
                last.then_inc(s.masked.sem, 1)
                chain.link(dve, nc.vector.tensor_scalar(away[:], rows[:, 1], cols[:, 1:2], LOWEST, ALU.not_equal, ALU.mult))
                dve.wait_ge(s.turned.sem, s.turned.at(i + 1))
                for h in range(HEADS):
                    chain.link(dve, nc.vector.tensor_tensor(junk[:], spread[:, h], away[:], ALU.add))
                    chain.link(dve, nc.vector.tensor_reduce(best[:, h:h + 1], junk[:], AX, ALU.max))
                dve.wait_ge(s.gathered[2].sem, s.gathered[2].at(16 * i + 16))
                nc.vector.tensor_tensor(high[:], best[:], so_far[:], ALU.max).then_inc(s.summed.sem, 1)
            turns(dve, ET, tile)
    chain.close(ET)
    s.scattered[0].close(16 * ET)
    for d in range(3):
        s.gathered[d].close(16 * ET)
    s.loaded.close(64 * ET)
    for sig in (s.summed, s.masked, s.turned):
        sig.close(ET)


def general_attend(nc, env):
    g = env
    with ExitStack() as ctx:
        sb = lambda n, s, d=F32: ctx.enter_context(nc.sbuf_tensor(f"gv_{n}", s, d))
        pb = lambda n, s: ctx.enter_context(nc.psum_tensor(f"gv_{n}", s, F32))
        edge_i, lead, rows, cols = sb("edge_i", [P, 3], I32), sb("lead", [P, 2], I32), sb("rows", [P, 3, P]), sb("cols", [P, 4])
        kv, q, prod, score = sb("kv", [P, 2 * D]), sb("q", [P, D]), sb("prod", [P, D]), sb("score", [P, HEADS])
        high, less, msg, same, total = sb("high", [P, HEADS]), sb("less", [P, HEADS]), sb("msg", [P, D + HEADS]), sb("same", [P, P]), sb("total", [P, D + HEADS])
        total_ps = pb("total_ps", [P, D + HEADS])
        s = g.gs
        chain = Chain(s.chain)
        block = ctx.enter_context(nc.Block())

        @block.sync
        def _(sp):
            def tile(i):
                if not isinstance(i, int):
                    sp.wait_ge(s.scattered[0].sem, s.scattered[0].at(16 * i)).then_inc(g.sp_gate, 1)
                e = bass.ts(i, P)
                sp.dma_start(edge_i[:], g.edge_i[e, :]).then_inc(s.loaded.sem, 16)
                sp.dma_start(lead[:], g.lead[e, :]).then_inc(s.loaded.sem, 16)
                sp.dma_start(rows[:], g.edge_rows[:, e].partition_broadcast(P)).then_inc(s.loaded.sem, 16)
                sp.dma_start(cols[:], g.edge_cols[e, :]).then_inc(s.loaded.sem, 16)
            turns(sp, ET, tile)
            sp.wait_ge(s.scattered[0].sem, s.scattered[0].at(16 * ET))

        @block.gpsimd
        def _(pool):
            def tile(i):
                pool.wait_ge(s.loaded.sem, s.loaded.at(64 * i + 64)).then_inc(s.gate.sem, 1)
                pool.indirect_dma_start(out=kv[:], out_offset=None, in_=g.KV2, in_offset=bass.IndirectOffsetOnAxis(
                    ap=edge_i[:, 2:3], axis=0)).then_inc(s.gathered[0].sem, 16)
                pool.indirect_dma_start(out=q[:], out_offset=None, in_=g.Q[:], in_offset=bass.IndirectOffsetOnAxis(
                    ap=edge_i[:, 1:2], axis=0)).then_inc(s.gathered[1].sem, 16)
                pool.indirect_dma_start(out=high[:], out_offset=None, in_=g.high[:], in_offset=bass.IndirectOffsetOnAxis(
                    ap=edge_i[:, 1:2], axis=0)).then_inc(s.gathered[2].sem, 16)
                pool.wait_ge(s.summed.sem, s.summed.at(i + 1)).then_inc(s.gate.sem, 1)
                pool.indirect_dma_start(out=g.acc68[:], out_offset=bass.IndirectOffsetOnAxis(ap=lead[:, 0:1], axis=0),
                                        in_=total[:], in_offset=None, compute_op=ALU.add).then_inc(s.scattered[0].sem, 16)
            turns(pool, ET, tile)

        @block.tensor
        def _(pe):
            def tile(i):
                pe.wait_ge(s.masked.sem, s.masked.at(i + 1))
                nc.tensor.matmul(total_ps[:], same[:], msg[:], start=True, stop=True).then_inc(s.joined.sem, 1)
            turns(pe, ET, tile)

        @block.vector
        def _(dve):
            def tile(i):
                chain.turn(i)
                dve.wait_ge(s.loaded.sem, s.loaded.at(64 * i + 64))
                nc.vector.tensor_scalar(same[:], rows[:, 1], cols[:, 1:2], None, ALU.is_equal)
                for d in range(3):
                    dve.wait_ge(s.gathered[d].sem, s.gathered[d].at(16 * i + 16))
                chain.link(dve, nc.vector.tensor_tensor(prod[:], kv[:, 0:D], q[:], ALU.mult))
                chain.link(dve, nc.vector.tensor_reduce(score[:], prod[:].rearrange("p (h d) -> p h d", h=HEADS), AX, ALU.add))
                nc.vector.tensor_tensor(less[:], score[:], high[:], ALU.subtract).then_inc(s.turned.sem, 1)
                dve.wait_ge(s.msg.sem, s.msg.at(i + 1))
                nc.vector.tensor_tensor(msg[:, 0:D].rearrange("p (h d) -> p h d", h=HEADS), kv[:, D:2 * D].rearrange("p (h d) -> p h d", h=HEADS),
                                        msg[:, D:D + HEADS].unsqueeze(2).to_broadcast([P, HEADS, HD]), ALU.mult).then_inc(s.masked.sem, 1)
            turns(dve, ET, tile)

        @block.scalar
        def _(act):
            def tile(i):
                act.wait_ge(s.turned.sem, s.turned.at(i + 1))
                nc.scalar.activation(msg[:, D:D + HEADS], less[:], ACT.Exp).then_inc(s.msg.sem, 1)
                act.wait_ge(s.joined.sem, s.joined.at(i + 1))
                nc.scalar.activation(total[:], total_ps[:], ACT.Copy).then_inc(s.summed.sem, 1)
            turns(act, ET, tile)
    chain.close(ET)
    s.scattered[0].close(16 * ET)
    for d in range(3):
        s.gathered[d].close(16 * ET)
    s.loaded.close(64 * ET)
    for sig in (s.summed, s.masked, s.joined, s.turned, s.msg):
        sig.close(ET)
def setup_constants(nc, g, inp):
    with ExitStack() as ctx:
        sb = lambda n, s, d=F32: ctx.enter_context(nc.sbuf_tensor(f"su_{n}", s, d))
        pb = lambda n, s: ctx.enter_context(nc.psum_tensor(f"su_{n}", s, F32))
        sem = lambda n: ctx.enter_context(nc.semaphore(f"su_{n}"))
        weights_in, edges_in, stored = sem("weights_in"), sem("edges_in"), sem("stored")
        zeroed, made, act_done, pe_done, dve = sem("zeroed"), sem("made"), sem("act_done"), sem("pe_done"), sem("dve")
        kt, vt = sb("kt", [D, 2, D]), sb("vt", [D, 2, D])
        rel = sb("rel", [D, 2, 2, D])
        relk, pri, skip = sb("relk", [D, 2, D]), sb("pri", [D, 2, D]), sb("skip", [P, 2])
        sig, dsig = sb("sig", [P, 2]), sb("dsig", [P, 1])
        w33u, u0, b33 = sb("w33u", [D, D]), sb("u0", [D, 1]), sb("b33", [D, 1])
        QR = NT // 4
        nt_i, nt_f = sb("nt_i", [QR, 4, P], I32), sb("nt_f", [QR, 4, P])
        raw = sb("raw", [P, 4, ET], I32)
        as_f = sb("as_f", [P, 4, ET])
        kvf = sb("kvf", [P, ET])
        ei, ec = sb("ei", [P, ET, 3], I32), sb("ec", [P, ET, 4])
        fold_ps, c_ps, t_ps = pb("fold_ps", [P, 2, 2, D]), pb("c_ps", [D, 1]), pb("t_ps", [P, 4, QR])
        NW = [0]
        block = ctx.enter_context(nc.Block())

        @block.sync
        def _(sp):
            for k, name in enumerate(("src", "dst", "edge_type_9", "edge_type_2")):
                sp.dma_start(raw[:, k], inp[name].rearrange("(p t) -> p t", p=P)).then_inc(edges_in, 16)
            sp.dma_start(nt_i[:], inp["node_type_2"].rearrange("(a b p) -> b a p", a=4, p=P)).then_inc(edges_in, 16)
            sp.wait_ge(zeroed, 1)

            def load(dst, src):
                sp.dma_start(dst, src).then_inc(weights_in, 16)
                NW[0] += 1
            W, B = inp["L0_gnn_weights"], inp["L0_gnn_biases"]
            for layer in range(3):
                for d in range(2):
                    base = R9 * (1 - d)
                    load(g.w0[0:D, layer, d], W[layer, base:base + R9:2].rearrange("g e f -> e g f"))
                    load(g.w0[D:P, layer, d, 0:NPAIR - 1], W[layer, base + 1:base + R9:2].rearrange("g e f -> e g f"))
                    load(g.b0[:, layer, d], B[layer, base:base + R9])
            col = lambda a: a.rearrange("(c a) -> c a", a=1)
            row = lambda a: a.rearrange("(a c) -> a c", a=1)
            load(g.w1[:], inp["L1_gnn_W1"])
            load(g.w2[:], inp["L1_gnn_W2"])
            load(g.w3[:], inp["L1_gnn_W3"])
            load(g.cb1[:], col(inp["L1_gnn_b1"]))
            load(g.gb1[:, 0:1], col(inp["L1_gnn_g1"]))
            load(g.gb1[:, 1:2], col(inp["L1_gnn_be1"]))
            load(g.cb2[:], col(inp["L1_gnn_b2"]))
            load(g.gb2[:, 0:1], col(inp["L1_gnn_g2"]))
            load(g.gb2[:, 1:2], col(inp["L1_gnn_be2"]))
            load(g.cb3[:], inp["L1_gnn_b3"].partition_broadcast(P))
            load(kt[:], inp["WkT"].rearrange("t o i -> o t i"))
            load(vt[:], inp["WvT"].rearrange("t o i -> o t i"))
            load(g.wqkv[:, 0:D], inp["L2_gnn_Wq"].rearrange("t i o -> (t i) o"))
            load(g.wa[:], inp["L2_gnn_Wa"].rearrange("t i o -> (t i) o"))
            for h in range(HEADS):
                b = slice(HD * h, HD * h + HD)
                load(rel[b, 0, :, b], inp["L2_gnn_Ratt"][h].rearrange("t d f -> d t f"))
                load(rel[b, 1, :, b], inp["L2_gnn_Rmsg"][h].rearrange("t d f -> d t f"))
            load(pri[:], inp["pri_rows"].partition_broadcast(D))
            load(skip[:], inp["L2_gnn_skip"].partition_broadcast(P))
            load(g.w31x[:], inp["L3_gnn_W1"][0:D, :])
            load(g.w31e[:], inp["L3_gnn_W1"][D:D + FE, :])
            load(g.b31[:], col(inp["L3_gnn_b1"]))
            load(g.w32[:], inp["L3_gnn_W2"])
            load(g.b32[:], inp["L3_gnn_b2"].partition_broadcast(P))
            load(g.w33[:], inp["L3_gnn_W3"][0:P, :])
            load(w33u[:], inp["L3_gnn_W3"][P:P + D, :])
            load(u0[:], inp["L3_gnn_u"][0:1, :].rearrange("a c -> c a"))
            load(b33[:], col(inp["L3_gnn_b3"]))
            load(g.w34[:], inp["L3_gnn_W4"])
            load(g.b34[:], inp["L3_gnn_b4"].partition_broadcast(P))
            n = 0
            for a in (*g.acc, g.acc68, g.count):
                sp.dma_start(a[NP:NR, :], g.zeros[:, 0:a.shape[1]]).then_inc(stored, 16)
                n += 1
            sp.wait_ge(zeroed, 2)
            sp.dma_start(g.high[NP:NR, :], g.lowest[:, 0:HEADS]).then_inc(stored, 16)
            sp.wait_ge(made, 1)
            sp.dma_start(g.edge_i.rearrange("(p t) c -> p (t c)", p=P), ei[:].rearrange("p t c -> p (t c)")).then_inc(stored, 16)
            sp.dma_start(g.edge_cols.rearrange("(p t) c -> p (t c)", p=P), ec[:].rearrange("p t c -> p (t c)")).then_inc(stored, 16)
            sp.dma_start(g.edge_rows.rearrange("c (p t) -> p c t", p=P), as_f[:, 0:3]).then_inc(stored, 16)
            sp.wait_ge(stored, 16 * (n + 4))

        @block.gpsimd
        def _(pool):
            pool.iota(g.pid_i[:], pattern=[[0, 1]], base=0, channel_multiplier=1).then_inc(g.pool_made, 1)
            pool.iota(g.iota_i[:], pattern=[[1, 3 * P]], base=0, channel_multiplier=0).then_inc(g.pool_made, 1)
            pool.memset(g.ident[:], 0.0)
            pool.memset(g.ones[:], 1.0)
            pool.memset(g.before[:], 1.0).then_inc(g.pool_made, 1)
            pool.wait_ge(g.pool_made, 3)
            pool.affine_select(out=g.ident[:], in_=g.ident[:], compare_op=ALU.not_equal, fill=1.0, base=0,
                               pattern=[[-1, P]], channel_multiplier=1).then_inc(g.pool_made, 1)
            pool.affine_select(out=g.before[:], in_=g.before[:], compare_op=ALU.is_gt, fill=0.0, base=0,
                               pattern=[[-1, P]], channel_multiplier=1).then_inc(g.pool_made, 1)

        @block.vector
        def _(v):
            nc.vector.memset(g.zeros[:], 0.0)
            nc.vector.memset(g.eps[:], EPS)
            nc.vector.memset(g.w0[:].rearrange("p a b c d -> p (a b c d)"), 0.0)
            nc.vector.memset(rel[:].rearrange("p a b c -> p (a b c)"), 0.0).then_inc(zeroed, 1)
            nc.vector.memset(g.lowest[:], LOWEST).then_inc(zeroed, 1)
            c = [0]

            def step(ins):
                c[0] += 1
                ins.then_inc(dve, 1)
                v.wait_ge(dve, c[0])
            for j in range(NPAIR):
                nc.vector.memset(g.type_of_row[0:D, j:j + 1], float(2 * j))
                step(nc.vector.memset(g.type_of_row[D:P, j:j + 1], float(2 * j + 1) if 2 * j + 1 < R9 else -1.0))
            v.wait_ge(g.pool_made, 5)
            nc.vector.tensor_copy(g.pid[:], g.pid_i[:])
            step(nc.vector.tensor_copy(g.iota_row[:], g.iota_i[:]))
            step(nc.vector.tensor_scalar(g.dump_row[:], g.pid[:], float(NP), None, ALU.add))
            v.wait_ge(edges_in, 16 * 5)
            step(nc.vector.tensor_copy(as_f[:], raw[:]))
            step(nc.vector.scalar_tensor_tensor(kvf[:], as_f[:, 0], 2.0, as_f[:, 3], ALU.mult, ALU.add))
            nc.vector.tensor_copy(ei[:, :, 0], raw[:, 0])
            nc.vector.tensor_copy(ei[:, :, 1], raw[:, 1])
            nc.vector.tensor_copy(ei[:, :, 2], kvf[:])
            for k in range(4):
                last = nc.vector.tensor_copy(ec[:, :, k], as_f[:, k])
            last.then_inc(made, 1)
            step(nc.vector.tensor_copy(nt_f[:], nt_i[:]))
            v.wait_ge(weights_in, 16 * NW[0])
            step(nc.vector.tensor_scalar(rel[:, 0], rel[:, 0], 1.0 / float(HD) ** 0.5, None, ALU.mult))
            nc.vector.tensor_tensor(relk[:], rel[:, 0], pri[:], ALU.mult).then_inc(made, 1)
            v.wait_ge(pe_done, 1)
            nc.vector.tensor_tensor(g.c3[:], c_ps[:], b33[:], ALU.add)
            step(nc.vector.tensor_copy(g.type1[:], t_ps[:].rearrange("p a b -> p (a b)")))
            v.wait_ge(act_done, 1)
            step(nc.vector.tensor_tensor(dsig[:], sig[:, 1:2], sig[:, 0:1], ALU.subtract))
            step(nc.vector.tensor_scalar(g.alpha[:], g.type1[:], dsig[:, 0:1], sig[:, 0:1], ALU.mult, ALU.add))
            nc.vector.tensor_scalar(g.beta[:], g.alpha[:], -1.0, 1.0, ALU.mult, ALU.add)

        @block.tensor
        def _(pe):
            pe.wait_ge(made, 2)
            pe.wait_ge(g.pool_made, 5)
            for t in range(2):
                for k, wt in enumerate((kt, vt)):
                    for r in range(2):
                        rhs = relk[:, r] if k == 0 else rel[:, 1, r]
                        nc.tensor.matmul(fold_ps[64 * t:64 * t + 64, r, k], wt[:, t], rhs, start=True, stop=True)
            nc.tensor.matmul(c_ps[:], w33u[:], u0[:], start=True, stop=True)
            for a in range(4):
                mm = nc.tensor.matmul(t_ps[:, a], nt_f[:, a], g.ident[0:QR, 0:QR], start=True, stop=True)
            mm.then_inc(pe_done, 1)

        @block.scalar
        def _(act):
            act.wait_ge(weights_in, 16 * NW[0])
            nc.scalar.activation(sig[:], skip[:], ACT.Sigmoid).then_inc(act_done, 1)
            act.wait_ge(pe_done, 1)
            nc.scalar.activation(g.wqkv[:, D:5 * D], fold_ps[:].rearrange("p a b c -> p (a b c)"), ACT.Copy)


def find_leaders(nc, g):
    with ExitStack() as ctx:
        sb = lambda n, s, d=F32: ctx.enter_context(nc.sbuf_tensor(f"fl_{n}", s, d))
        s = g.ns
        U = 8
        rows = [sb(f"rows{h}", [P, 2, U * P]) for h in range(2)]
        cols = [sb(f"cols{h}", [P, U, 4]) for h in range(2)]
        same, junk = sb("same", [P, P]), sb("junk", [P, P])
        prev, move, later = sb("prev", [P, U, 2]), sb("move", [P, U, 2]), sb("later", [P, U, 2])
        lead_f = sb("lead_f", [P, U, 2])
        lead_i = [sb(f"lead_i{h}", [P, U, 2], I32) for h in range(2)]
        TURNS = ET // U
        assert TURNS * U == ET and TURNS % 2 == 1
        chain = Chain(s.chain)
        block = ctx.enter_context(nc.Block())

        def pairs(eng, body):
            body(0, 0, 0)
            body(1, 0, 1)
            with eng.Fori(1, TURNS // 2) as i:
                body(2 * i, i, 0)
                body(2 * i + 1, i, 1)
            body(TURNS - 1, TURNS // 2, 0)

        @block.sync
        def _(sp):
            def turn(n, i, h):
                first = isinstance(i, int) and i == 0
                if not first:
                    sp.wait_ge(s.ready.sem, s.ready.at(n - 1)).then_inc(g.sp_gate, 1)
                e = bass.ts(n, U * P)
                sp.dma_start(rows[h][:], g.edge_rows[0:2, e].partition_broadcast(P)).then_inc(s.loaded[h].sem, 16)
                sp.dma_start(cols[h][:], g.edge_cols[e, :].rearrange("(u p) c -> p u c", p=P)).then_inc(s.loaded[h].sem, 16)
            pairs(sp, turn)
            sp.wait_ge(s.stored[0].sem, s.stored[0].at(16 * (TURNS // 2 + 1)))
            sp.wait_ge(s.stored[1].sem, s.stored[1].at(16 * (TURNS // 2)))

        @block.vector
        def _(dve):
            def turn(n, i, h):
                first = isinstance(i, int) and i == 0
                dve.wait_ge(s.loaded[h].sem, s.loaded[h].at(32 * (i + 1)))
                if not first:
                    dve.wait_ge(s.stored[h].sem, s.stored[h].at(16 * i))
                chain.turn(n)
                for u in range(U):
                    for d in range(2):
                        chain.link(dve, nc.vector.tensor_scalar(same[:], rows[h][:, 1 - d, u * P:(u + 1) * P], cols[h][:, u, 1 - d:2 - d],
                                                                None, ALU.is_equal))
                        chain.link(dve, nc.vector.tensor_tensor_reduce(junk[:], same[:], g.before[:], 1.0, 0.0, ALU.mult, ALU.add,
                                                                       prev[:, u, d:d + 1]))
                chain.link(dve, nc.vector.tensor_scalar(later[:], prev[:], 0.0, None, ALU.is_gt))
                for d in range(2):
                    last = nc.vector.tensor_scalar(move[:, :, d], cols[h][:, :, 1 - d], -1.0, g.dump_row[:, 0:1], ALU.mult, ALU.add)
                chain.link(dve, last)
                chain.link(dve, nc.vector.tensor_tensor(move[:], move[:], later[:], ALU.mult))
                for d in range(2):
                    last = nc.vector.tensor_tensor(lead_f[:, :, d], cols[h][:, :, 1 - d], move[:, :, d], ALU.add)
                chain.link(dve, last)
                nc.vector.tensor_copy(lead_i[h][:], lead_f[:]).then_inc(s.ready.sem, 1)
                dve.wait_ge(s.ready.sem, s.ready.at(n + 1))
            pairs(dve, turn)

        @block.scalar
        def _(act):
            def turn(n, i, h):
                first = isinstance(i, int) and i == 0
                act.wait_ge(s.ready.sem, s.ready.at(n + 1))
                act.dma_start(g.lead[bass.ts(n, U * P), :].rearrange("(u p) c -> p u c", p=P), lead_i[h][:]).then_inc(s.stored[h].sem, 16)
            pairs(act, turn)
    s.ready.close(TURNS)
    chain.close(TURNS)
    s.loaded[0].close(32 * (TURNS // 2 + 1))
    s.loaded[1].close(32 * (TURNS // 2))
    s.stored[0].close(16 * (TURNS // 2 + 1))
    s.stored[1].close(16 * (TURNS // 2))


def degrees(nc, g):
    with ExitStack() as ctx:
        QR = NT // 4
        rows = ctx.enter_context(nc.sbuf_tensor("dg_rows", [QR, 4, P], F32))
        count = ctx.enter_context(nc.sbuf_tensor("dg_count", [P, NT], F32))
        most, root = (ctx.enter_context(nc.sbuf_tensor(f"dg_{n}", [P, NT], F32)) for n in ("most", "root"))
        t_ps = ctx.enter_context(nc.psum_tensor("dg_ps", [P, 4, QR], F32))
        rooted = ctx.enter_context(nc.semaphore("dg_rooted"))
        read, turned, dve = (ctx.enter_context(nc.semaphore(f"dg_{n}")) for n in ("read", "turned", "dve"))
        block = ctx.enter_context(nc.Block())

        @block.sync
        def _(sp):
            sp.dma_start(rows[:], g.count[0:NP, :].rearrange("(a b p) o -> b a (p o)", a=4, p=P)).then_inc(read, 16)

        @block.tensor
        def _(pe):
            pe.wait_ge(read, 16)
            for a in range(4):
                mm = nc.tensor.matmul(t_ps[:, a], rows[:, a], g.ident[0:QR, 0:QR], start=True, stop=True)
            mm.then_inc(turned, 1)

        @block.vector
        def _(v):
            v.wait_ge(turned, 1)
            nc.vector.tensor_copy(count[:], t_ps[:].rearrange("p a b -> p (a b)")).then_inc(dve, 1)
            v.wait_ge(dve, 1)
            nc.vector.tensor_scalar(most[:], count[:], 1.0, None, ALU.max).then_inc(dve, 1)
            v.wait_ge(dve, 2)
            nc.vector.reciprocal(g.rcount[:], most[:])
            v.wait_ge(rooted, 1)
            nc.vector.reciprocal(g.dinv[:], root[:])

        @block.scalar
        def _(act):
            act.wait_ge(dve, 1)
            nc.scalar.activation(root[:], count[:], ACT.Sqrt, bias=g.ones[:, 0:1]).then_inc(rooted, 1)


def program(nc, inp, out):
    with ExitStack() as ctx:
        g = Env()
        sb = lambda n, s, d=F32: ctx.enter_context(nc.sbuf_tensor(n, s, d))
        dram = lambda n, s, d=F32: nc.dram_tensor(n, s, d, kind="Internal").ap()
        g.x, g.feat_t, g.out = inp["x"], inp["feat_t"], out
        g.T0, g.X, g.UT = dram("T0", [NP, D]), dram("X", [NP, D]), dram("UT", [P, NP])
        g.acc = [dram(f"acc{k}", [NR, D]) for k in range(2)]
        g.acc68, g.count, g.high = dram("acc68", [NR, D + HEADS]), dram("count", [NR, 1]), dram("high", [NR, HEADS])
        g.Q, g.KV = dram("Q", [NP, D]), dram("KV", [NP, 4 * D])
        g.KV2 = g.KV.rearrange("n (r c) -> (n r) c", r=2)
        g.edge_i, g.lead = dram("edge_i", [EP, 3], I32), dram("lead", [EP, 2], I32)
        g.edge_cols, g.edge_rows = dram("edge_cols", [EP, 4]), dram("edge_rows", [3, EP])
        g.pid_i, g.iota_i = sb("pid_i", [P, 1], I32), sb("iota_i", [P, 3 * P], I32)
        g.pid, g.iota_row, g.dump_row = sb("pid", [P, 1]), sb("iota_row", [P, 3 * P]), sb("dump_row", [P, 1])
        g.eps = sb("eps", [P, 1])
        g.ident, g.ones, g.before = sb("ident", [P, P]), sb("ones", [P, P]), sb("before", [P, P])
        g.zeros, g.lowest, g.type_of_row = sb("zeros", [P, G7 * (D + HEADS)]), sb("lowest", [P, G7 * HEADS]), sb("type_of_row", [P, NPAIR])
        g.w0, g.b0 = sb("w0", [P, 3, 2, NPAIR, D]), sb("b0", [R9, 3, 2, D])
        g.w1, g.w2, g.w3 = sb("w1", [D, P]), sb("w2", [P, D]), sb("w3", [D, D])
        g.cb1, g.gb1, g.cb2, g.gb2, g.cb3 = sb("cb1", [P, 1]), sb("gb1", [P, 2]), sb("cb2", [D, 1]), sb("gb2", [D, 2]), sb("cb3", [P, D])
        g.mv, g.bn = sb("mv", [P, 2]), sb("bn", [P, 4])
        g.wqkv, g.wa = sb("wqkv", [P, 5 * D]), sb("wa", [P, D])
        g.w31x, g.w31e, g.b31, g.w32, g.b32 = sb("w31x", [D, P]), sb("w31e", [FE, P]), sb("b31", [P, 1]), sb("w32", [P, D]), sb("b32", [P, D])
        g.w33, g.c3, g.w34, g.b34 = sb("w33", [P, D]), sb("c3", [D, 1]), sb("w34", [D, D]), sb("b34", [P, D])
        g.type1, g.alpha, g.beta, g.dinv, g.rcount = (sb(n, [P, NT]) for n in ("type1", "alpha", "beta", "dinv", "rcount"))
        g.sp_gate = ctx.enter_context(nc.semaphore("sp_gate"))
        g.pool_made = ctx.enter_context(nc.semaphore("pool_made"))
        g.ns, g.gs = Env(), Env()
        sg = lambda n: Signal(nc, ctx, n)
        n_, e_ = g.ns, g.gs
        n_.ready = sg("n_ready")
        n_.out = sg("n_out")
        n_.out2 = sg("n_out2")
        n_.turned = sg("n_turned")
        n_.half = sg("n_half")
        n_.product = sg("n_product")
        n_.chain = sg("n_chain")
        n_.stat = sg("n_stat")
        n_.squares = sg("n_squares")
        n_.root = sg("n_root")
        g.ns.loaded = [Signal(nc, ctx, f"n_loaded{h}") for h in range(2)]
        g.ns.stored = [Signal(nc, ctx, f"n_stored{h}") for h in range(2)]
        e_.loaded = sg("g_loaded")
        e_.gate = sg("g_gate")
        e_.summed = sg("g_summed")
        e_.turned = sg("g_turned")
        e_.masked = sg("g_masked")
        e_.product = sg("g_product")
        e_.msg = sg("g_msg")
        e_.joined = sg("g_joined")
        e_.chain = sg("g_chain")
        g.gs.gathered = [Signal(nc, ctx, f"g_gathered{d}") for d in range(3)]
        g.gs.scattered = [Signal(nc, ctx, f"g_scattered{d}") for d in range(2)]

        setup_constants(nc, g, inp)
        find_leaders(nc, g)
        stage_norm(nc, g, "n0", True, [])
        general_sum_edges(nc, g, "gc", None, g.count, 1, count=True)
        degrees(nc, g)
        for layer in range(3):
            general_transform_edges(nc, g, layer)
            if layer < 2:
                stage_norm(nc, g, f"n1{layer}", False, g.acc)
        stage_first_residual(nc, g)
        general_sum_edges(nc, g, "g1", g.T0, g.acc[0], D)
        stage_conv_stats(nc, g, "n3", P)
        stage_conv_next(nc, g, "n4", P, g.w2[:])
        general_sum_edges(nc, g, "g2", g.T0, g.acc[0], D)
        stage_conv_stats(nc, g, "n5", D)
        stage_conv_next(nc, g, "n6", D, g.w3[:])
        general_sum_edges(nc, g, "g3", g.T0, g.acc[0], D)
        stage_typed(nc, g)
        general_scores(nc, g)
        general_attend(nc, g)
        stage_attended(nc, g)
        general_sum_edges(nc, g, "g4", g.T0, g.acc[0], D, mlp=True)
        stage_last(nc, g)


def kernel(**inputs):
    import numpy as np
    import concourse.bacc as bacc
    from concourse import mybir as mb
    from concourse.bass_utils import run_bass_kernel_spmd

    a = {k: np.asarray(v) for k, v in inputs.items()}
    pad = NP - N
    own = np.arange(N, NP, dtype=np.int32)
    lay = {"x": np.concatenate([a["x"], np.zeros((pad, D), np.float32)]),
           "src": np.concatenate([a["src"], own]), "dst": np.concatenate([a["dst"], own]),
           "feat_t": np.concatenate([a["edge_attr_32"], np.zeros((pad, FE), np.float32)]).T,
           "WkT": a["L2_gnn_Wk"].transpose(0, 2, 1), "WvT": a["L2_gnn_Wv"].transpose(0, 2, 1),
           "pri_rows": np.repeat(a["L2_gnn_pri"].T, HD, axis=1).reshape(-1)}
    for n in ("edge_type_9", "edge_type_2", "node_type_2"):
        lay[n] = np.concatenate([a[n], np.zeros(pad, np.int32)])
    for n, v in a.items():
        if n[:2] in ("L0", "L1", "L2", "L3") and n not in ("L2_gnn_Wk", "L2_gnn_Wv", "L2_gnn_pri"):
            lay[n] = v
    nc = bacc.Bacc("TRN2", target_bir_lowering=False, num_devices=1)
    arrays, inp = {}, {}
    for n, v in lay.items():
        arrays[f"in_{n}"] = np.ascontiguousarray(v)
        inp[n] = nc.dram_tensor(f"in_{n}", v.shape, mb.dt.from_np(v.dtype), kind="ExternalInput").ap()
    out = nc.dram_tensor("out", (NP, D), mb.dt.float32, kind="ExternalOutput").ap()
    program(nc, inp, out)
    r = run_bass_kernel_spmd(nc, [arrays], core_ids=[0])
    return r.results[0]["out"][:N]
```

```python
from contextlib import ExitStack

import concourse.bass as bass
from concourse import mybir

ALU = mybir.AluOpType
ACT = mybir.ActivationFunctionType
F32 = mybir.dt.float32
I32 = mybir.dt.int32
U8 = mybir.dt.uint8
AX = mybir.AxisListType.X

P = 128
N = 50000
D = 64
G7 = 7
SN = G7 * P
NJ = -(-N // SN)
NP = NJ * SN
NT = NP // P
ET = NP // P
EP = ET * P
NR = NP + P
R9 = 9
NPAIR = 5
VALID_LAST = N - (NJ - 1) * SN
HEADS, HD = 4, 16
FE = 32
EPS = 1e-5
LEAK = 0.01
LOWEST = -3.0e38
WIN = 1024
KC = WIN // P
NC = NJ * KC
CR = NC // 4
BAND = 3


class Signal:

    def __init__(self, nc, ctx, name):
        self.sem = ctx.enter_context(nc.semaphore(name))
        self.base = 0

    def at(self, n):
        return n + self.base if self.base else n

    def close(self, n):
        self.base += n


class Chain:

    def __init__(self, steps):
        self.steps, self.per, self.n, self.loops = steps, 0, 0, 0

    def turn(self, i):
        if isinstance(i, int) and i == 0:
            self.first = True
        else:
            if self.first:
                self.per, self.first = self.n, False
        self.i, self.n = i, 0

    def link(self, eng, ins):
        self.n += 1
        ins.then_inc(self.steps.sem, 1)
        eng.wait_ge(self.steps.sem, self.steps.at(self.i * self.per + self.n))

    def close(self, turns):
        per = self.n if self.first else self.per
        assert self.first or self.n == self.per
        self.steps.close(per * turns)


def turns(eng, count, body):
    body(0)
    if count > 1:
        with eng.Fori(1, count) as i:
            body(i)
class Env:
    pass


def node_view(table, j, width=None):
    return table[bass.ts(j, SN), :].rearrange("(q p) d -> p q d", p=P)


def bc(ap, n=D):
    return ap.unsqueeze(2).to_broadcast([ap.shape[0], ap.shape[1], n])


def twice_over(ap):
    return ap.unsqueeze(2).to_broadcast([P, G7, 2, D])


def layernorm_relu(nc, g, dve, chain, n, x, xc, sq, st, out, twice=False):
    s = g.ns
    total, mean, ssq, std, rstd = (st[:, k] for k in range(5))
    chain.link(dve, nc.vector.tensor_reduce(total, x, AX, ALU.add))
    chain.link(dve, nc.vector.tensor_scalar(mean, total, 1.0 / D, None, ALU.mult))
    chain.link(dve, nc.vector.tensor_tensor(xc, x, bc(mean), ALU.subtract))
    chain.link(dve, nc.vector.tensor_tensor(sq, xc, xc, ALU.mult))
    nc.vector.tensor_reduce(ssq, sq, AX, ALU.add).then_inc(s.squares.sem, 1)
    dve.wait_ge(s.root.sem, s.root.at(n + 1))
    chain.link(dve, nc.vector.reciprocal(rstd, std))
    chain.link(dve, nc.vector.tensor_tensor(sq, xc, bc(rstd), ALU.mult))
    return nc.vector.tensor_scalar(out, twice_over(sq) if twice else sq, 0.0, None, ALU.max)


def deviation(nc, g, act, n, st):
    s = g.ns
    act.wait_ge(s.squares.sem, s.squares.at(n + 1))
    nc.scalar.activation(st[:, 3], st[:, 2], ACT.Sqrt, scale=1.0 / D, bias=g.eps[:, 0:1]).then_inc(s.root.sem, 1)


def node_programs(nc, g, block, loads, ns, read):
    s = g.ns

    @block.sync
    def _(sp):
        def pair(i):
            for h in range(2):
                if not isinstance(i, int):
                    sp.wait_ge(read.sem, read.at(2 * i + h - 1)).then_inc(g.sp_gate, 1)
                for dst, src in loads(2 * i + h, h):
                    sp.dma_start(dst, src).then_inc(s.loaded[h].sem, 16)
        turns(sp, NJ // 2, pair)
        for h in range(2):
            sp.wait_ge(s.stored[h].sem, s.stored[h].at(16 * ns * (NJ // 2)))


def node_close(s, nl, ns):
    for h in range(2):
        s.loaded[h].close(16 * nl * (NJ // 2))
        s.stored[h].close(16 * ns * (NJ // 2))


def stage_norm(nc, g, name, first, acc_in, relu_only=False):
    s = g.ns
    with ExitStack() as ctx:
        sb = lambda n, sh, d=F32: ctx.enter_context(nc.sbuf_tensor(f"{name}_{n}", sh, d))
        inp = [sb(f"inp{h}", [P, max(1, len(acc_in)), G7, D]) for h in range(2)]
        out = [sb(f"out{h}", [P, G7, 2, D]) for h in range(2)]
        xc, sq, st = sb("xc", [P, G7, D]), sb("sq", [P, G7, D]), sb("st", [P, 5, G7])
        chain = Chain(s.chain)
        zeroed = g.back[0] if first else []
        nl, ns = (len(acc_in) or 1), 1 + len(zeroed)

        def loads(j, h):
            if first:
                return [(inp[h][:, 0], node_view(g.x, j))]
            return [(inp[h][:, k], node_view(a, j)) for k, a in enumerate(acc_in)]
        block = ctx.enter_context(nc.Block())
        node_programs(nc, g, block, loads, ns, s.ready)

        @block.vector
        def _(dve):
            def pair(i):
                chain.turn(i)
                for h in range(2):
                    dve.wait_ge(s.loaded[h].sem, s.loaded[h].at(16 * nl * (i + 1)))
                    if not isinstance(i, int):
                        dve.wait_ge(s.stored[h].sem, s.stored[h].at(16 * ns * i))
                    if first:
                        last = layernorm_relu(nc, g, dve, chain, 2 * i + h, inp[h][:, 0], xc[:], sq[:], st, out[h][:], twice=True)
                    else:
                        cur = inp[h][:, 0]
                        for k in range(1, len(acc_in)):
                            chain.link(dve, nc.vector.tensor_tensor(xc[:], cur, inp[h][:, k], ALU.add))
                            cur = xc[:]
                        last = nc.vector.tensor_scalar(out[h][:], twice_over(cur), 0.0, None, ALU.max)
                    last.then_inc(s.ready.sem, 1)
                    dve.wait_ge(s.ready.sem, s.ready.at(2 * i + h + 1))
            turns(dve, NJ // 2, pair)

        @block.scalar
        def _(act):
            def pair(i):
                for h in range(2):
                    j = 2 * i + h
                    if first:
                        deviation(nc, g, act, j, st)
                    act.wait_ge(s.ready.sem, s.ready.at(j + 1))
                    act.dma_start(node_view(g.T2, j), out[h][:].rearrange("p q t d -> p q (t d)")).then_inc(s.stored[h].sem, 16)
                    for a in zeroed:
                        act.dma_start(node_view(a, j), g.zeros[:, 0:G7 * D].rearrange("p (q d) -> p q d", q=G7)).then_inc(s.stored[h].sem, 16)
            turns(act, NJ // 2, pair)
    chain.close(NJ // 2)
    node_close(s, nl, ns)
    s.ready.close(NJ)
    if first:
        s.squares.close(NJ)
        s.root.close(NJ)


def stage_first_residual(nc, g):
    s = g.ns
    name = "n2"
    with ExitStack() as ctx:
        sb = lambda n, sh, d=F32: ctx.enter_context(nc.sbuf_tensor(f"{name}_{n}", sh, d))
        accs = [g.acc, *g.back[2]]
        na = len(accs)
        inp = [sb(f"inp{h}", [P, 1 + na, G7, D]) for h in range(2)]
        x1 = [sb(f"x1{h}", [P, G7, D]) for h in range(2)]
        out = [sb(f"out{h}", [P, G7, D]) for h in range(2)]
        xc, sq, st, y = sb("xc", [P, G7, D]), sb("sq", [P, G7, D]), sb("st", [P, 5, G7]), sb("y", [P, G7, D])
        chain = Chain(s.chain)
        nl, ns = 1 + na, 2
        block = ctx.enter_context(nc.Block())
        node_programs(nc, g, block, lambda j, h: [(inp[h][:, 0], node_view(g.x, j))] + [
            (inp[h][:, 1 + k], node_view(a, j)) for k, a in enumerate(accs)], ns, s.ready)

        @block.vector
        def _(dve):
            def pair(i):
                chain.turn(i)
                for h in range(2):
                    dve.wait_ge(s.loaded[h].sem, s.loaded[h].at(16 * nl * (i + 1)))
                    if not isinstance(i, int):
                        dve.wait_ge(s.stored[h].sem, s.stored[h].at(16 * ns * i))
                    cur = inp[h][:, 1]
                    for k in range(1, na):
                        chain.link(dve, nc.vector.tensor_tensor(y[:], cur, inp[h][:, 1 + k], ALU.add))
                        cur = y[:]
                    chain.link(dve, nc.vector.tensor_tensor(x1[h][:], cur, inp[h][:, 0], ALU.add))
                    chain.link(dve, layernorm_relu(nc, g, dve, chain, 2 * i + h, x1[h][:], xc[:], sq[:], st, y[:]))
                    nc.vector.tensor_tensor(out[h][:], y[:], bc(g.dinv[:, bass.ts(2 * i + h, G7)]), ALU.mult).then_inc(s.ready.sem, 1)
                    dve.wait_ge(s.ready.sem, s.ready.at(2 * i + h + 1))
            turns(dve, NJ // 2, pair)

        @block.scalar
        def _(act):
            def pair(i):
                for h in range(2):
                    j = 2 * i + h
                    deviation(nc, g, act, j, st)
                    act.wait_ge(s.ready.sem, s.ready.at(2 * i + h + 1))
                    act.dma_start(node_view(g.X, j), x1[h][:]).then_inc(s.stored[h].sem, 16)
                    act.dma_start(node_view(g.T0, j), out[h][:]).then_inc(s.stored[h].sem, 16)
            turns(act, NJ // 2, pair)
    chain.close(NJ // 2)
    node_close(s, nl, ns)
    for sig in (s.ready, s.squares, s.root):
        sig.close(NJ)


def stage_conv_stats(nc, g, name, channels):
    s = g.ns
    HALF = SN // 2
    with ExitStack() as ctx:
        sb = lambda n, sh, d=F32: ctx.enter_context(nc.sbuf_tensor(f"{name}_{n}", sh, d))
        pb = lambda n, sh: ctx.enter_context(nc.psum_tensor(f"{name}_{n}", sh, F32))
        inp = [sb(f"inp{h}", [P, 2, G7, D]) for h in range(2)]
        y, agg = sb("y", [P, G7, D]), [sb(f"agg{h}", [P, G7, D]) for h in range(2)]
        agg_t = sb("agg_t", [D, SN])
        ut = [sb(f"ut{h}", [channels, SN]) for h in range(2)]
        stats = sb("stats", [channels, 2 * NJ, 6])
        agg_ps = [pb(f"agg_ps{k}", [D, 4 * P]) for k in range(2)]
        u_ps = [pb(f"u_ps{k}", [channels, HALF]) for k in range(2)]
        chain = Chain(s.chain)
        nl, ns = 2, 1
        block = ctx.enter_context(nc.Block())
        node_programs(nc, g, block, lambda j, h: [(inp[h][:, 0], node_view(g.T0, j)), (inp[h][:, 1], node_view(g.acc, j))], ns, s.ready)

        @block.vector
        def _(dve):
            def statistics(n, h):
                dve.wait_ge(s.out.sem, s.out.at(n + 1))
                for k in range(2):
                    last = nc.vector.bn_stats(stats[:, bass.ds(2 * n + k, 1), :].rearrange("c a s -> c (a s)"), ut[h][:, k * HALF:(k + 1) * HALF])
                last.then_inc(s.stat.sem, 1)

            def pair(i):
                chain.turn(i)
                for h in range(2):
                    dve.wait_ge(s.loaded[h].sem, s.loaded[h].at(16 * nl * (i + 1)))
                    if h or not isinstance(i, int):
                        dve.wait_ge(s.ready.sem, s.ready.at(2 * i + h))
                    chain.link(dve, nc.vector.tensor_tensor(y[:], inp[h][:, 0], inp[h][:, 1], ALU.add))
                    if not isinstance(i, int):
                        dve.wait_ge(s.turned.sem, s.turned.at(2 * i + h - 1))
                    nc.vector.tensor_tensor(agg[h][:], y[:], bc(g.dinv[:, bass.ts(2 * i + h, G7)]), ALU.mult).then_inc(s.ready.sem, 1)
                    if h or not isinstance(i, int):
                        statistics(2 * i + h - 1, 1 - h)
            turns(dve, NJ // 2, pair)
            statistics(NJ - 1, 1)
            h = 1
            assert VALID_LAST > HALF
            dve.wait_ge(s.stat.sem, s.stat.at(NJ))
            nc.vector.bn_stats(stats[:, 2 * NJ - 1, :], ut[h][:, HALF:VALID_LAST]).then_inc(s.stat.sem, 1)
            dve.wait_ge(s.stat.sem, s.stat.at(NJ + 1))
            nc.vector.bn_aggr(g.mv[0:channels, :], stats[:].rearrange("c a s -> c (a s)")).then_inc(s.stat.sem, 1)
            mv, gb = g.mv, g.gb1 if channels == P else g.gb2
            step = lambda n, ins: (ins.then_inc(s.stat.sem, 1), dve.wait_ge(s.stat.sem, s.stat.at(NJ + 2 + n)))
            dve.wait_ge(s.root.sem, s.root.at(1))
            step(1, nc.vector.reciprocal(g.bn[0:channels, 2:3], g.bn[0:channels, 3:4]))
            step(2, nc.vector.tensor_tensor(g.bn[0:channels, 0:1], g.bn[0:channels, 2:3], gb[0:channels, 0:1], ALU.mult))
            step(3, nc.vector.tensor_tensor(g.bn[0:channels, 3:4], mv[0:channels, 0:1], g.bn[0:channels, 0:1], ALU.mult))
            step(4, nc.vector.tensor_tensor(g.bn[0:channels, 1:2], gb[0:channels, 1:2], g.bn[0:channels, 3:4], ALU.subtract))

        @block.tensor
        def _(pe):
            def pair(i):
                for h in range(2):
                    n = 2 * i + h
                    pe.wait_ge(s.ready.sem, s.ready.at(n + 1))
                    if h or not isinstance(i, int):
                        pe.wait_ge(s.half.sem, s.half.at(n))
                        pe.wait_ge(s.out.sem, s.out.at(n))
                    for q in range(G7):
                        mm = nc.tensor.matmul(agg_ps[q // 4][:, bass.ts(q % 4, P)], agg[h][:, q], g.ident[:], start=True, stop=True)
                    mm.then_inc(s.turned.sem, 1)
                    if channels == P:
                        pe.wait_ge(s.half.sem, s.half.at(n + 1))
                        for k in range(2):
                            mm = nc.tensor.matmul(u_ps[k][:], g.w1[:], agg_t[:, k * HALF:(k + 1) * HALF], start=True, stop=True)
                        mm.then_inc(s.product.sem, 1)
            turns(pe, NJ // 2, pair)

        @block.scalar
        def _(act):
            def pair(i):
                for h in range(2):
                    n = 2 * i + h
                    act.wait_ge(s.turned.sem, s.turned.at(n + 1))
                    if not isinstance(i, int):
                        act.wait_ge(s.stored[h].sem, s.stored[h].at(16 * ns * i))
                        act.wait_ge(s.stat.sem, s.stat.at(n - 1))
                    if channels == P:
                        nc.scalar.activation(agg_t[:, 0:4 * P], agg_ps[0][:], ACT.Copy)
                        nc.scalar.activation(agg_t[:, 4 * P:SN], agg_ps[1][:, 0:3 * P], ACT.Copy).then_inc(s.half.sem, 1)
                        act.wait_ge(s.product.sem, s.product.at(n + 1))
                        for k in range(2):
                            last = nc.scalar.activation(ut[h][:, k * HALF:(k + 1) * HALF], u_ps[k][:], ACT.Identity, bias=g.cb1[:, 0:1])
                    else:
                        nc.scalar.activation(ut[h][:, 0:4 * P], agg_ps[0][:], ACT.Identity, bias=g.cb2[0:D, 0:1])
                        last = nc.scalar.activation(ut[h][:, 4 * P:SN], agg_ps[1][:, 0:3 * P], ACT.Identity, bias=g.cb2[0:D, 0:1])
                        last.then_inc(s.half.sem, 1)
                    if channels == P:
                        last.then_inc(s.out.sem, 1)
                    else:
                        act.wait_ge(s.half.sem, s.half.at(n + 1)).then_inc(s.out.sem, 1)
                    act.wait_ge(s.out.sem, s.out.at(n + 1))
                    act.dma_start(g.UT[0:channels, bass.ts(n, SN)], ut[h][:]).then_inc(s.stored[h].sem, 16)
            turns(act, NJ // 2, pair)
            act.wait_ge(s.stat.sem, s.stat.at(NJ + 2))
            nc.scalar.activation(g.bn[0:channels, 3:4], g.mv[0:channels, 1:2], ACT.Sqrt, bias=g.eps[0:channels, 0:1]).then_inc(s.root.sem, 1)
    chain.close(NJ // 2)
    node_close(s, nl, ns)
    s.root.close(1)
    for sig in (s.ready, s.turned, s.half, s.out):
        sig.close(NJ)
    if channels == P:
        s.product.close(NJ)
    s.stat.close(NJ + 6)


def stage_conv_next(nc, g, name, channels, weight):
    s = g.ns
    with ExitStack() as ctx:
        sb = lambda n, sh, d=F32: ctx.enter_context(nc.sbuf_tensor(f"{name}_{n}", sh, d))
        pb = lambda n, sh: ctx.enter_context(nc.psum_tensor(f"{name}_{n}", sh, F32))
        ut = [sb(f"ut{h}", [channels, SN]) for h in range(2)]
        lin, z = sb("lin", [channels, SN]), sb("z", [channels, SN])
        out = [sb(f"out{h}", [P, G7, D]) for h in range(2)]
        v_ps = pb("v_ps", [P, G7, D])
        chain = Chain(s.chain)
        nl, ns = 1, 1
        block = ctx.enter_context(nc.Block())
        node_programs(nc, g, block, lambda j, h: [(ut[h][:], g.UT[0:channels, bass.ts(j, SN)])], ns, s.ready)

        @block.scalar
        def _(act):
            def pair(i):
                for h in range(2):
                    n = 2 * i + h
                    act.wait_ge(s.loaded[h].sem, s.loaded[h].at(16 * nl * (i + 1)))
                    if h or not isinstance(i, int):
                        act.wait_ge(s.half.sem, s.half.at(n))
                    nc.scalar.activation(lin[:], ut[h][:], ACT.Identity, bias=g.bn[0:channels, 1:2], scale=g.bn[0:channels, 0:1]).then_inc(s.ready.sem, 1)
                    act.wait_ge(s.out.sem, s.out.at(n + 1))
                    act.dma_start(node_view(g.T0, n), out[h][:]).then_inc(s.stored[h].sem, 16)
            turns(act, NJ // 2, pair)

        @block.vector
        def _(dve):
            def pair(i):
                for h in range(2):
                    n = 2 * i + h
                    dve.wait_ge(s.ready.sem, s.ready.at(n + 1))
                    if h or not isinstance(i, int):
                        dve.wait_ge(s.product.sem, s.product.at(n))
                    nc.vector.scalar_tensor_tensor(z[:], lin[:], LEAK, lin[:], ALU.mult, ALU.max).then_inc(s.half.sem, 1)
                    dve.wait_ge(s.product.sem, s.product.at(n + 1))
                    if not isinstance(i, int):
                        dve.wait_ge(s.stored[h].sem, s.stored[h].at(16 * ns * i))
                    nc.vector.tensor_tensor(out[h][:], v_ps[:], bc(g.dinv[:, bass.ts(n, G7)]), ALU.mult).then_inc(s.out.sem, 1)
            turns(dve, NJ // 2, pair)

        @block.tensor
        def _(pe):
            def pair(i):
                for h in range(2):
                    n = 2 * i + h
                    pe.wait_ge(s.half.sem, s.half.at(n + 1))
                    if h or not isinstance(i, int):
                        pe.wait_ge(s.out.sem, s.out.at(n))
                    for q in range(G7):
                        mm = nc.tensor.matmul(v_ps[:, q], z[:, bass.ts(q, P)], weight, start=True, stop=True)
                    mm.then_inc(s.product.sem, 1)
            turns(pe, NJ // 2, pair)
    node_close(s, nl, ns)
    for sig in (s.ready, s.half, s.out, s.product):
        sig.close(NJ)


def stage_typed(nc, g):
    s = g.ns
    name = "n7"
    with ExitStack() as ctx:
        sb = lambda n, sh, d=F32: ctx.enter_context(nc.sbuf_tensor(f"{name}_{n}", sh, d))
        pb = lambda n, sh: ctx.enter_context(nc.psum_tensor(f"{name}_{n}", sh, F32))
        inp = [sb(f"inp{h}", [P, 3, G7, D]) for h in range(2)]
        xo = [sb(f"xo{h}", [P, G7, D]) for h in range(2)]
        q_out = [sb(f"q_out{h}", [P, G7, D]) for h in range(2)]
        kv_out = [sb(f"kv_out{h}", [P, G7, 4 * D]) for h in range(2)]
        xc, sq, st, y, hh = sb("xc", [P, G7, D]), sb("sq", [P, G7, D]), sb("st", [P, 5, G7]), sb("y", [P, G7, D]), sb("hh", [P, G7, D])
        typed, typed_t = [sb(f"typed{h}", [P, G7, 2, D]) for h in range(2)], sb("typed_t", [P, G7, P])
        t_ps = [pb(f"t_ps{k}", [P, 4, P]) for k in range(2)]
        o_ps = [pb(f"o_ps{k}", [P, 5 * D]) for k in range(4)]
        chain = Chain(s.chain)
        nl, ns = 3, 3
        block = ctx.enter_context(nc.Block())
        node_programs(nc, g, block, lambda j, h: [(inp[h][:, 0], node_view(g.X, j)), (inp[h][:, 1], node_view(g.T0, j)),
                                                  (inp[h][:, 2], node_view(g.acc, j))], ns, s.out)

        @block.vector
        def _(dve):
            def pair(i):
                chain.turn(i)
                for h in range(2):
                    n = 2 * i + h
                    dve.wait_ge(s.loaded[h].sem, s.loaded[h].at(16 * nl * (i + 1)))
                    if not isinstance(i, int):
                        dve.wait_ge(s.stored[h].sem, s.stored[h].at(16 * ns * i))
                    L = lambda ins: chain.link(dve, ins)
                    cols = bass.ts(n, G7)
                    L(nc.vector.tensor_tensor(y[:], inp[h][:, 1], inp[h][:, 2], ALU.add))
                    L(nc.vector.tensor_tensor(y[:], y[:], bc(g.dinv[:, cols]), ALU.mult))
                    L(nc.vector.tensor_tensor(y[:], y[:], g.cb3[:].unsqueeze(1).to_broadcast([P, G7, D]), ALU.add))
                    L(nc.vector.tensor_tensor(y[:], y[:], inp[h][:, 0], ALU.add))
                    L(layernorm_relu(nc, g, dve, chain, n, y[:], xc[:], sq[:], st, hh[:]))
                    if not isinstance(i, int):
                        dve.wait_ge(s.turned.sem, s.turned.at(2 * (n - 1)))
                    L(nc.vector.tensor_tensor(typed[h][:, :, 1], hh[:], bc(g.type1[:, cols]), ALU.mult))
                    nc.vector.tensor_tensor(typed[h][:, :, 0], hh[:], typed[h][:, :, 1], ALU.subtract).then_inc(s.ready.sem, 1)
                    L(nc.vector.tensor_tensor(sq[:], hh[:], bc(g.beta[:, cols]), ALU.mult))
                    nc.vector.tensor_tensor(xo[h][:], y[:], sq[:], ALU.add).then_inc(s.out.sem, 1)
                    dve.wait_ge(s.out.sem, s.out.at(n + 1))
            turns(dve, NJ // 2, pair)

        @block.tensor
        def _(pe):
            def pair(i):
                for h in range(2):
                    n = 2 * i + h
                    pe.wait_ge(s.ready.sem, s.ready.at(n + 1))
                    if h or not isinstance(i, int):
                        pe.wait_ge(s.half.sem, s.half.at(2 * n))
                    for k in range(2):
                        for q in range(4 * k, min(G7, 4 * k + 4)):
                            mm = nc.tensor.transpose(t_ps[k][:, q % 4], typed[h][:, q].rearrange("p t d -> p (t d)"), g.ident[:])
                        mm.then_inc(s.turned.sem, 1)
                    for q in range(G7):
                        pe.wait_ge(s.half.sem, s.half.at(2 * n + q // 4 + 1))
                        if q >= 4:
                            pe.wait_ge(s.out2.sem, s.out2.at(G7 * n + q - 3))
                        elif h or not isinstance(i, int):
                            pe.wait_ge(s.out2.sem, s.out2.at(G7 * n))
                        nc.tensor.matmul(o_ps[q % 4][:], typed_t[:, q], g.wqkv[:], start=True, stop=True).then_inc(s.product.sem, 1)
            turns(pe, NJ // 2, pair)

        @block.scalar
        def _(act):
            def pair(i):
                first, final = isinstance(i, int) and i == 0, isinstance(i, int) and i > 0
                for h in range(2):
                    n = 2 * i + h
                    for k in range(2):
                        act.wait_ge(s.turned.sem, s.turned.at(2 * n + k + 1))
                        if k == 0 and (h or not first):
                            act.wait_ge(s.product.sem, s.product.at(G7 * n))
                        m = min(G7, 4 * k + 4) - 4 * k
                        nc.scalar.activation(typed_t[:, 4 * k:4 * k + m], t_ps[k][:, 0:m], ACT.Copy).then_inc(s.half.sem, 1)
                    if not first:
                        act.wait_ge(s.stored[h].sem, s.stored[h].at(16 * ns * i))
                    for q in range(G7):
                        act.wait_ge(s.product.sem, s.product.at(G7 * n + q + 1))
                        nc.scalar.activation(q_out[h][:, q], o_ps[q % 4][:, 0:D], ACT.Copy)
                        nc.scalar.activation(kv_out[h][:, q], o_ps[q % 4][:, D:5 * D], ACT.Copy).then_inc(s.out2.sem, 1)
                        if q == G7 - 1 and not (final and h):
                            deviation(nc, g, act, n + 1, st)
                    act.wait_ge(s.out2.sem, s.out2.at(G7 * n + G7))
                    act.wait_ge(s.out.sem, s.out.at(n + 1))
                    act.dma_start(node_view(g.X, n), xo[h][:]).then_inc(s.stored[h].sem, 16)
                    act.dma_start(node_view(g.Q, n), q_out[h][:]).then_inc(s.stored[h].sem, 16)
                    act.dma_start(node_view(g.KV, n), kv_out[h][:]).then_inc(s.stored[h].sem, 16)
            deviation(nc, g, act, 0, st)
            pair(0)
            with act.Fori(1, NJ // 2 - 1) as i:
                pair(i)
            pair(NJ // 2 - 1)
    chain.close(NJ // 2)
    node_close(s, nl, ns)
    s.ready.close(NJ)
    s.out.close(NJ)
    s.turned.close(2 * NJ)
    s.half.close(2 * NJ)
    s.squares.close(NJ)
    s.root.close(NJ)
    for sig in (s.product, s.out2):
        sig.close(G7 * NJ)


def stage_attended(nc, g):
    s = g.ns
    name = "n8"
    with ExitStack() as ctx:
        sb = lambda n, sh, d=F32: ctx.enter_context(nc.sbuf_tensor(f"{name}_{n}", sh, d))
        pb = lambda n, sh: ctx.enter_context(nc.psum_tensor(f"{name}_{n}", sh, F32))
        acc = [sb(f"acc{h}", [P, G7, D + HEADS]) for h in range(2)]
        x_in = [sb(f"x_in{h}", [P, G7, D]) for h in range(2)]
        xo, out = ([sb(f"{m}{h}", [P, G7, D]) for h in range(2)] for m in ("xo", "out"))
        xc, sq, st, y = sb("xc", [P, G7, D]), sb("sq", [P, G7, D]), sb("st", [P, 5, G7]), sb("y", [P, G7, D])
        den, rden = sb("den", [P, G7, HEADS]), sb("rden", [P, G7, HEADS])
        typed, typed_t = sb("typed", [P, G7, 2, D]), sb("typed_t", [P, G7, P])
        t_ps = [pb(f"t_ps{k}", [P, 4, P]) for k in range(2)]
        o_ps = pb("o_ps", [P, G7, D])
        chain = Chain(s.chain)
        nl, ns = 2, 2
        block = ctx.enter_context(nc.Block())
        node_programs(nc, g, block, lambda j, h: [(acc[h][:], node_view(g.acc68, j)), (x_in[h][:], node_view(g.X, j))], ns, s.out)

        @block.vector
        def _(dve):
            def pair(i):
                chain.turn(i)
                for h in range(2):
                    n = 2 * i + h
                    L = lambda ins: chain.link(dve, ins)
                    cols = bass.ts(n, G7)
                    dve.wait_ge(s.loaded[h].sem, s.loaded[h].at(16 * nl * (i + 1)))
                    L(nc.vector.tensor_scalar(den[:], acc[h][:, :, D:D + HEADS], 1e-30, None, ALU.max))
                    L(nc.vector.reciprocal(rden[:], den[:]))
                    for hd in range(HEADS):
                        r = slice(HD * hd, HD * hd + HD)
                        last = nc.vector.tensor_tensor(y[:, :, r], acc[h][:, :, r], rden[:, :, hd:hd + 1].to_broadcast([P, G7, HD]), ALU.mult)
                    L(last)
                    L(nc.vector.tensor_tensor(typed[:, :, 1], y[:], bc(g.type1[:, cols]), ALU.mult))
                    nc.vector.tensor_tensor(typed[:, :, 0], y[:], typed[:, :, 1], ALU.subtract).then_inc(s.ready.sem, 1)
                    dve.wait_ge(s.product.sem, s.product.at(n + 1))
                    L(nc.vector.tensor_tensor(xc[:], o_ps[:], bc(g.alpha[:, cols]), ALU.mult))
                    if not isinstance(i, int):
                        dve.wait_ge(s.stored[h].sem, s.stored[h].at(16 * ns * i))
                    L(nc.vector.tensor_tensor(xo[h][:], xc[:], x_in[h][:], ALU.add))
                    layernorm_relu(nc, g, dve, chain, n, xo[h][:], xc[:], sq[:], st, out[h][:]).then_inc(s.out.sem, 1)
                    dve.wait_ge(s.out.sem, s.out.at(n + 1))
            turns(dve, NJ // 2, pair)

        @block.tensor
        def _(pe):
            def pair(i):
                for h in range(2):
                    n = 2 * i + h
                    pe.wait_ge(s.ready.sem, s.ready.at(n + 1))
                    for k in range(2):
                        for q in range(4 * k, min(G7, 4 * k + 4)):
                            mm = nc.tensor.transpose(t_ps[k][:, q % 4], typed[:, q].rearrange("p t d -> p (t d)"), g.ident[:])
                        mm.then_inc(s.turned.sem, 1)
                    for q in range(G7):
                        pe.wait_ge(s.half.sem, s.half.at(2 * n + q // 4 + 1))
                        mm = nc.tensor.matmul(o_ps[:, q], typed_t[:, q], g.wa[:], start=True, stop=True)
                    mm.then_inc(s.product.sem, 1)
            turns(pe, NJ // 2, pair)

        @block.scalar
        def _(act):
            def pair(i):
                for h in range(2):
                    n = 2 * i + h
                    for k in range(2):
                        act.wait_ge(s.turned.sem, s.turned.at(2 * n + k + 1))
                        m = min(G7, 4 * k + 4) - 4 * k
                        nc.scalar.activation(typed_t[:, 4 * k:4 * k + m], t_ps[k][:, 0:m], ACT.Copy).then_inc(s.half.sem, 1)
                    deviation(nc, g, act, n, st)
                    act.wait_ge(s.out.sem, s.out.at(n + 1))
                    act.dma_start(node_view(g.X, n), xo[h][:]).then_inc(s.stored[h].sem, 16)
                    act.dma_start(node_view(g.T0, n), out[h][:]).then_inc(s.stored[h].sem, 16)
            turns(act, NJ // 2, pair)
    chain.close(NJ // 2)
    node_close(s, nl, ns)
    for sig in (s.ready, s.product, s.out, s.squares, s.root):
        sig.close(NJ)
    s.turned.close(2 * NJ)
    s.half.close(2 * NJ)


def stage_last(nc, g):
    s = g.ns
    name = "n9"
    HALF = SN // 2
    with ExitStack() as ctx:
        sb = lambda n, sh, d=F32: ctx.enter_context(nc.sbuf_tensor(f"{name}_{n}", sh, d))
        pb = lambda n, sh: ctx.enter_context(nc.psum_tensor(f"{name}_{n}", sh, F32))
        inp = [sb(f"inp{h}", [P, G7, D]) for h in range(2)]
        both = [sb(f"both{h}", [P, G7, 2, D]) for h in range(2)]
        x_in = [sb(f"x_in{h}", [P, G7, D]) for h in range(2)]
        out = [sb(f"out{h}", [P, G7, D]) for h in range(2)]
        y, both_t, hid = sb("y", [P, G7, D]), sb("both_t", [P, SN]), sb("hid", [D, SN])
        t_ps = [pb(f"t_ps{k}", [P, 4 * P]) for k in range(2)]
        h_ps = [pb(f"h_ps{k}", [D, HALF]) for k in range(2)]
        o_ps = pb("o_ps", [P, G7, D])
        nl, ns = 3, 1
        block = ctx.enter_context(nc.Block())
        node_programs(nc, g, block, lambda j, h: [(both[h][:, :, 0], node_view(g.T0, j)), (inp[h][:], node_view(g.acc, j)),
                                                  (x_in[h][:], node_view(g.X, j))], ns, s.out)

        @block.vector
        def _(dve):
            def add_up(n, h, i):
                dve.wait_ge(s.product.sem, s.product.at(2 * n + 2))
                if not (isinstance(n, int) and n == 0):
                    dve.wait_ge(s.out.sem, s.out.at(n))
                nc.vector.tensor_tensor(y[:], o_ps[:], g.b34[:].unsqueeze(1).to_broadcast([P, G7, D]), ALU.add).then_inc(s.chain.sem, 1)
                dve.wait_ge(s.chain.sem, s.chain.at(n + 1))
                if not (isinstance(n, int) and n < 2):
                    dve.wait_ge(s.stored[h].sem, s.stored[h].at(16 * ns * i))
                nc.vector.tensor_tensor(out[h][:], y[:], x_in[h][:], ALU.add).then_inc(s.out.sem, 1)

            def pair(i):
                for h in range(2):
                    n = 2 * i + h
                    dve.wait_ge(s.loaded[h].sem, s.loaded[h].at(16 * nl * (i + 1)))
                    nc.vector.tensor_tensor(both[h][:, :, 1], inp[h][:], bc(g.rcount[:, bass.ts(n, G7)]), ALU.mult).then_inc(s.ready.sem, 1)
                    if h or not isinstance(i, int):
                        add_up(n - 1, 1 - h, i if h else i - 1)
            turns(dve, NJ // 2, pair)
            add_up(NJ - 1, 1, NJ // 2 - 1)

        @block.tensor
        def _(pe):
            def pair(i):
                for h in range(2):
                    n = 2 * i + h
                    pe.wait_ge(s.ready.sem, s.ready.at(n + 1))
                    for q in range(G7):
                        mm = nc.tensor.transpose(t_ps[q // 4][:, bass.ts(q % 4, P)], both[h][:, q].rearrange("p t d -> p (t d)"), g.ident[:])
                    mm.then_inc(s.turned.sem, 1)
                    pe.wait_ge(s.half.sem, s.half.at(2 * n + 1))
                    for k in range(2):
                        mm = nc.tensor.matmul(h_ps[k][:], g.w33[:], both_t[:, k * HALF:(k + 1) * HALF], start=True, stop=True)
                    mm.then_inc(s.product.sem, 1)
                    pe.wait_ge(s.half.sem, s.half.at(2 * n + 2))
                    if h or not isinstance(i, int):
                        pe.wait_ge(s.out.sem, s.out.at(n))
                    for q in range(G7):
                        mm = nc.tensor.matmul(o_ps[:, q], hid[:, bass.ts(q, P)], g.w34[:], start=True, stop=True)
                    mm.then_inc(s.product.sem, 1)
            turns(pe, NJ // 2, pair)

        @block.scalar
        def _(act):
            def pair(i):
                for h in range(2):
                    n = 2 * i + h
                    act.wait_ge(s.turned.sem, s.turned.at(n + 1))
                    nc.scalar.activation(both_t[:, 0:4 * P], t_ps[0][:], ACT.Copy)
                    nc.scalar.activation(both_t[:, 4 * P:SN], t_ps[1][:, 0:3 * P], ACT.Copy).then_inc(s.half.sem, 1)
                    act.wait_ge(s.product.sem, s.product.at(2 * n + 1))
                    for k in range(2):
                        last = nc.scalar.activation(hid[:, k * HALF:(k + 1) * HALF], h_ps[k][:], ACT.Relu, bias=g.c3[0:D, 0:1])
                    last.then_inc(s.half.sem, 1)
                    act.wait_ge(s.out.sem, s.out.at(n + 1))
                    act.dma_start(node_view(g.out, n), out[h][:]).then_inc(s.stored[h].sem, 16)
            turns(act, NJ // 2, pair)
    s.chain.close(NJ)
    node_close(s, nl, ns)
    s.ready.close(NJ)
    s.turned.close(NJ)
    s.out.close(NJ)
    s.product.close(2 * NJ)
    s.half.close(2 * NJ)
def general_transform_edges(nc, env, layer):
    g = env
    with ExitStack() as ctx:
        sb = lambda n, s, d=F32: ctx.enter_context(nc.sbuf_tensor(f"ge{layer}_{n}", s, d))
        pb = lambda n, s: ctx.enter_context(nc.psum_tensor(f"ge{layer}_{n}", s, F32))
        edge_i, lead, rows, cols = sb("edge_i", [P, 3], I32), sb("lead", [P, 2], I32), sb("rows", [P, 3, P]), sb("cols", [P, 4])
        far = sb("far", [P, 2, 2 * D])
        masked, onehot, same = sb("masked", [P, NPAIR, P]), sb("onehot", [R9, P]), sb("same", [P, P])
        msg, total = sb("msg", [P, D]), sb("total", [P, 2, D])
        far_t, msg_ps, total_ps = pb("far_t", [P, P]), pb("msg_ps", [P, D]), pb("total_ps", [P, D])
        s = g.gs
        block = ctx.enter_context(nc.Block())

        @block.sync
        def _(sp):
            def tile(i):
                if not isinstance(i, int):
                    sp.wait_ge(s.scattered[0].sem, s.scattered[0].at(16 * i)).then_inc(g.sp_gate, 1)
                    sp.wait_ge(s.scattered[1].sem, s.scattered[1].at(16 * i)).then_inc(g.sp_gate, 1)
                e = bass.ts(i, P)
                sp.dma_start(edge_i[:], g.edge_i[e, :]).then_inc(s.loaded.sem, 16)
                sp.dma_start(lead[:], g.lead[e, :]).then_inc(s.loaded.sem, 16)
                sp.dma_start(rows[:], g.edge_rows[:, e].partition_broadcast(P)).then_inc(s.loaded.sem, 16)
                sp.dma_start(cols[:], g.edge_cols[e, :]).then_inc(s.loaded.sem, 16)
            turns(sp, ET, tile)
            for d in range(2):
                sp.wait_ge(s.scattered[d].sem, s.scattered[d].at(16 * ET))

        @block.gpsimd
        def _(pool):
            def tile(i):
                pool.wait_ge(s.loaded.sem, s.loaded.at(64 * i + 64)).then_inc(s.gate.sem, 1)
                for d in range(2):
                    pool.indirect_dma_start(out=far[:, d], out_offset=None, in_=g.T2[:], in_offset=bass.IndirectOffsetOnAxis(
                        ap=edge_i[:, d:d + 1], axis=0)).then_inc(s.gathered[d].sem, 16)
                for d in range(2):
                    pool.wait_ge(s.summed.sem, s.summed.at(2 * i + d + 1)).then_inc(s.gate.sem, 1)
                    pool.indirect_dma_start(out=(g.acc, g.back[layer][0])[d][:], out_offset=bass.IndirectOffsetOnAxis(ap=lead[:, d:d + 1], axis=0),
                                            in_=total[:, d], in_offset=None, compute_op=ALU.add).then_inc(s.scattered[d].sem, 16)
            turns(pool, ET, tile)

        @block.tensor
        def _(pe):
            def tile(i):
                for d in range(2):
                    pe.wait_ge(s.gathered[d].sem, s.gathered[d].at(16 * i + 16))
                    nc.tensor.transpose(far_t[:], far[:, d], g.ident[:]).then_inc(s.turned.sem, 1)
                    pe.wait_ge(s.masked.sem, s.masked.at(2 * i + d + 1))
                    for j in range(NPAIR):
                        nc.tensor.matmul(msg_ps[:], masked[:, j], g.w0[:, layer, d, j], start=(j == 0), stop=False)
                    nc.tensor.matmul(msg_ps[:], onehot[:], g.b0[:, layer, d], start=False, stop=True).then_inc(s.product.sem, 1)
                    pe.wait_ge(s.msg.sem, s.msg.at(2 * i + d + 1))
                    nc.tensor.matmul(total_ps[:], same[:], msg[:], start=True, stop=True).then_inc(s.joined.sem, 1)
            turns(pe, ET, tile)

        @block.vector
        def _(dve):
            def tile(i):
                for d in range(2):
                    dve.wait_ge(s.turned.sem, s.turned.at(2 * i + d + 1))
                    dve.wait_ge(s.loaded.sem, s.loaded.at(64 * i + 64))
                    if d or not isinstance(i, int):
                        dve.wait_ge(s.joined.sem, s.joined.at(2 * i + d))
                    nc.vector.tensor_scalar(same[:], rows[:, 1 - d], cols[:, 1 - d:2 - d], None, ALU.is_equal)
                    nc.vector.tensor_scalar(onehot[:], rows[0:R9, 2], g.pid[0:R9, :], None, ALU.is_equal)
                    for j in range(NPAIR):
                        last = nc.vector.scalar_tensor_tensor(masked[:, j], rows[:, 2], g.type_of_row[:, j:j + 1], far_t[:],
                                                              ALU.is_equal, ALU.mult)
                    last.then_inc(s.masked.sem, 1)
            turns(dve, ET, tile)

        @block.scalar
        def _(act):
            def tile(i):
                for d in range(2):
                    act.wait_ge(s.product.sem, s.product.at(2 * i + d + 1))
                    nc.scalar.activation(msg[:], msg_ps[:], ACT.Copy).then_inc(s.msg.sem, 1)
                    act.wait_ge(s.joined.sem, s.joined.at(2 * i + d + 1))
                    nc.scalar.activation(total[:, d], total_ps[:], ACT.Copy).then_inc(s.summed.sem, 1)
            turns(act, ET, tile)
    for d in range(2):
        s.scattered[d].close(16 * ET)
        s.gathered[d].close(16 * ET)
    s.loaded.close(64 * ET)
    for sig in (s.summed, s.turned, s.masked, s.product, s.msg, s.joined):
        sig.close(2 * ET)


def general_sum_edges(nc, env, name, table, out, width, mlp=False, count=False):
    g = env
    with ExitStack() as ctx:
        sb = lambda n, s, d=F32: ctx.enter_context(nc.sbuf_tensor(f"{name}_{n}", s, d))
        pb = lambda n, s: ctx.enter_context(nc.psum_tensor(f"{name}_{n}", s, F32))
        edge_i, lead, rows, cols = sb("edge_i", [P, 3], I32), sb("lead", [P, 2], I32), sb("rows", [P, 3, P]), sb("cols", [P, 4])
        far, same, total = sb("far", [P, D]), sb("same", [P, P]), sb("total", [P, width])
        total_ps = pb("total_ps", [P, width])
        if mlp:
            feat, far_sb, hid, msg = sb("feat", [FE, P]), sb("far_sb", [D, P]), sb("hid", [P, P]), sb("msg", [P, D])
            far_t, hid_ps, msg_ps = pb("far_t", [D, P]), pb("hid_ps", [P, P]), pb("msg_ps", [P, D])
        s = g.gs
        loads = 5 if mlp else 4
        block = ctx.enter_context(nc.Block())

        @block.sync
        def _(sp):
            def tile(i):
                if not isinstance(i, int):
                    sp.wait_ge(s.scattered[0].sem, s.scattered[0].at(16 * i)).then_inc(g.sp_gate, 1)
                e = bass.ts(i, P)
                sp.dma_start(edge_i[:], g.edge_i[e, :]).then_inc(s.loaded.sem, 16)
                sp.dma_start(lead[:], g.lead[e, :]).then_inc(s.loaded.sem, 16)
                sp.dma_start(rows[:], g.edge_rows[:, e].partition_broadcast(P)).then_inc(s.loaded.sem, 16)
                sp.dma_start(cols[:], g.edge_cols[e, :]).then_inc(s.loaded.sem, 16)
                if mlp:
                    sp.dma_start(feat[:], g.feat_t[:, e]).then_inc(s.loaded.sem, 16)
            turns(sp, ET, tile)
            sp.wait_ge(s.scattered[0].sem, s.scattered[0].at(16 * ET))

        @block.gpsimd
        def _(pool):
            def tile(i):
                pool.wait_ge(s.loaded.sem, s.loaded.at(16 * loads * (i + 1))).then_inc(s.gate.sem, 1)
                if not count:
                    pool.indirect_dma_start(out=far[:], out_offset=None, in_=table[:], in_offset=bass.IndirectOffsetOnAxis(
                        ap=edge_i[:, 0:1], axis=0)).then_inc(s.gathered[0].sem, 16)
                pool.wait_ge(s.summed.sem, s.summed.at(i + 1)).then_inc(s.gate.sem, 1)
                pool.indirect_dma_start(out=out[:], out_offset=bass.IndirectOffsetOnAxis(ap=lead[:, 0:1], axis=0),
                                        in_=total[:], in_offset=None, compute_op=ALU.add).then_inc(s.scattered[0].sem, 16)
            turns(pool, ET, tile)

        @block.tensor
        def _(pe):
            def tile(i):
                if not count:
                    pe.wait_ge(s.gathered[0].sem, s.gathered[0].at(16 * i + 16))
                if mlp:
                    nc.tensor.matmul(far_t[:], far[:], g.ident[:], start=True, stop=True).then_inc(s.turned.sem, 1)
                    pe.wait_ge(s.msg.sem, s.msg.at(3 * i + 1))
                    nc.tensor.matmul(hid_ps[:], g.w31x[:], far_sb[:], start=True, stop=False)
                    nc.tensor.matmul(hid_ps[:], g.w31e[:], feat[:], start=False, stop=True).then_inc(s.turned.sem, 1)
                    pe.wait_ge(s.msg.sem, s.msg.at(3 * i + 2))
                    nc.tensor.matmul(msg_ps[:], hid[:], g.w32[:], start=True, stop=True).then_inc(s.turned.sem, 1)
                    pe.wait_ge(s.msg.sem, s.msg.at(3 * i + 3))
                pe.wait_ge(s.masked.sem, s.masked.at(i + 1))
                rhs = g.ones[:, 0:1] if count else msg[:] if mlp else far[:]
                nc.tensor.matmul(total_ps[:], same[:], rhs, start=True, stop=True).then_inc(s.joined.sem, 1)
            turns(pe, ET, tile)

        @block.vector
        def _(dve):
            def tile(i):
                dve.wait_ge(s.loaded.sem, s.loaded.at(16 * loads * (i + 1)))
                nc.vector.tensor_scalar(same[:], rows[:, 1], cols[:, 1:2], None, ALU.is_equal).then_inc(s.masked.sem, 1)
                if mlp:
                    dve.wait_ge(s.turned.sem, s.turned.at(3 * i + 3))
                    nc.vector.tensor_tensor(msg[:], msg_ps[:], g.b32[:], ALU.add).then_inc(s.msg.sem, 1)
            turns(dve, ET, tile)

        @block.scalar
        def _(act):
            def tile(i):
                if mlp:
                    act.wait_ge(s.loaded.sem, s.loaded.at(16 * loads * (i + 1)))
                    act.wait_ge(s.turned.sem, s.turned.at(3 * i + 1))
                    nc.scalar.activation(far_sb[:], far_t[:], ACT.Copy).then_inc(s.msg.sem, 1)
                    act.wait_ge(s.turned.sem, s.turned.at(3 * i + 2))
                    nc.scalar.activation(hid[:], hid_ps[:], ACT.Relu, bias=g.b31[:, 0:1]).then_inc(s.msg.sem, 1)
                act.wait_ge(s.joined.sem, s.joined.at(i + 1))
                nc.scalar.activation(total[:], total_ps[:], ACT.Copy).then_inc(s.summed.sem, 1)
            turns(act, ET, tile)
    s.scattered[0].close(16 * ET)
    if not count:
        s.gathered[0].close(16 * ET)
    s.loaded.close(16 * loads * ET)
    for sig in (s.summed, s.masked, s.joined):
        sig.close(ET)
    if mlp:
        s.turned.close(3 * ET)
        s.msg.close(3 * ET)


def general_scores(nc, env):
    g = env
    with ExitStack() as ctx:
        sb = lambda n, s, d=F32: ctx.enter_context(nc.sbuf_tensor(f"gs_{n}", s, d))
        pb = lambda n, s: ctx.enter_context(nc.psum_tensor(f"gs_{n}", s, F32))
        edge_i, lead, rows, cols = sb("edge_i", [P, 3], I32), sb("lead", [P, 2], I32), sb("rows", [P, 3, P]), sb("cols", [P, 4])
        kv, q, prod, score = sb("kv", [P, 2 * D]), sb("q", [P, D]), sb("prod", [P, D]), sb("score", [P, HEADS])
        diag, away, junk = sb("diag", [P, HEADS, P]), sb("away", [P, P]), sb("junk", [P, P])
        best, so_far, high = sb("best", [P, HEADS]), sb("so_far", [P, HEADS]), sb("high", [P, HEADS])
        spread = pb("spread", [P, HEADS, P])
        s = g.gs
        chain = Chain(s.chain)
        block = ctx.enter_context(nc.Block())

        @block.sync
        def _(sp):
            def tile(i):
                if not isinstance(i, int):
                    sp.wait_ge(s.scattered[0].sem, s.scattered[0].at(16 * i)).then_inc(g.sp_gate, 1)
                e = bass.ts(i, P)
                sp.dma_start(edge_i[:], g.edge_i[e, :]).then_inc(s.loaded.sem, 16)
                sp.dma_start(lead[:], g.lead[e, :]).then_inc(s.loaded.sem, 16)
                sp.dma_start(rows[:], g.edge_rows[:, e].partition_broadcast(P)).then_inc(s.loaded.sem, 16)
                sp.dma_start(cols[:], g.edge_cols[e, :]).then_inc(s.loaded.sem, 16)
            turns(sp, ET, tile)
            sp.wait_ge(s.scattered[0].sem, s.scattered[0].at(16 * ET))

        @block.gpsimd
        def _(pool):
            def tile(i):
                if not isinstance(i, int):
                    pool.wait_ge(s.scattered[0].sem, s.scattered[0].at(16 * i)).then_inc(s.gate.sem, 1)
                pool.wait_ge(s.loaded.sem, s.loaded.at(64 * i + 64)).then_inc(s.gate.sem, 1)
                pool.indirect_dma_start(out=kv[:], out_offset=None, in_=g.KV2, in_offset=bass.IndirectOffsetOnAxis(
                    ap=edge_i[:, 2:3], axis=0)).then_inc(s.gathered[0].sem, 16)
                pool.indirect_dma_start(out=q[:], out_offset=None, in_=g.Q[:], in_offset=bass.IndirectOffsetOnAxis(
                    ap=edge_i[:, 1:2], axis=0)).then_inc(s.gathered[1].sem, 16)
                pool.indirect_dma_start(out=so_far[:], out_offset=None, in_=g.high[:], in_offset=bass.IndirectOffsetOnAxis(
                    ap=edge_i[:, 1:2], axis=0)).then_inc(s.gathered[2].sem, 16)
                pool.wait_ge(s.summed.sem, s.summed.at(i + 1)).then_inc(s.gate.sem, 1)
                pool.indirect_dma_start(out=g.high[:], out_offset=bass.IndirectOffsetOnAxis(ap=lead[:, 0:1], axis=0),
                                        in_=high[:], in_offset=None).then_inc(s.scattered[0].sem, 16)
            turns(pool, ET, tile)

        @block.tensor
        def _(pe):
            def tile(i):
                pe.wait_ge(s.masked.sem, s.masked.at(i + 1))
                nc.tensor.matmul(spread[:], g.ones[:], diag[:], start=True, stop=True).then_inc(s.turned.sem, 1)
            turns(pe, ET, tile)

        @block.vector
        def _(dve):
            def tile(i):
                chain.turn(i)
                dve.wait_ge(s.loaded.sem, s.loaded.at(64 * i + 64))
                dve.wait_ge(s.gathered[0].sem, s.gathered[0].at(16 * i + 16))
                dve.wait_ge(s.gathered[1].sem, s.gathered[1].at(16 * i + 16))
                chain.link(dve, nc.vector.tensor_tensor(prod[:], kv[:, 0:D], q[:], ALU.mult))
                chain.link(dve, nc.vector.tensor_reduce(score[:], prod[:].rearrange("p (h d) -> p h d", h=HEADS), AX, ALU.add))
                for h in range(HEADS):
                    last = nc.vector.tensor_scalar(diag[:, h], g.ident[:], score[:, h:h + 1], None, ALU.mult)
                last.then_inc(s.masked.sem, 1)
                chain.link(dve, nc.vector.tensor_scalar(away[:], rows[:, 1], cols[:, 1:2], LOWEST, ALU.not_equal, ALU.mult))
                dve.wait_ge(s.turned.sem, s.turned.at(i + 1))
                for h in range(HEADS):
                    chain.link(dve, nc.vector.tensor_tensor(junk[:], spread[:, h], away[:], ALU.add))
                    chain.link(dve, nc.vector.tensor_reduce(best[:, h:h + 1], junk[:], AX, ALU.max))
                dve.wait_ge(s.gathered[2].sem, s.gathered[2].at(16 * i + 16))
                nc.vector.tensor_tensor(high[:], best[:], so_far[:], ALU.max).then_inc(s.summed.sem, 1)
            turns(dve, ET, tile)
    chain.close(ET)
    s.scattered[0].close(16 * ET)
    for d in range(3):
        s.gathered[d].close(16 * ET)
    s.loaded.close(64 * ET)
    for sig in (s.summed, s.masked, s.turned):
        sig.close(ET)


def general_attend(nc, env):
    g = env
    with ExitStack() as ctx:
        sb = lambda n, s, d=F32: ctx.enter_context(nc.sbuf_tensor(f"gv_{n}", s, d))
        pb = lambda n, s: ctx.enter_context(nc.psum_tensor(f"gv_{n}", s, F32))
        edge_i, lead, rows, cols = sb("edge_i", [P, 3], I32), sb("lead", [P, 2], I32), sb("rows", [P, 3, P]), sb("cols", [P, 4])
        kv, q, prod, score = sb("kv", [P, 2 * D]), sb("q", [P, D]), sb("prod", [P, D]), sb("score", [P, HEADS])
        high, less, msg, same, total = sb("high", [P, HEADS]), sb("less", [P, HEADS]), sb("msg", [P, D + HEADS]), sb("same", [P, P]), sb("total", [P, D + HEADS])
        total_ps = pb("total_ps", [P, D + HEADS])
        s = g.gs
        chain = Chain(s.chain)
        block = ctx.enter_context(nc.Block())

        @block.sync
        def _(sp):
            def tile(i):
                if not isinstance(i, int):
                    sp.wait_ge(s.scattered[0].sem, s.scattered[0].at(16 * i)).then_inc(g.sp_gate, 1)
                e = bass.ts(i, P)
                sp.dma_start(edge_i[:], g.edge_i[e, :]).then_inc(s.loaded.sem, 16)
                sp.dma_start(lead[:], g.lead[e, :]).then_inc(s.loaded.sem, 16)
                sp.dma_start(rows[:], g.edge_rows[:, e].partition_broadcast(P)).then_inc(s.loaded.sem, 16)
                sp.dma_start(cols[:], g.edge_cols[e, :]).then_inc(s.loaded.sem, 16)
            turns(sp, ET, tile)
            sp.wait_ge(s.scattered[0].sem, s.scattered[0].at(16 * ET))

        @block.gpsimd
        def _(pool):
            def tile(i):
                pool.wait_ge(s.loaded.sem, s.loaded.at(64 * i + 64)).then_inc(s.gate.sem, 1)
                pool.indirect_dma_start(out=kv[:], out_offset=None, in_=g.KV2, in_offset=bass.IndirectOffsetOnAxis(
                    ap=edge_i[:, 2:3], axis=0)).then_inc(s.gathered[0].sem, 16)
                pool.indirect_dma_start(out=q[:], out_offset=None, in_=g.Q[:], in_offset=bass.IndirectOffsetOnAxis(
                    ap=edge_i[:, 1:2], axis=0)).then_inc(s.gathered[1].sem, 16)
                pool.indirect_dma_start(out=high[:], out_offset=None, in_=g.high[:], in_offset=bass.IndirectOffsetOnAxis(
                    ap=edge_i[:, 1:2], axis=0)).then_inc(s.gathered[2].sem, 16)
                pool.wait_ge(s.summed.sem, s.summed.at(i + 1)).then_inc(s.gate.sem, 1)
                pool.indirect_dma_start(out=g.acc68[:], out_offset=bass.IndirectOffsetOnAxis(ap=lead[:, 0:1], axis=0),
                                        in_=total[:], in_offset=None, compute_op=ALU.add).then_inc(s.scattered[0].sem, 16)
            turns(pool, ET, tile)

        @block.tensor
        def _(pe):
            def tile(i):
                pe.wait_ge(s.masked.sem, s.masked.at(i + 1))
                nc.tensor.matmul(total_ps[:], same[:], msg[:], start=True, stop=True).then_inc(s.joined.sem, 1)
            turns(pe, ET, tile)

        @block.vector
        def _(dve):
            def tile(i):
                chain.turn(i)
                dve.wait_ge(s.loaded.sem, s.loaded.at(64 * i + 64))
                nc.vector.tensor_scalar(same[:], rows[:, 1], cols[:, 1:2], None, ALU.is_equal)
                for d in range(3):
                    dve.wait_ge(s.gathered[d].sem, s.gathered[d].at(16 * i + 16))
                chain.link(dve, nc.vector.tensor_tensor(prod[:], kv[:, 0:D], q[:], ALU.mult))
                chain.link(dve, nc.vector.tensor_reduce(score[:], prod[:].rearrange("p (h d) -> p h d", h=HEADS), AX, ALU.add))
                nc.vector.tensor_tensor(less[:], score[:], high[:], ALU.subtract).then_inc(s.turned.sem, 1)
                dve.wait_ge(s.msg.sem, s.msg.at(i + 1))
                nc.vector.tensor_tensor(msg[:, 0:D].rearrange("p (h d) -> p h d", h=HEADS), kv[:, D:2 * D].rearrange("p (h d) -> p h d", h=HEADS),
                                        msg[:, D:D + HEADS].unsqueeze(2).to_broadcast([P, HEADS, HD]), ALU.mult).then_inc(s.masked.sem, 1)
            turns(dve, ET, tile)

        @block.scalar
        def _(act):
            def tile(i):
                act.wait_ge(s.turned.sem, s.turned.at(i + 1))
                nc.scalar.activation(msg[:, D:D + HEADS], less[:], ACT.Exp).then_inc(s.msg.sem, 1)
                act.wait_ge(s.joined.sem, s.joined.at(i + 1))
                nc.scalar.activation(total[:], total_ps[:], ACT.Copy).then_inc(s.summed.sem, 1)
            turns(act, ET, tile)
    chain.close(ET)
    s.scattered[0].close(16 * ET)
    for d in range(3):
        s.gathered[d].close(16 * ET)
    s.loaded.close(64 * ET)
    for sig in (s.summed, s.masked, s.joined, s.turned, s.msg):
        sig.close(ET)
def fast_tables(nc, g):
    s = g.fs
    with ExitStack() as ctx:
        sb = lambda n, sh, d=F32: ctx.enter_context(nc.sbuf_tensor(f"ft_{n}", sh, d))
        src = [sb(f"src{h}", [P, WIN]) for h in range(2)]
        typ = [sb(f"typ{h}", [P, WIN]) for h in range(2)]
        mask = [sb(f"mask{h}", [P, KC, NPAIR, P], U8) for h in range(2)]
        onehot = [sb(f"onehot{h}", [R9, WIN]) for h in range(2)]
        lead_i = [sb(f"lead_i{h}", [P, KC], I32) for h in range(2)]
        same, junk = sb("same", [P, P]), sb("junk", [P, P])
        prev, ok, mine, away = (sb(n, [P, KC]) for n in ("prev", "ok", "mine", "away"))
        chain = Chain(s.chain)
        block = ctx.enter_context(nc.Block())

        @block.sync
        def _(sp):
            def pair(i):
                for h in range(2):
                    j = 2 * i + h
                    if not isinstance(i, int):
                        sp.wait_ge(s.ready.sem, s.ready.at(j - 1)).then_inc(g.sp_gate, 1)
                    e = bass.ts(j, KC)
                    sp.dma_start(src[h][:], g.win_src[e, :].rearrange("k e -> (k e)").partition_broadcast(P)).then_inc(s.loaded[h].sem, 16)
                    sp.dma_start(typ[h][:], g.win_type[e, :].rearrange("k e -> (k e)").partition_broadcast(P)).then_inc(s.loaded[h].sem, 16)
            turns(sp, NJ // 2, pair)
            for h in range(2):
                sp.wait_ge(s.stored[h].sem, s.stored[h].at(48 * (NJ // 2)))

        @block.vector
        def _(v):
            def pair(i):
                chain.turn(i)
                for h in range(2):
                    j = 2 * i + h
                    v.wait_ge(s.loaded[h].sem, s.loaded[h].at(32 * (i + 1)))
                    if not isinstance(i, int):
                        v.wait_ge(s.stored[h].sem, s.stored[h].at(48 * i))
                    nc.vector.tensor_scalar(onehot[h][:], typ[h][0:R9, :], g.pid[0:R9, :], None, ALU.is_equal)
                    for k in range(KC):
                        e = slice(k * P, k * P + P)
                        nc.vector.tensor_tensor(mask[h][:, k], typ[h][:, e].unsqueeze(1).to_broadcast([P, NPAIR, P]),
                                                g.type_of_row[:].unsqueeze(2).to_broadcast([P, NPAIR, P]), ALU.is_equal)
                        chain.link(v, nc.vector.tensor_scalar(same[:], src[h][:, e], g.src_m[:, bass.ds(KC * j + k, 1)], None, ALU.is_equal))
                        chain.link(v, nc.vector.tensor_tensor_reduce(junk[:], same[:], g.before[:], 1.0, 0.0, ALU.mult, ALU.add,
                                                                     prev[:, k:k + 1]))
                    cols = bass.ts(j, KC)
                    chain.link(v, nc.vector.tensor_scalar(ok[:], prev[:], 0.0, None, ALU.is_equal))
                    chain.link(v, nc.vector.tensor_scalar(mine[:], g.src_m[:, cols], 0.0, None, ALU.is_ge))
                    chain.link(v, nc.vector.tensor_tensor(ok[:], ok[:], mine[:], ALU.mult))
                    chain.link(v, nc.vector.scalar_tensor_tensor(away[:], g.src_m[:, cols], g.dump_row[:, 0:1], ok[:], ALU.subtract, ALU.mult))
                    nc.vector.tensor_scalar(lead_i[h][:], away[:], g.dump_row[:, 0:1], None, ALU.add).then_inc(s.ready.sem, 1)
                    v.wait_ge(s.ready.sem, s.ready.at(j + 1))
            turns(v, NJ // 2, pair)

        @block.scalar
        def _(act):
            def pair(i):
                for h in range(2):
                    j = 2 * i + h
                    act.wait_ge(s.ready.sem, s.ready.at(j + 1))
                    act.dma_start(g.win_mask[bass.ts(j, P), :], mask[h][:].rearrange("p k a e -> p (k a e)")).then_inc(s.stored[h].sem, 16)
                    act.dma_start(g.win_onehot[bass.ts(j, R9), :], onehot[h][:]).then_inc(s.stored[h].sem, 16)
                    act.dma_start(g.win_lead[bass.ts(j, P), :], lead_i[h][:]).then_inc(s.stored[h].sem, 16)
            turns(act, NJ // 2, pair)
    chain.close(NJ // 2)
    s.ready.close(NJ)
    for h in range(2):
        s.loaded[h].close(32 * (NJ // 2))
        s.stored[h].close(48 * (NJ // 2))


def band(k):
    return [(q, q - (k - 1)) for q in range(k - 1, k + 2) if 0 <= q < G7]


def fast_transform_edges(nc, g, layer):
    s = g.fs
    LAG = 6
    with ExitStack() as ctx:
        sb = lambda n, sh, d=F32: ctx.enter_context(nc.sbuf_tensor(f"fe{layer}_{n}", sh, d))
        pb = lambda n, sh: ctx.enter_context(nc.psum_tensor(f"fe{layer}_{n}", sh, F32))
        two = lambda n, sh, d=F32: [sb(f"{n}{h}", sh, d) for h in range(2)]
        idx, lead = two("idx", [P, 3, KC], I32), two("lead", [P, KC], I32)
        mask, onehot, src = two("mask", [P, KC, NPAIR, P], U8), two("onehot", [R9, WIN]), two("src", [P, WIN])
        far, near = sb("far", [P, 2, KC, 2 * D]), sb("near", [P, 2, KC, 2 * D])
        band_m = sb("band_m", [P, KC, BAND, P])
        masked_f, masked_r = two("masked_f", [P, NPAIR, P]), two("masked_r", [P, NPAIR, P])
        columns, msg = sb("columns", [P, P]), sb("msg", [P, KC, 2 * D + 1])
        same, total = [sb(f"same{a}", [P, P]) for a in range(4)], sb("total", [P, KC, D])
        agg = two("agg", [P, G7, D])
        far_t, near_t = pb("far_t", [P, P]), pb("near_t", [P, P])
        both_ps, back_ps, tot_ps = pb("both_ps", [P, P]), pb("back_ps", [P, P]), pb("tot_ps", [P, D])
        agg_ps = [pb(f"agg_ps{h}", [P, G7, D + 1]) for h in range(2)]
        block = ctx.enter_context(nc.Block())
        NL = 4

        @block.sync
        def _(sp):
            def pair(i):
                for h in range(2):
                    j = 2 * i + h
                    rows = bass.ts(j, P)
                    if not isinstance(i, int):
                        sp.wait_ge(s.picked.sem, s.picked.at(KC * (j - 1))).then_inc(g.sp_gate, 1)
                    sp.dma_start(idx[h][:].rearrange("p a k -> p (a k)"), g.win_idx[rows, :]).then_inc(s.indices[h].sem, 16)
                    if not isinstance(i, int):
                        sp.wait_ge(s.joined.sem, s.joined.at(KC * (j - 1))).then_inc(g.sp_gate, 1)
                    for dst, source in ((mask[h][:].rearrange("p k a e -> p (k a e)"), g.win_mask[rows, :]),
                                        (onehot[h][:], g.win_onehot[bass.ts(j, R9), :]),
                                        (src[h][:], g.win_src[bass.ts(j, KC), :].rearrange("k e -> (k e)").partition_broadcast(P))):
                        sp.dma_start(dst, source).then_inc(s.loaded[h].sem, 16)
                    if not isinstance(i, int):
                        for k in range(KC):
                            sp.wait_ge(s.scattered[k].sem, s.scattered[k].at(16 * (j - 1))).then_inc(g.sp_gate, 1)
                    sp.dma_start(lead[h][:], g.win_lead[rows, :]).then_inc(s.loaded[h].sem, 16)
                    if layer < 2:
                        for k in range(2):
                            sp.dma_start(node_view(g.back[layer + 1][k], j), g.zeros[:, 0:G7 * D].rearrange("p (q d) -> p q d", q=G7))\
                                .then_inc(s.zeroed.sem, 16)
            turns(sp, NJ // 2, pair)
            if layer < 2:
                sp.wait_ge(s.zeroed.sem, s.zeroed.at(2 * 16 * NJ))
            for k in range(KC):
                sp.wait_ge(s.scattered[k].sem, s.scattered[k].at(16 * NJ))
            for h in range(2):
                sp.wait_ge(s.stored[h].sem, s.stored[h].at(16 * (NJ // 2)))

        @block.gpsimd
        def _(pool):
            def scatter(c, j, k, h, first):
                pool.wait_ge(s.summed.sem, s.summed.at(c + 1)).then_inc(s.gate.sem, 1)
                if not first:
                    jj, kk = (j, k - 2) if k >= 2 else (j - 1, k + KC - 2)
                    pool.wait_ge(s.scattered[kk].sem, s.scattered[kk].at(16 * (jj + 1))).then_inc(s.gate.sem, 1)
                pool.indirect_dma_start(out=g.back[layer][k % 2][:], out_offset=bass.IndirectOffsetOnAxis(ap=lead[h][:, k:k + 1], axis=0),
                                        in_=total[:, k], in_offset=None, compute_op=ALU.add).then_inc(s.scattered[k].sem, 16)

            def pair(i):
                for h in range(2):
                    j = 2 * i + h
                    pool.wait_ge(s.indices[h].sem, s.indices[h].at(16 * (i + 1))).then_inc(s.gate.sem, 1)
                    for k in range(KC):
                        c = KC * j + k
                        if k == LAG:
                            pool.wait_ge(s.loaded[h].sem, s.loaded[h].at(16 * NL * (i + 1))).then_inc(s.gate.sem, 1)
                        if not isinstance(i, int):
                            pool.wait_ge(s.picked.sem, s.picked.at(c + 1 - 2 * KC)).then_inc(s.gate.sem, 1)
                        for rows, a, done in ((far, 0, s.gathered[k]), (near, 2, s.gathered_near[k])):
                            if not isinstance(j, int) or j:
                                pool.wait_ge(done.sem, done.at(16 * j)).then_inc(s.gate.sem, 1)
                            pool.indirect_dma_start(out=rows[:, h, k], out_offset=None, in_=g.T2[:], in_offset=bass.IndirectOffsetOnAxis(
                                ap=idx[h][:, a, k:k + 1], axis=0)).then_inc(done.sem, 16)
                        if k >= LAG:
                            scatter(c - LAG, j, k - LAG, h, isinstance(j, int) and j == 0 and k - LAG < 2)
                        elif not isinstance(j, int) or j:
                            scatter(c - LAG, j - 1, k + KC - LAG, 1 - h, False)
            turns(pool, NJ // 2, pair)
            for k in range(KC - LAG, KC):
                scatter(KC * (NJ - 1) + k, NJ - 1, k, 1, False)

        @block.tensor
        def _(pe):
            def multiply(c, j, k, h, i):
                if k == 0:
                    pe.wait_ge(s.loaded[h].sem, s.loaded[h].at(16 * NL * (i + 1)))
                if not (isinstance(c, int) and c == 0):
                    pe.wait_ge(s.columns.sem, s.columns.at(c))
                for masked, d, sig, out_sig in ((masked_f, 0, s.masked_f, s.product_f), (masked_r, 1, s.masked_r, s.product_r)):
                    pe.wait_ge(sig.sem, sig.at(c + 1))
                    ps = both_ps[D * (1 - d):D * (1 - d) + D, :]
                    for a in range(NPAIR):
                        nc.tensor.matmul(ps, g.w0[:, layer, d, a], masked[k % 2][:, a], start=(a == 0), stop=False)
                    nc.tensor.matmul(ps, g.b0[:, layer, d], onehot[h][:, k * P:k * P + P], start=False, stop=True).then_inc(out_sig.sem, 1)

            def turn_back(c):
                pe.wait_ge(s.columns.sem, s.columns.at(c + 1))
                if not (isinstance(c, int) and c == 0):
                    pe.wait_ge(s.msg_f.sem, s.msg_f.at(c))
                nc.tensor.transpose(back_ps[:], columns[:], g.ident[:]).then_inc(s.returned.sem, 1)

            def collect(c, j, k, h):
                pe.wait_ge(s.msg_f.sem, s.msg_f.at(c + 1))
                pe.wait_ge(s.same.sem, s.same.at(c + 1))
                if not (isinstance(c, int) and c == 0):
                    pe.wait_ge(s.summed.sem, s.summed.at(c))
                nc.tensor.matmul(tot_ps[:], same[k % 4][:], msg[:, k, 0:D], start=True, stop=True).then_inc(s.joined.sem, 1)
                if k == 0:
                    return
                q = k - 1
                pe.wait_ge(s.band.sem, s.band.at(c + 1))
                if q == 0 and not (isinstance(j, int) and j < 2):
                    pe.wait_ge(s.agg.sem, s.agg.at(j - 1))
                chunks = [kk for kk in range(k - 2, k + 1) if kk >= 0]
                for kk in chunks:
                    mm = nc.tensor.matmul(agg_ps[h][:, q], band_m[:, kk, q - (kk - 1)], msg[:, kk, D:2 * D + 1], start=(kk == chunks[0]), stop=(kk == k))
                mm.then_inc(s.placed.sem, 1)

            def pair(i):
                for h in range(2):
                    j = 2 * i + h
                    for k in range(KC):
                        c = KC * j + k
                        start = isinstance(c, int) and c == 0
                        before = (c - 1, j, k - 1, h) if k else (c - 1, j - 1, KC - 1, 1 - h)
                        pe.wait_ge(s.gathered[k].sem, s.gathered[k].at(16 * (j + 1)))
                        if not start:
                            pe.wait_ge(s.masked_f.sem, s.masked_f.at(c))
                        nc.tensor.transpose(far_t[:], far[:, h, k], g.ident[:]).then_inc(s.turned.sem, 1)
                        pe.wait_ge(s.gathered_near[k].sem, s.gathered_near[k].at(16 * (j + 1)))
                        if not start:
                            pe.wait_ge(s.masked_r.sem, s.masked_r.at(c))
                        nc.tensor.transpose(near_t[:], near[:, h, k], g.ident[:]).then_inc(s.picked.sem, 1)
                        if not (isinstance(c, int) and c < 2):
                            turn_back(c - 2)
                        if not start:
                            multiply(*before, i)
                        if not (isinstance(c, int) and c < 2):
                            collect(*((c - 2, j, k - 2, h) if k >= 2 else (c - 2, j - 1, k + KC - 2, 1 - h)))
            turns(pe, NJ // 2, pair)
            last = (KC * NJ - 1, NJ - 1, KC - 1, 1)
            turn_back(KC * NJ - 2)
            multiply(*last, NJ // 2 - 1)
            collect(KC * NJ - 2, NJ - 1, KC - 2, 1)
            turn_back(KC * NJ - 1)
            collect(*last)

        @block.vector
        def _(v):
            def build(c, j, k):
                if not (isinstance(j, int) and j == 0):
                    v.wait_ge(s.placed.sem, s.placed.at(G7 * (j - 1) + min(k + 1, G7 - 1) + 1))
                nc.vector.tensor_scalar(band_m[:, k].rearrange("p b e -> p (b e)"), g.iota_row[:], g.place[:, bass.ds(c, 1)], None,
                                        ALU.is_equal).then_inc(s.band.sem, 1)

            def pair(i):
                for h in range(2):
                    j = 2 * i + h
                    for k in range(KC):
                        c = KC * j + k
                        early = isinstance(c, int) and c < 2
                        if k == 0:
                            build(c, j, k)
                            v.wait_ge(s.loaded[h].sem, s.loaded[h].at(16 * NL * (i + 1)))
                        if k + 1 < KC:
                            build(c + 1, j, k + 1)
                        if not (isinstance(c, int) and c < 4):
                            v.wait_ge(s.joined.sem, s.joined.at(c - 3))
                        nc.vector.tensor_scalar(same[k % 4][:], src[h][:, k * P:k * P + P], g.src_m[:, bass.ds(c, 1)], None,
                                                ALU.is_equal).then_inc(s.same.sem, 1)
                        v.wait_ge(s.turned.sem, s.turned.at(c + 1))
                        if not early:
                            v.wait_ge(s.product_f.sem, s.product_f.at(c - 1))
                        nc.vector.tensor_tensor(masked_f[k % 2][:], mask[h][:, k], far_t[:].unsqueeze(1).to_broadcast([P, NPAIR, P]),
                                                ALU.mult).then_inc(s.masked_f.sem, 1)
                        v.wait_ge(s.picked.sem, s.picked.at(c + 1))
                        if not early:
                            v.wait_ge(s.product_r.sem, s.product_r.at(c - 1))
                        nc.vector.tensor_tensor(masked_r[k % 2][:], mask[h][:, k], near_t[:].unsqueeze(1).to_broadcast([P, NPAIR, P]),
                                                ALU.mult).then_inc(s.masked_r.sem, 1)
            nc.vector.memset(msg[:, :, 2 * D:2 * D + 1], 1.0).then_inc(s.ones.sem, 1)
            turns(v, NJ // 2, pair)

        @block.scalar
        def _(act):
            def take_columns(c):
                act.wait_ge(s.product_r.sem, s.product_r.at(c + 1))
                if not (isinstance(c, int) and c == 0):
                    act.wait_ge(s.returned.sem, s.returned.at(c))
                nc.scalar.activation(columns[:], both_ps[:], ACT.Copy).then_inc(s.columns.sem, 1)

            def messages(c, j, k, h):
                act.wait_ge(s.returned.sem, s.returned.at(c + 1))
                if not (isinstance(j, int) and j == 0):
                    act.wait_ge(s.placed.sem, s.placed.at(G7 * (j - 1) + min(k + 1, G7 - 1) + 1))
                nc.scalar.activation(msg[:, k, 0:2 * D], back_ps[:], ACT.Copy).then_inc(s.msg_f.sem, 1)

            def totals(c, j, k, h, i):
                act.wait_ge(s.joined.sem, s.joined.at(c + 1))
                if not (isinstance(j, int) and j == 0):
                    act.wait_ge(s.scattered[k].sem, s.scattered[k].at(16 * j))
                nc.scalar.activation(total[:, k], tot_ps[:], ACT.Copy).then_inc(s.summed.sem, 1)
                if k == KC - 1:
                    act.wait_ge(s.placed.sem, s.placed.at(G7 * (j + 1)))
                    if not (isinstance(j, int) and j < 2):
                        act.wait_ge(s.stored[h].sem, s.stored[h].at(16 * i))
                    nc.scalar.activation(agg[h][:], agg_ps[h][:, :, 0:D], ACT.Copy)
                    nc.scalar.activation(g.indegree[:, bass.ts(j, G7)], agg_ps[h][:, :, D], ACT.Copy).then_inc(s.agg.sem, 1)
                    act.wait_ge(s.agg.sem, s.agg.at(j + 1))
                    act.dma_start(node_view(g.acc, j), agg[h][:]).then_inc(s.stored[h].sem, 16)

            def pair(i):
                for h in range(2):
                    j = 2 * i + h
                    for k in range(KC):
                        c = KC * j + k
                        two_before = (c - 2, j, k - 2, h) if k >= 2 else (c - 2, j - 1, k + KC - 2, 1 - h)
                        if not (isinstance(c, int) and c < 2):
                            messages(*two_before)
                        if not (isinstance(c, int) and c == 0):
                            take_columns(c - 1)
                        if not (isinstance(c, int) and c < 2):
                            totals(*((c - 2, j, k - 2, h, i) if k >= 2 else (c - 2, j - 1, k + KC - 2, 1 - h, i if h else i - 1)))
            act.wait_ge(s.ones.sem, s.ones.at(1))
            turns(act, NJ // 2, pair)
            messages(KC * NJ - 2, NJ - 1, KC - 2, 1)
            take_columns(KC * NJ - 1)
            totals(KC * NJ - 2, NJ - 1, KC - 2, 1, NJ // 2 - 1)
            messages(KC * NJ - 1, NJ - 1, KC - 1, 1)
            totals(KC * NJ - 1, NJ - 1, KC - 1, 1, NJ // 2 - 1)
    for k in range(KC):
        s.gathered[k].close(16 * NJ)
        s.gathered_near[k].close(16 * NJ)
        s.scattered[k].close(16 * NJ)
    for h in range(2):
        s.indices[h].close(16 * (NJ // 2))
        s.loaded[h].close(16 * NL * (NJ // 2))
        s.stored[h].close(16 * (NJ // 2))
    for sig in (s.turned, s.band, s.picked, s.masked_f, s.masked_r, s.product_f, s.product_r, s.msg_f,
                s.columns, s.returned, s.same, s.joined, s.summed):
        sig.close(KC * NJ)
    s.placed.close(G7 * NJ)
    s.agg.close(NJ)
    s.ones.close(1)
    if layer < 2:
        s.zeroed.close(2 * 16 * NJ)


def fast_sum_edges(nc, g, name, table, mlp=False):
    s = g.fs
    HK = KC // 2
    with ExitStack() as ctx:
        sb = lambda n, sh, d=F32: ctx.enter_context(nc.sbuf_tensor(f"{name}_{n}", sh, d))
        pb = lambda n, sh: ctx.enter_context(nc.psum_tensor(f"{name}_{n}", sh, F32))
        two = lambda n, sh, d=F32: [sb(f"{n}{h}", sh, d) for h in range(2)]
        idx = two("idx", [P, 3, KC], I32)
        far, band_m, agg = two("far", [P, KC, D]), two("band_m", [P, KC, BAND, P]), two("agg", [P, G7, D])
        agg_ps = [pb(f"agg_ps{h}", [P, G7, D]) for h in range(2)]
        if mlp:
            feat, msg = two("feat", [FE, WIN]), two("msg", [P, KC, D])
            far_sb, hid = two("far_sb", [D, HK * P]), two("hid", [P, HK * P])
            far_t = [pb(f"far_t{a}", [D, HK * P]) for a in range(2)]
            hid_ps = [pb(f"hid_ps{a}", [P, HK * P]) for a in range(2)]
            msg_ps = pb("msg_ps", [P, HK, D])
        NL = 2 if mlp else 1
        block = ctx.enter_context(nc.Block())

        @block.sync
        def _(sp):
            def pair(i):
                for h in range(2):
                    j = 2 * i + h
                    if not isinstance(i, int):
                        if mlp:
                            sp.wait_ge(s.product_f.sem, s.product_f.at(2 * (j - 1))).then_inc(g.sp_gate, 1)
                        else:
                            sp.wait_ge(s.placed.sem, s.placed.at(G7 * (j - 1))).then_inc(g.sp_gate, 1)
                    sp.dma_start(idx[h][:].rearrange("p a k -> p (a k)"), g.win_idx[bass.ts(j, P), :]).then_inc(s.loaded[h].sem, 16)
                    if mlp:
                        sp.dma_start(feat[h][:], g.win_feat[bass.ts(j, FE), :]).then_inc(s.loaded[h].sem, 16)
            turns(sp, NJ // 2, pair)
            for h in range(2):
                sp.wait_ge(s.stored[h].sem, s.stored[h].at(16 * (NJ // 2)))

        @block.gpsimd
        def _(pool):
            def pair(i):
                for h in range(2):
                    j = 2 * i + h
                    pool.wait_ge(s.loaded[h].sem, s.loaded[h].at(16 * NL * (i + 1))).then_inc(s.gate.sem, 1)
                    for k in range(KC):
                        if not (isinstance(j, int) and j == 0):
                            pool.wait_ge(s.gathered[k].sem, s.gathered[k].at(16 * j)).then_inc(s.gate.sem, 1)
                        pool.indirect_dma_start(out=far[h][:, k], out_offset=None, in_=table[:], in_offset=bass.IndirectOffsetOnAxis(
                            ap=idx[h][:, 0, k:k + 1], axis=0)).then_inc(s.gathered[k].sem, 16)
            turns(pool, NJ // 2, pair)

        @block.tensor
        def _(pe):
            def sums(j, h):
                rows = msg[h] if mlp else far[h]
                if mlp:
                    pe.wait_ge(s.msg_f.sem, s.msg_f.at(2 * j + 2))
                if not (isinstance(j, int) and j < 2):
                    pe.wait_ge(s.agg.sem, s.agg.at(j - 1))
                for q in range(G7):
                    chunks = [k for k in range(q - 1, q + 2) if k >= 0]
                    if not mlp:
                        for k in (chunks if q == 0 else chunks[-1:]):
                            pe.wait_ge(s.gathered[k].sem, s.gathered[k].at(16 * (j + 1)))
                    pe.wait_ge(s.band.sem, s.band.at(KC * j + chunks[-1] + 1))
                    for k in chunks:
                        mm = nc.tensor.matmul(agg_ps[h][:, q], band_m[h][:, k, q - (k - 1)], rows[:, k], start=(k == chunks[0]),
                                              stop=(k == chunks[-1]))
                    mm.then_inc(s.placed.sem, 1)

            def pair(i):
                for h in range(2):
                    j = 2 * i + h
                    early = isinstance(j, int) and j == 0
                    if mlp:
                        for a in range(2):
                            for k in range(HK * a, HK * a + HK):
                                pe.wait_ge(s.gathered[k].sem, s.gathered[k].at(16 * (j + 1)))
                                if k == HK * a and not early:
                                    pe.wait_ge(s.half.sem, s.half.at(2 * (j - 1) + a + 1))
                                mm = nc.tensor.matmul(far_t[a][:, (k % HK) * P:(k % HK) * P + P], far[h][:, k], g.ident[:], start=True, stop=True)
                            mm.then_inc(s.turned.sem, 1)
                        if not early:
                            sums(j - 1, 1 - h)
                        pe.wait_ge(s.loaded[h].sem, s.loaded[h].at(16 * NL * (i + 1)))
                        for a in range(2):
                            pe.wait_ge(s.half.sem, s.half.at(2 * j + a + 1))
                            if not early:
                                pe.wait_ge(s.hidden.sem, s.hidden.at(2 * (j - 1) + a + 1))
                            nc.tensor.matmul(hid_ps[a][:], g.w31x[:], far_sb[a][:], start=True, stop=False)
                            nc.tensor.matmul(hid_ps[a][:], g.w31e[:], feat[h][:, a * HK * P:(a + 1) * HK * P], start=False, stop=True)\
                                .then_inc(s.product_f.sem, 1)
                        for a in range(2):
                            pe.wait_ge(s.hidden.sem, s.hidden.at(2 * j + a + 1))
                            if not (early and a == 0):
                                pe.wait_ge(s.msg_f.sem, s.msg_f.at(2 * j + a))
                            for k in range(HK):
                                mm = nc.tensor.matmul(msg_ps[:, k], hid[a][:, k * P:k * P + P], g.w32[:], start=True, stop=True)
                            mm.then_inc(s.product_r.sem, 1)
                    else:
                        sums(j, h)
            turns(pe, NJ // 2, pair)
            if mlp:
                sums(NJ - 1, 1)

        @block.vector
        def _(v):
            def pair(i):
                for h in range(2):
                    j = 2 * i + h
                    if not isinstance(i, int):
                        v.wait_ge(s.placed.sem, s.placed.at(G7 * (j - 1)))
                    for k in range(KC):
                        nc.vector.tensor_scalar(band_m[h][:, k].rearrange("p b e -> p (b e)"), g.iota_row[:],
                                                g.place[:, bass.ds(KC * j + k, 1)], None, ALU.is_equal).then_inc(s.band.sem, 1)
                    if mlp:
                        for a in range(2):
                            v.wait_ge(s.product_r.sem, s.product_r.at(2 * j + a + 1))
                            nc.vector.tensor_tensor(msg[h][:, a * HK:(a + 1) * HK], msg_ps[:], g.b32[:].unsqueeze(1).to_broadcast([P, HK, D]),
                                                    ALU.add).then_inc(s.msg_f.sem, 1)
            turns(v, NJ // 2, pair)

        @block.scalar
        def _(act):
            def take_sums(j, h, i):
                act.wait_ge(s.placed.sem, s.placed.at(G7 * (j + 1)))
                if not (isinstance(j, int) and j < 2):
                    act.wait_ge(s.stored[h].sem, s.stored[h].at(16 * i))
                nc.scalar.activation(agg[h][:], agg_ps[h][:], ACT.Copy).then_inc(s.agg.sem, 1)
                act.wait_ge(s.agg.sem, s.agg.at(j + 1))
                act.dma_start(node_view(g.acc, j), agg[h][:]).then_inc(s.stored[h].sem, 16)

            def pair(i):
                for h in range(2):
                    j = 2 * i + h
                    early = isinstance(j, int) and j == 0
                    if mlp:
                        for a in range(2):
                            act.wait_ge(s.turned.sem, s.turned.at(2 * j + a + 1))
                            if not early:
                                act.wait_ge(s.product_f.sem, s.product_f.at(2 * (j - 1) + a + 1))
                            nc.scalar.activation(far_sb[a][:], far_t[a][:], ACT.Copy).then_inc(s.half.sem, 1)
                        if not early:
                            take_sums(j - 1, 1 - h, i if h else i - 1)
                        for a in range(2):
                            act.wait_ge(s.product_f.sem, s.product_f.at(2 * j + a + 1))
                            if not early:
                                act.wait_ge(s.product_r.sem, s.product_r.at(2 * (j - 1) + a + 1))
                            nc.scalar.activation(hid[a][:], hid_ps[a][:], ACT.Relu, bias=g.b31[:, 0:1]).then_inc(s.hidden.sem, 1)
                    else:
                        take_sums(j, h, i)
            turns(act, NJ // 2, pair)
            if mlp:
                take_sums(NJ - 1, 1, NJ // 2 - 1)
    for k in range(KC):
        s.gathered[k].close(16 * NJ)
    for h in range(2):
        s.loaded[h].close(16 * NL * (NJ // 2))
        s.stored[h].close(16 * (NJ // 2))
    s.placed.close(G7 * NJ)
    s.agg.close(NJ)
    s.band.close(KC * NJ)
    if mlp:
        for sig in (s.turned, s.half, s.product_f, s.product_r, s.hidden, s.msg_f):
            sig.close(2 * NJ)
def fast_scores(nc, g, score, value):
    s = g.fs
    with ExitStack() as ctx:
        sb = lambda n, sh, d=F32: ctx.enter_context(nc.sbuf_tensor(f"fq_{n}", sh, d))
        pb = lambda n, sh: ctx.enter_context(nc.psum_tensor(f"fq_{n}", sh, F32))
        two = lambda n, sh, d=F32: [sb(f"{n}{h}", sh, d) for h in range(2)]
        idx, kv, query = two("idx", [P, 3, KC], I32), two("kv", [P, KC, 2 * D]), two("query", [P, G7, D])
        band_m, band_t = two("band_m", [P, BAND, P]), two("band_t", [P, BAND, P])
        prod = sb("prod", [P, KC, D])
        bt_ps = [pb(f"bt_ps{a}", [P, BAND, P]) for a in range(2)]
        q_ps = [pb(f"q_ps{h}", [P, KC, D]) for h in range(2)]
        NL = 2
        block = ctx.enter_context(nc.Block())

        @block.sync
        def _(sp):
            def pair(i):
                for h in range(2):
                    j = 2 * i + h
                    if not isinstance(i, int):
                        sp.wait_ge(s.joined.sem, s.joined.at(j - 1)).then_inc(g.sp_gate, 1)
                        sp.wait_ge(s.summed.sem, s.summed.at(j - 1)).then_inc(g.sp_gate, 1)
                    sp.dma_start(idx[h][:].rearrange("p a k -> p (a k)"), g.win_idx[bass.ts(j, P), :]).then_inc(s.loaded[h].sem, 16)
                    sp.dma_start(query[h][:], node_view(g.Q, j)).then_inc(s.loaded[h].sem, 16)
            turns(sp, NJ // 2, pair)

        @block.gpsimd
        def _(pool):
            def pair(i):
                for h in range(2):
                    j = 2 * i + h
                    pool.wait_ge(s.loaded[h].sem, s.loaded[h].at(16 * NL * (i + 1))).then_inc(s.gate.sem, 1)
                    for k in range(KC):
                        if not (isinstance(j, int) and j == 0):
                            pool.wait_ge(s.gathered[k].sem, s.gathered[k].at(16 * j)).then_inc(s.gate.sem, 1)
                        pool.indirect_dma_start(out=kv[h][:, k], out_offset=None, in_=g.KV2, in_offset=bass.IndirectOffsetOnAxis(
                            ap=idx[h][:, 1, k:k + 1], axis=0)).then_inc(s.gathered[k].sem, 16)
            turns(pool, NJ // 2, pair)

        @block.tensor
        def _(pe):
            def pick(c, j, k, h):
                pe.wait_ge(s.band_t.sem, s.band_t.at(c + 1))
                tiles = band(k)
                for q, b in tiles:
                    mm = nc.tensor.matmul(q_ps[h][:, k], band_t[k % 2][:, b], query[h][:, q], start=(q == tiles[0][0]), stop=(q == tiles[-1][0]))
                mm.then_inc(s.picked.sem, 1)

            def pair(i):
                for h in range(2):
                    j = 2 * i + h
                    for k in range(KC):
                        c = KC * j + k
                        pe.wait_ge(s.band.sem, s.band.at(c + 1))
                        if not (isinstance(c, int) and c < 2):
                            pe.wait_ge(s.band_t.sem, s.band_t.at(c - 1))
                        for q, b in band(k):
                            mm = nc.tensor.transpose(bt_ps[k % 2][:, b], band_m[k % 2][:, b], g.ident[:])
                        mm.then_inc(s.band_turned.sem, 1)
                        if k == 1:
                            pe.wait_ge(s.loaded[h].sem, s.loaded[h].at(16 * NL * (i + 1)))
                            if not (isinstance(j, int) and j < 2):
                                pe.wait_ge(s.joined.sem, s.joined.at(j - 1))
                        if k:
                            pick(c - 1, j, k - 1, h)
                    pick(KC * j + KC - 1, j, KC - 1, h)
            turns(pe, NJ // 2, pair)

        @block.vector
        def _(v):
            def pair(i):
                for h in range(2):
                    j = 2 * i + h
                    for k in range(KC):
                        c = KC * j + k
                        if not (isinstance(c, int) and c < 2):
                            v.wait_ge(s.band_turned.sem, s.band_turned.at(c - 1))
                        nc.vector.tensor_scalar(band_m[k % 2][:].rearrange("p b e -> p (b e)"), g.iota_row[:], g.place[:, bass.ds(c, 1)],
                                                None, ALU.is_equal).then_inc(s.band.sem, 1)
                    for k in range(KC):
                        v.wait_ge(s.gathered[k].sem, s.gathered[k].at(16 * (j + 1)))
                    v.wait_ge(s.picked.sem, s.picked.at(KC * (j + 1)))
                    if not (isinstance(j, int) and j == 0):
                        v.wait_ge(s.ready.sem, s.ready.at(j))
                    nc.vector.tensor_tensor(prod[:], kv[h][:, :, 0:D], q_ps[h][:], ALU.mult).then_inc(s.joined.sem, 1)
                    v.wait_ge(s.joined.sem, s.joined.at(j + 1))
                    nc.vector.tensor_reduce(score[:, bass.ts(j, KC * HEADS)], prod[:].rearrange("p k (h d) -> p (k h) d", h=HEADS), AX,
                                            ALU.add).then_inc(s.ready.sem, 1)
            turns(v, NJ // 2, pair)

        @block.scalar
        def _(act):
            def pair(i):
                for h in range(2):
                    j = 2 * i + h
                    for k in range(KC):
                        c = KC * j + k
                        act.wait_ge(s.band_turned.sem, s.band_turned.at(c + 1))
                        if not (isinstance(c, int) and c < 2):
                            act.wait_ge(s.picked.sem, s.picked.at(c - 1))
                        b0, b1 = band(k)[0][1], band(k)[-1][1] + 1
                        nc.scalar.activation(band_t[k % 2][:, b0:b1], bt_ps[k % 2][:, b0:b1], ACT.Copy).then_inc(s.band_t.sem, 1)
                    for k in range(KC):
                        act.wait_ge(s.gathered[k].sem, s.gathered[k].at(16 * (j + 1)))
                    nc.scalar.activation(value[:, bass.ts(j, KC * D)].rearrange("p (k d) -> p k d", k=KC), kv[h][:, :, D:2 * D], ACT.Copy)\
                        .then_inc(s.summed.sem, 1)
            turns(act, NJ // 2, pair)
    for k in range(KC):
        s.gathered[k].close(16 * NJ)
    for h in range(2):
        s.loaded[h].close(16 * NL * (NJ // 2))
    for sig in (s.band, s.band_t, s.band_turned, s.picked):
        sig.close(KC * NJ)
    for sig in (s.joined, s.ready, s.summed):
        sig.close(NJ)


def fast_weights(nc, g, score):
    NG = NC * HEADS // P
    HJ = NJ // 2
    ROWS = HEADS * HJ
    with ExitStack() as ctx:
        sb = lambda n, sh, d=F32: ctx.enter_context(nc.sbuf_tensor(f"fw_{n}", sh, d))
        pb = lambda n, sh: ctx.enter_context(nc.psum_tensor(f"fw_{n}", sh, F32))
        sem = lambda n: ctx.enter_context(nc.semaphore(f"fw_{n}"))
        flip, rev, dst_rev = sb("flip", [P, P]), sb("rev", [P, NC * HEADS]), sb("dst_rev", [P, NC])
        turned = sb("turned", [P, NG, P])
        dturn = sb("dturn", [CR, 4, P])
        data, dst, new = sb("data", [ROWS, WIN]), sb("dst", [ROWS, WIN]), sb("new", [ROWS, WIN])
        best = sb("best", [ROWS, WIN])
        t_ps = [pb(f"t_ps{a}", [P, 4, P]) for a in range(2)]
        made, dve, pe_s, act_s, stored, read = sem("made"), sem("dve"), sem("pe"), sem("act"), sem("stored"), sem("read")
        block = ctx.enter_context(nc.Block())
        J4 = lambda t: t.rearrange("p (j k h) -> p j k h", k=KC, h=HEADS)
        groups = [(q, min(4, NG - q)) for q in range(0, NG, 4)]
        nb = len(groups)
        s_dram, m_dram = g.s_rows, g.m_rows

        @block.gpsimd
        def _(pool):
            pool.memset(flip[:], 0.0).then_inc(made, 1)
            pool.wait_ge(made, 1)
            pool.affine_select(out=flip[:], in_=flip[:], compare_op=ALU.not_equal, fill=1.0, base=-(P - 1), pattern=[[1, P]],
                               channel_multiplier=1).then_inc(made, 1)

        plan = []
        loads = 0
        for way in range(2):
            for half in range(2):
                loads += HEADS * 2
                plan.append((way, half, loads))
        READS = [loads + 1, loads + 2]

        @block.tensor
        def _(pe):
            n = 0

            def turn(source, rhs, count):
                nonlocal n
                for q, m in count:
                    if n >= 2:
                        pe.wait_ge(act_s, n - 1)
                    for a in range(m):
                        mm = nc.tensor.matmul(t_ps[n % 2][:, a], source(q + a), rhs, start=True, stop=True)
                    mm.then_inc(pe_s, 1)
                    n += 1
            pe.wait_ge(made, 2)
            pe.wait_ge(dve, 2)
            turn(lambda q: score[:, q * P:(q + 1) * P], g.ident[:], groups)
            turn(lambda q: rev[:, q * P:(q + 1) * P], flip[:], groups)
            if n >= 2:
                pe.wait_ge(act_s, n - 1)
            for a in range(4):
                mm = nc.tensor.matmul(t_ps[n % 2][0:CR, a], dst_rev[:, a * CR:(a + 1) * CR], flip[:], start=True, stop=True)
            mm.then_inc(pe_s, 1)
            n += 1
            for way in range(2):
                pe.wait_ge(read, 16 * READS[way])
                turn(lambda q: turned[:, q], g.ident[:], groups)
            for q, m in groups:
                pe.wait_ge(act_s, n - 1)
                nc.tensor.matmul(t_ps[n % 2][:, 0:m].rearrange("p a e -> p (a e)"), flip[:], g.high_r[:, q * P:(q + m) * P],
                                 start=True, stop=True).then_inc(pe_s, 1)
                n += 1

        @block.sync
        def _(sp):
            sp.wait_ge(act_s, nb)
            sp.dma_start(s_dram[0].rearrange("j k h e -> (j k h) e").rearrange("(q p) e -> p q e", p=P), turned[:]).then_inc(stored, 16)
            sp.wait_ge(act_s, 2 * nb)
            sp.dma_start(s_dram[1].rearrange("j k h e -> (j k h) e").rearrange("(q p) e -> p q e", p=P), turned[:]).then_inc(stored, 16)
            sp.wait_ge(act_s, 2 * nb + 1)
            sp.dma_start(g.dst_back.rearrange("(a c) e -> c a e", a=4), dturn[:]).then_inc(stored, 16)
            sp.wait_ge(stored, 48)
            for n, (way, half, _) in enumerate(plan):
                if n:
                    sp.wait_ge(dve, 2 + 4 * n)
                js = slice(half * HJ, half * HJ + HJ)
                d_rows = (g.win_dst if way == 0 else g.dst_back).rearrange("(j k) e -> j (k e)", k=KC)
                for hd in range(HEADS):
                    sp.dma_start(data[hd * HJ:(hd + 1) * HJ, :].rearrange("p (k e) -> p k e", k=KC), s_dram[way, js, :, hd]).then_inc(read, 16)
                    sp.dma_start(dst[hd * HJ:(hd + 1) * HJ, :], d_rows[js, :]).then_inc(read, 16)
                sp.wait_ge(dve, 2 + 4 * (n + 1))
                for hd in range(HEADS):
                    sp.dma_start(m_dram[way, js, :, hd], best[hd * HJ:(hd + 1) * HJ, :].rearrange("p (k e) -> p k e", k=KC)).then_inc(stored, 16)
                sp.wait_ge(stored, 48 + 16 * HEADS * (n + 1))
            sp.dma_start(turned[:], m_dram[0].rearrange("j k h e -> (j k h) e").rearrange("(q p) e -> p q e", p=P)).then_inc(read, 16)
            sp.wait_ge(pe_s, 3 * nb + 1)
            sp.dma_start(turned[:], m_dram[1].rearrange("j k h e -> (j k h) e").rearrange("(q p) e -> p q e", p=P)).then_inc(read, 16)

        @block.scalar
        def _(act):
            n = 0

            def take(dest, wait_store):
                nonlocal n
                for q, m in groups:
                    act.wait_ge(pe_s, n + 1)
                    if wait_store and q == 0:
                        act.wait_ge(stored, wait_store)
                    nc.scalar.activation(dest(q, m), t_ps[n % 2][:, 0:m], ACT.Copy).then_inc(act_s, 1)
                    n += 1
            take(lambda q, m: turned[:, q:q + m], 0)
            take(lambda q, m: turned[:, q:q + m], 16)
            act.wait_ge(pe_s, n + 1)
            nc.scalar.activation(dturn[:], t_ps[n % 2][0:CR], ACT.Copy).then_inc(act_s, 1)
            n += 1
            flat = lambda t: (lambda q, m: t[:, q * P:(q + m) * P].rearrange("p (a e) -> p a e", e=P))
            take(flat(g.high_l), 0)
            take(flat(g.high_r), 0)
            take(flat(rev), 0)
            act.wait_ge(dve, 2 + 4 * 4 + 2)
            nc.scalar.activation(score[:], g.high_r[:], ACT.Exp).then_inc(act_s, 1)

        @block.vector
        def _(v):
            for k in range(KC):
                last = nc.vector.tensor_copy(J4(rev[:])[:, :, k], J4(score[:])[:, :, KC - 1 - k])
            last.then_inc(dve, 1)
            for k in range(KC):
                last = nc.vector.tensor_copy(dst_rev[:].rearrange("p (j k) -> p j k", k=KC)[:, :, k],
                                             g.dst_col[:].rearrange("p (j k) -> p j k", k=KC)[:, :, KC - 1 - k])
            last.then_inc(dve, 1)
            for n, (way, half, loads) in enumerate(plan):
                v.wait_ge(read, 16 * loads)
                nc.vector.memset(new[:, 0:1], 0.0).then_inc(dve, 1)
                nc.vector.tensor_tensor(new[:, 1:WIN], dst[:, 1:WIN], dst[:, 0:WIN - 1], ALU.not_equal).then_inc(dve, 1)
                v.wait_ge(dve, 2 + 4 * n + 2)
                nc.vector.tensor_scalar(new[:], new[:], LOWEST / 3, None, ALU.mult).then_inc(dve, 1)
                v.wait_ge(dve, 2 + 4 * n + 3)
                nc.vector.tensor_tensor_scan(best[:], new[:], data[:], LOWEST / 3, ALU.add, ALU.max).then_inc(dve, 1)
                v.wait_ge(dve, 2 + 4 * n + 4)
                v.wait_ge(stored, 48 + 16 * HEADS * (n + 1))
            v.wait_ge(act_s, 5 * nb + 1)
            for k in range(KC):
                last = nc.vector.tensor_tensor(J4(g.high_l[:])[:, :, k], J4(g.high_l[:])[:, :, k], J4(rev[:])[:, :, KC - 1 - k], ALU.max)
            last.then_inc(dve, 1)
            v.wait_ge(dve, 2 + 16 + 1)
            nc.vector.tensor_tensor(g.high_r[:], score[:], g.high_l[:], ALU.subtract).then_inc(dve, 1)


def fast_attend(nc, g, weight, value):
    s = g.fs
    W68 = D + HEADS
    with ExitStack() as ctx:
        sb = lambda n, sh, d=F32: ctx.enter_context(nc.sbuf_tensor(f"fa_{n}", sh, d))
        two = lambda n, sh, d=F32: [sb(f"{n}{h}", sh, d) for h in range(2)]
        band_m, msg, agg = two("band_m", [P, KC, BAND, P]), two("msg", [P, KC, W68]), two("agg", [P, G7, W68])
        agg_ps = [ctx.enter_context(nc.psum_tensor(f"fa_agg_ps{h}", [P, G7, W68], F32)) for h in range(2)]
        block = ctx.enter_context(nc.Block())

        @block.vector
        def _(v):
            def pair(i):
                for h in range(2):
                    j = 2 * i + h
                    if not isinstance(i, int):
                        v.wait_ge(s.placed.sem, s.placed.at(j - 1))
                    for k in range(KC):
                        nc.vector.tensor_scalar(band_m[h][:, k].rearrange("p b e -> p (b e)"), g.iota_row[:],
                                                g.place[:, bass.ds(KC * j + k, 1)], None, ALU.is_equal)
                    w = weight[:, bass.ts(j, KC * HEADS)].rearrange("p (k h) -> p k h", k=KC)
                    for hd in range(HEADS):
                        r = slice(HD * hd, HD * hd + HD)
                        last = nc.vector.tensor_tensor(msg[h][:, :, r], value[:, bass.ts(j, KC * D)].rearrange("p (k d) -> p k d", k=KC)[:, :, r],
                                                       w[:, :, hd:hd + 1].to_broadcast([P, KC, HD]), ALU.mult)
                    last.then_inc(s.ready.sem, 1)
            turns(v, NJ // 2, pair)

        @block.tensor
        def _(pe):
            def pair(i):
                for h in range(2):
                    j = 2 * i + h
                    pe.wait_ge(s.ready.sem, s.ready.at(j + 1))
                    pe.wait_ge(s.summed.sem, s.summed.at(j + 1))
                    if not isinstance(i, int):
                        pe.wait_ge(s.agg.sem, s.agg.at(j - 1))
                    for q in range(G7):
                        chunks = [k for k in range(q - 1, q + 2) if k >= 0]
                        for k in chunks:
                            mm = nc.tensor.matmul(agg_ps[h][:, q], band_m[h][:, k, q - (k - 1)], msg[h][:, k], start=(k == chunks[0]),
                                                  stop=(k == chunks[-1]))
                    mm.then_inc(s.placed.sem, 1)
            turns(pe, NJ // 2, pair)

        @block.scalar
        def _(act):
            def pair(i):
                for h in range(2):
                    j = 2 * i + h
                    if not isinstance(i, int):
                        act.wait_ge(s.placed.sem, s.placed.at(j - 1))
                    nc.scalar.activation(msg[h][:, :, D:W68], weight[:, bass.ts(j, KC * HEADS)].rearrange("p (k h) -> p k h", k=KC),
                                         ACT.Copy).then_inc(s.summed.sem, 1)
                    act.wait_ge(s.placed.sem, s.placed.at(j + 1))
                    if not isinstance(i, int):
                        act.wait_ge(s.stored[h].sem, s.stored[h].at(16 * i))
                    nc.scalar.activation(agg[h][:], agg_ps[h][:], ACT.Copy).then_inc(s.agg.sem, 1)
                    act.wait_ge(s.agg.sem, s.agg.at(j + 1))
                    act.dma_start(node_view(g.acc68, j), agg[h][:]).then_inc(s.stored[h].sem, 16)
            turns(act, NJ // 2, pair)

        @block.sync
        def _(sp):
            for h in range(2):
                sp.wait_ge(s.stored[h].sem, s.stored[h].at(16 * (NJ // 2)))
    for sig in (s.ready, s.summed, s.placed, s.agg):
        sig.close(NJ)
    for h in range(2):
        s.stored[h].close(16 * (NJ // 2))
def setup_windows(nc, g, inp):
    with ExitStack() as ctx:
        sb = lambda n, s, d=F32: ctx.enter_context(nc.sbuf_tensor(f"sw_{n}", s, d))
        dst_i, dst_f, nxt_i, nxt_f = sb("dst_i", [P, ET], I32), sb("dst_f", [P, ET]), sb("nxt_i", [P, ET], I32), sb("nxt_f", [P, ET])
        first_i, first_f = sb("first_i", [P, NJ], I32), sb("first_f", [P, NJ])
        below, count, rise = sb("below", [P, ET]), sb("count", [P, NJ]), sb("rise", [P, 1])
        starts = sb("starts", [P, NJ], I32)
        with ExitStack() as c2:
            sem = lambda n: c2.enter_context(nc.semaphore(f"sw_{n}"))
            read, dve, summed, thr, copied = sem("read"), sem("dve"), sem("summed"), sem("thr"), sem("copied")
            s_ps = c2.enter_context(nc.psum_tensor("sw_s_ps", [P, NJ], F32))
            block = c2.enter_context(nc.Block())

            @block.gpsimd
            def _(pool):
                pool.iota(first_i[:], pattern=[[SN, NJ]], base=0, channel_multiplier=0).then_inc(thr, 1)

            @block.sync
            def _(sp):
                sp.dma_start(dst_i[:], inp["edges"][1, 0:EP].rearrange("(p t) -> p t", p=P)).then_inc(read, 16)
                sp.dma_start(nxt_i[:], inp["edges"][1, 1:EP + 1].rearrange("(p t) -> p t", p=P)).then_inc(read, 16)
                sp.wait_ge(dve, 7 + 2 * NJ)
                def window(j):
                    start = sp.value_load(starts[0:1, bass.ds(j, 1)], min_val=0, max_val=EP)
                    sp.dma_start(g.win_edges[bass.ts(j, KC), :, :], inp["edges"][:, bass.ds(start, WIN)].rearrange(
                        "a (k e) -> k a e", e=P)).then_inc(copied, 16)
                    sp.dma_start(g.win_feat[bass.ts(j, FE), :], g.feat_t[:, bass.ds(start, WIN)]).then_inc(copied, 16)
                turns(sp, NJ, window)
                sp.wait_ge(copied, 32 * NJ)

            @block.vector
            def _(v):
                v.wait_ge(read, 32)
                nc.vector.tensor_copy(dst_f[:], dst_i[:]).then_inc(dve, 1)
                nc.vector.tensor_copy(nxt_f[:], nxt_i[:]).then_inc(dve, 1)
                v.wait_ge(thr, 1)
                nc.vector.tensor_copy(first_f[:], first_i[:]).then_inc(dve, 1)
                v.wait_ge(dve, 3)
                nc.vector.tensor_tensor(nxt_f[:], nxt_f[:], dst_f[:], ALU.subtract).then_inc(dve, 1)
                v.wait_ge(dve, 4)
                nc.vector.tensor_reduce(rise[:], nxt_f[:], AX, ALU.min).then_inc(dve, 1)
                v.wait_ge(dve, 5)
                nc.vector.tensor_scalar(g.rising[:], rise[:], 0.0, None, ALU.is_ge).then_inc(dve, 1)
                v.wait_ge(dve, 6)

                def supertile(j):
                    nc.vector.tensor_scalar(below[:], dst_f[:], first_f[:, bass.ds(j, 1)], None, ALU.is_lt).then_inc(dve, 1)
                    v.wait_ge(dve, 2 * j + 7)
                    nc.vector.tensor_reduce(count[:, bass.ds(j, 1)], below[:], AX, ALU.add).then_inc(dve, 1)
                    v.wait_ge(dve, 2 * j + 8)
                turns(v, NJ, supertile)
                v.wait_ge(summed, 1)
                nc.vector.tensor_copy(starts[:], s_ps[:]).then_inc(dve, 1)

            @block.tensor
            def _(pe):
                pe.wait_ge(dve, 6 + 2 * NJ)
                nc.tensor.matmul(s_ps[:], g.ones[:], count[:], start=True, stop=True).then_inc(summed, 1)
    with ExitStack() as ctx:
        sb = lambda n, s, d=F32: ctx.enter_context(nc.sbuf_tensor(f"sx_{n}", s, d))
        pb = lambda n, s: ctx.enter_context(nc.psum_tensor(f"sx_{n}", s, F32))
        sem = lambda n: ctx.enter_context(nc.semaphore(f"sx_{n}"))
        rows_i, rows_f = sb("rows_i", [CR, 4, 4, P], I32), sb("rows_f", [CR, 4, 4, P])
        col = sb("col", [P, 4, NC])
        base_i, base_f, first_i, first_f = sb("base_i", [P, NC], I32), sb("base_f", [P, NC]), sb("first_i", [P, NC], I32), sb("first_f", [P, NC])
        a, b, own, rel, place = (sb(n, [P, NC]) for n in ("a", "b", "own", "rel", "place"))
        idx = sb("idx", [P, NJ, 3, KC], I32)
        kvf, pid1, src_m, total = sb("kvf", [P, NC]), sb("pid1", [P, 1]), sb("src_m", [P, NC]), sb("total", [P, 2])
        back = sb("back", [CR, 4, P])
        both = sb("both", [P, 2])
        fits_f, fits_i = sb("fits_f", [1, 2]), sb("fits_i", [1, 1], I32)
        read, dve, made, turned, act_done, stored, tabled = sem("read"), sem("dve"), sem("made"), sem("turned"), sem("act_done"), sem("stored"), sem("tabled")
        t_ps = [pb(f"t_ps{k}", [P, 4, CR]) for k in range(4)]
        b_ps, f_ps = pb("b_ps", [CR, 4, P]), pb("f_ps", [1, 2])
        block = ctx.enter_context(nc.Block())

        @block.gpsimd
        def _(pool):
            pool.iota(base_i[:], pattern=[[SN, NJ], [P, KC]], base=-P, channel_multiplier=0)
            pool.iota(first_i[:], pattern=[[SN, NJ], [0, KC]], base=0, channel_multiplier=0).then_inc(made, 1)

        @block.sync
        def _(sp):
            sp.dma_start(rows_i[:], g.win_edges.rearrange("(g c) a e -> c g a e", g=4)).then_inc(read, 16)
            sp.wait_ge(tabled, 1)
            sp.dma_start(g.win_idx.rearrange("(j p) w -> p j w", p=P), idx[:].rearrange("p j a k -> p j (a k)")).then_inc(stored, 16)
            sp.dma_start(g.win_dst.rearrange("(g c) e -> c g e", g=4), rows_f[:, :, 1]).then_inc(stored, 16)
            sp.dma_start(g.win_type.rearrange("(g c) e -> c g e", g=4), rows_f[:, :, 2]).then_inc(stored, 16)
            sp.wait_ge(act_done, 5)
            sp.dma_start(g.win_src.rearrange("(g c) e -> c g e", g=4), back[:]).then_inc(stored, 16)
            sp.wait_ge(stored, 64)

        @block.tensor
        def _(pe):
            pe.wait_ge(dve, 1)
            for k in range(4):
                for q in range(4):
                    mm = nc.tensor.matmul(t_ps[k][:, q], rows_f[:, q, k], g.ident[0:CR, 0:CR], start=True, stop=True)
            mm.then_inc(turned, 1)
            pe.wait_ge(tabled, 1)
            for q in range(4):
                mm = nc.tensor.matmul(b_ps[:, q], src_m[:, q * CR:(q + 1) * CR], g.ident[:], start=True, stop=True)
            mm.then_inc(turned, 1)
            nc.tensor.matmul(f_ps[:], g.ones[:, 0:1], both[:], start=True, stop=True).then_inc(turned, 1)

        @block.scalar
        def _(act):
            act.wait_ge(turned, 1)
            for k in range(4):
                nc.scalar.activation(col[:, k], t_ps[k][:].rearrange("p a b -> p (a b)"), ACT.Copy).then_inc(act_done, 1)
            act.wait_ge(turned, 2)
            nc.scalar.activation(back[:], b_ps[:], ACT.Copy).then_inc(act_done, 1)

        @block.vector
        def _(v):
            c = [0]

            def step(ins):
                c[0] += 1
                ins.then_inc(dve, 1)
                v.wait_ge(dve, c[0])
            v.wait_ge(read, 16)
            step(nc.vector.tensor_copy(rows_f[:], rows_i[:]))
            v.wait_ge(made, 1)
            step(nc.vector.tensor_copy(base_f[:], base_i[:]))
            step(nc.vector.tensor_copy(first_f[:], first_i[:]))
            v.wait_ge(act_done, 4)
            step(nc.vector.tensor_tensor(rel[:], col[:, 1], first_f[:], ALU.subtract))
            step(nc.vector.tensor_tensor(place[:], col[:, 1], base_f[:], ALU.subtract))
            step(nc.vector.tensor_scalar(a[:], rel[:], 0.0, None, ALU.is_ge))
            step(nc.vector.tensor_scalar(b[:], rel[:], float(SN), None, ALU.is_lt))
            step(nc.vector.tensor_tensor(own[:], a[:], b[:], ALU.mult))
            step(nc.vector.tensor_scalar(a[:], place[:], 0.0, None, ALU.is_ge))
            step(nc.vector.tensor_tensor(own[:], own[:], a[:], ALU.mult))
            step(nc.vector.tensor_scalar(b[:], place[:], float(BAND * P), None, ALU.is_lt))
            step(nc.vector.tensor_tensor(own[:], own[:], b[:], ALU.mult))
            step(nc.vector.scalar_tensor_tensor(a[:], place[:], 1.0, own[:], ALU.add, ALU.mult))
            step(nc.vector.tensor_scalar(g.place[:], a[:], -1.0, None, ALU.add))
            step(nc.vector.tensor_scalar(pid1[:], g.pid[:], 1.0, None, ALU.add))
            step(nc.vector.scalar_tensor_tensor(a[:], col[:, 0], pid1[:, 0:1], own[:], ALU.add, ALU.mult))
            step(nc.vector.tensor_scalar(src_m[:], a[:], pid1[:, 0:1], None, ALU.subtract))
            step(nc.vector.tensor_copy(g.src_m[:], src_m[:]))
            step(nc.vector.tensor_copy(g.dst_col[:], col[:, 1]))
            step(nc.vector.scalar_tensor_tensor(kvf[:], col[:, 0], 2.0, col[:, 3], ALU.mult, ALU.add))
            step(nc.vector.tensor_copy(idx[:, :, 0], col[:, 0].rearrange("p (j k) -> p j k", k=KC)))
            step(nc.vector.tensor_copy(idx[:, :, 1], kvf[:].rearrange("p (j k) -> p j k", k=KC)))
            step(nc.vector.tensor_scalar(kvf[:], col[:, 1], float(NP - 1), None, ALU.min))
            step(nc.vector.tensor_copy(idx[:, :, 2], kvf[:].rearrange("p (j k) -> p j k", k=KC)))
            step(nc.vector.tensor_reduce(both[:, 0:1], own[:], AX, ALU.add))
            nc.vector.tensor_copy(both[:, 1:2], g.rising[:]).then_inc(tabled, 1)
            v.wait_ge(turned, 3)
            nc.vector.tensor_scalar(fits_f[:, 0:1], f_ps[:, 0:1], float(EP), None, ALU.is_equal).then_inc(dve, 1)
            nc.vector.tensor_scalar(fits_f[:, 1:2], f_ps[:, 1:2], float(P), None, ALU.is_equal).then_inc(dve, 1)
            v.wait_ge(dve, c[0] + 2)
            nc.vector.tensor_tensor(g.fits[:], fits_f[:, 0:1], fits_f[:, 1:2], ALU.mult)
def setup_constants(nc, g, inp):
    with ExitStack() as ctx:
        sb = lambda n, s, d=F32: ctx.enter_context(nc.sbuf_tensor(f"su_{n}", s, d))
        pb = lambda n, s: ctx.enter_context(nc.psum_tensor(f"su_{n}", s, F32))
        sem = lambda n: ctx.enter_context(nc.semaphore(f"su_{n}"))
        weights_in, edges_in, stored = sem("weights_in"), sem("edges_in"), sem("stored")
        zeroed, made, act_done, pe_done, dve = sem("zeroed"), sem("made"), sem("act_done"), sem("pe_done"), sem("dve")
        kt, vt = sb("kt", [D, 2, D]), sb("vt", [D, 2, D])
        rel = sb("rel", [D, 2, 2, D])
        relk, pri, skip = sb("relk", [D, 2, D]), sb("pri", [D, 2, D]), sb("skip", [P, 2])
        sig, dsig = sb("sig", [P, 2]), sb("dsig", [P, 1])
        w33u, u0, b33 = sb("w33u", [D, D]), sb("u0", [D, 1]), sb("b33", [D, 1])
        QR = NT // 4
        nt_i, nt_f = sb("nt_i", [QR, 4, P], I32), sb("nt_f", [QR, 4, P])
        raw = sb("raw", [P, 4, ET], I32)
        as_f = sb("as_f", [P, 4, ET])
        kvf = sb("kvf", [P, ET])
        ei, ec = sb("ei", [P, ET, 3], I32), sb("ec", [P, ET, 4])
        fold_ps, c_ps, t_ps = pb("fold_ps", [P, 2, 2, D]), pb("c_ps", [D, 1]), pb("t_ps", [P, 4, QR])
        NW = [0]
        block = ctx.enter_context(nc.Block())

        @block.sync
        def _(sp):
            for k in range(4):
                sp.dma_start(raw[:, k], inp["edges"][k, 0:EP].rearrange("(p t) -> p t", p=P)).then_inc(edges_in, 16)
            sp.dma_start(nt_i[:], inp["node_type_2"].rearrange("(a b p) -> b a p", a=4, p=P)).then_inc(edges_in, 16)
            sp.wait_ge(zeroed, 1)

            def load(dst, src):
                sp.dma_start(dst, src).then_inc(weights_in, 16)
                NW[0] += 1
            W, B = inp["L0_gnn_weights"], inp["L0_gnn_biases"]
            for layer in range(3):
                for d in range(2):
                    base = R9 * (1 - d)
                    load(g.w0[0:D, layer, d], W[layer, base:base + R9:2].rearrange("g e f -> e g f"))
                    load(g.w0[D:P, layer, d, 0:NPAIR - 1], W[layer, base + 1:base + R9:2].rearrange("g e f -> e g f"))
                    load(g.b0[:, layer, d], B[layer, base:base + R9])
            col = lambda a: a.rearrange("(c a) -> c a", a=1)
            row = lambda a: a.rearrange("(a c) -> a c", a=1)
            load(g.w1[:], inp["L1_gnn_W1"])
            load(g.w2[:], inp["L1_gnn_W2"])
            load(g.w3[:], inp["L1_gnn_W3"])
            load(g.cb1[:], col(inp["L1_gnn_b1"]))
            load(g.gb1[:, 0:1], col(inp["L1_gnn_g1"]))
            load(g.gb1[:, 1:2], col(inp["L1_gnn_be1"]))
            load(g.cb2[:], col(inp["L1_gnn_b2"]))
            load(g.gb2[:, 0:1], col(inp["L1_gnn_g2"]))
            load(g.gb2[:, 1:2], col(inp["L1_gnn_be2"]))
            load(g.cb3[:], inp["L1_gnn_b3"].partition_broadcast(P))
            load(kt[:], inp["WkT"].rearrange("t o i -> o t i"))
            load(vt[:], inp["WvT"].rearrange("t o i -> o t i"))
            load(g.wqkv[:, 0:D], inp["L2_gnn_Wq"].rearrange("t i o -> (t i) o"))
            load(g.wa[:], inp["L2_gnn_Wa"].rearrange("t i o -> (t i) o"))
            for h in range(HEADS):
                b = slice(HD * h, HD * h + HD)
                load(rel[b, 0, :, b], inp["L2_gnn_Ratt"][h].rearrange("t d f -> d t f"))
                load(rel[b, 1, :, b], inp["L2_gnn_Rmsg"][h].rearrange("t d f -> d t f"))
            load(pri[:], inp["pri_rows"].partition_broadcast(D))
            load(skip[:], inp["L2_gnn_skip"].partition_broadcast(P))
            load(g.w31x[:], inp["L3_gnn_W1"][0:D, :])
            load(g.w31e[:], inp["L3_gnn_W1"][D:D + FE, :])
            load(g.b31[:], col(inp["L3_gnn_b1"]))
            load(g.w32[:], inp["L3_gnn_W2"])
            load(g.b32[:], inp["L3_gnn_b2"].partition_broadcast(P))
            load(g.w33[:], inp["L3_gnn_W3"][0:P, :])
            load(w33u[:], inp["L3_gnn_W3"][P:P + D, :])
            load(u0[:], inp["L3_gnn_u"][0:1, :].rearrange("a c -> c a"))
            load(b33[:], col(inp["L3_gnn_b3"]))
            load(g.w34[:], inp["L3_gnn_W4"])
            load(g.b34[:], inp["L3_gnn_b4"].partition_broadcast(P))
            n = 0
            for a in (g.acc, *(b for two in g.back for b in two), g.acc68, g.count):
                sp.dma_start(a[NP:NR, :], g.zeros[:, 0:a.shape[1]]).then_inc(stored, 16)
                n += 1
            sp.wait_ge(zeroed, 2)
            sp.dma_start(g.high[NP:NR, :], g.lowest[:, 0:HEADS]).then_inc(stored, 16)
            sp.wait_ge(made, 1)
            sp.dma_start(g.edge_i.rearrange("(p t) c -> p (t c)", p=P), ei[:].rearrange("p t c -> p (t c)")).then_inc(stored, 16)
            sp.dma_start(g.edge_cols.rearrange("(p t) c -> p (t c)", p=P), ec[:].rearrange("p t c -> p (t c)")).then_inc(stored, 16)
            sp.dma_start(g.edge_rows.rearrange("c (p t) -> p c t", p=P), as_f[:, 0:3]).then_inc(stored, 16)
            sp.wait_ge(stored, 16 * (n + 4))

        @block.gpsimd
        def _(pool):
            pool.iota(g.pid_i[:], pattern=[[0, 1]], base=0, channel_multiplier=1).then_inc(g.pool_made, 1)
            pool.iota(g.iota_i[:], pattern=[[1, 3 * P]], base=0, channel_multiplier=0).then_inc(g.pool_made, 1)
            pool.memset(g.ident[:], 0.0)
            pool.memset(g.ones[:], 1.0)
            pool.memset(g.before[:], 1.0).then_inc(g.pool_made, 1)
            pool.wait_ge(g.pool_made, 3)
            pool.affine_select(out=g.ident[:], in_=g.ident[:], compare_op=ALU.not_equal, fill=1.0, base=0,
                               pattern=[[-1, P]], channel_multiplier=1).then_inc(g.pool_made, 1)
            pool.affine_select(out=g.before[:], in_=g.before[:], compare_op=ALU.is_gt, fill=0.0, base=0,
                               pattern=[[-1, P]], channel_multiplier=1).then_inc(g.pool_made, 1)

        @block.vector
        def _(v):
            nc.vector.memset(g.zeros[:], 0.0)
            nc.vector.memset(g.eps[:], EPS)
            nc.vector.memset(g.w0[:].rearrange("p a b c d -> p (a b c d)"), 0.0)
            nc.vector.memset(rel[:].rearrange("p a b c -> p (a b c)"), 0.0).then_inc(zeroed, 1)
            nc.vector.memset(g.lowest[:], LOWEST).then_inc(zeroed, 1)
            c = [0]

            def step(ins):
                c[0] += 1
                ins.then_inc(dve, 1)
                v.wait_ge(dve, c[0])
            for j in range(NPAIR):
                nc.vector.memset(g.type_of_row[0:D, j:j + 1], float(2 * j))
                step(nc.vector.memset(g.type_of_row[D:P, j:j + 1], float(2 * j + 1) if 2 * j + 1 < R9 else -1.0))
            v.wait_ge(g.pool_made, 5)
            nc.vector.tensor_copy(g.pid[:], g.pid_i[:])
            step(nc.vector.tensor_copy(g.iota_row[:], g.iota_i[:]))
            step(nc.vector.tensor_scalar(g.dump_row[:], g.pid[:], float(NP), None, ALU.add))
            v.wait_ge(edges_in, 16 * 5)
            step(nc.vector.tensor_copy(as_f[:], raw[:]))
            step(nc.vector.scalar_tensor_tensor(kvf[:], as_f[:, 0], 2.0, as_f[:, 3], ALU.mult, ALU.add))
            nc.vector.tensor_copy(ei[:, :, 0], raw[:, 0])
            nc.vector.tensor_copy(ei[:, :, 1], raw[:, 1])
            nc.vector.tensor_copy(ei[:, :, 2], kvf[:])
            for k in range(4):
                last = nc.vector.tensor_copy(ec[:, :, k], as_f[:, k])
            last.then_inc(made, 1)
            step(nc.vector.tensor_copy(nt_f[:], nt_i[:]))
            v.wait_ge(weights_in, 16 * NW[0])
            step(nc.vector.tensor_scalar(rel[:, 0], rel[:, 0], 1.0 / float(HD) ** 0.5, None, ALU.mult))
            nc.vector.tensor_tensor(relk[:], rel[:, 0], pri[:], ALU.mult).then_inc(made, 1)
            v.wait_ge(pe_done, 1)
            nc.vector.tensor_tensor(g.c3[:], c_ps[:], b33[:], ALU.add)
            step(nc.vector.tensor_copy(g.type1[:], t_ps[:].rearrange("p a b -> p (a b)")))
            v.wait_ge(act_done, 1)
            step(nc.vector.tensor_tensor(dsig[:], sig[:, 1:2], sig[:, 0:1], ALU.subtract))
            step(nc.vector.tensor_scalar(g.alpha[:], g.type1[:], dsig[:, 0:1], sig[:, 0:1], ALU.mult, ALU.add))
            nc.vector.tensor_scalar(g.beta[:], g.alpha[:], -1.0, 1.0, ALU.mult, ALU.add)

        @block.tensor
        def _(pe):
            pe.wait_ge(made, 2)
            pe.wait_ge(g.pool_made, 5)
            for t in range(2):
                for k, wt in enumerate((kt, vt)):
                    for r in range(2):
                        rhs = relk[:, r] if k == 0 else rel[:, 1, r]
                        nc.tensor.matmul(fold_ps[64 * t:64 * t + 64, r, k], wt[:, t], rhs, start=True, stop=True)
            nc.tensor.matmul(c_ps[:], w33u[:], u0[:], start=True, stop=True)
            for a in range(4):
                mm = nc.tensor.matmul(t_ps[:, a], nt_f[:, a], g.ident[0:QR, 0:QR], start=True, stop=True)
            mm.then_inc(pe_done, 1)

        @block.scalar
        def _(act):
            act.wait_ge(weights_in, 16 * NW[0])
            nc.scalar.activation(sig[:], skip[:], ACT.Sigmoid).then_inc(act_done, 1)
            act.wait_ge(pe_done, 1)
            nc.scalar.activation(g.wqkv[:, D:5 * D], fold_ps[:].rearrange("p a b c -> p (a b c)"), ACT.Copy)


def find_leaders(nc, g):
    with ExitStack() as ctx:
        sb = lambda n, s, d=F32: ctx.enter_context(nc.sbuf_tensor(f"fl_{n}", s, d))
        s = g.ls
        U = 8
        rows = [sb(f"rows{h}", [P, 2, U * P]) for h in range(2)]
        cols = [sb(f"cols{h}", [P, U, 4]) for h in range(2)]
        same, junk = sb("same", [P, P]), sb("junk", [P, P])
        prev, move, later = sb("prev", [P, U, 2]), sb("move", [P, U, 2]), sb("later", [P, U, 2])
        lead_f = sb("lead_f", [P, U, 2])
        lead_i = [sb(f"lead_i{h}", [P, U, 2], I32) for h in range(2)]
        TURNS = ET // U
        assert TURNS * U == ET and TURNS % 2 == 1
        chain = Chain(s.chain)
        block = ctx.enter_context(nc.Block())

        def pairs(eng, body):
            body(0, 0, 0)
            body(1, 0, 1)
            with eng.Fori(1, TURNS // 2) as i:
                body(2 * i, i, 0)
                body(2 * i + 1, i, 1)
            body(TURNS - 1, TURNS // 2, 0)

        @block.sync
        def _(sp):
            def turn(n, i, h):
                first = isinstance(i, int) and i == 0
                if not first:
                    sp.wait_ge(s.ready.sem, s.ready.at(n - 1)).then_inc(g.sp_gate, 1)
                e = bass.ts(n, U * P)
                sp.dma_start(rows[h][:], g.edge_rows[0:2, e].partition_broadcast(P)).then_inc(s.loaded[h].sem, 16)
                sp.dma_start(cols[h][:], g.edge_cols[e, :].rearrange("(u p) c -> p u c", p=P)).then_inc(s.loaded[h].sem, 16)
            pairs(sp, turn)
            sp.wait_ge(s.stored[0].sem, s.stored[0].at(16 * (TURNS // 2 + 1)))
            sp.wait_ge(s.stored[1].sem, s.stored[1].at(16 * (TURNS // 2)))

        @block.vector
        def _(dve):
            def turn(n, i, h):
                first = isinstance(i, int) and i == 0
                dve.wait_ge(s.loaded[h].sem, s.loaded[h].at(32 * (i + 1)))
                if not first:
                    dve.wait_ge(s.stored[h].sem, s.stored[h].at(16 * i))
                chain.turn(n)
                for u in range(U):
                    for d in range(2):
                        chain.link(dve, nc.vector.tensor_scalar(same[:], rows[h][:, 1 - d, u * P:(u + 1) * P], cols[h][:, u, 1 - d:2 - d],
                                                                None, ALU.is_equal))
                        chain.link(dve, nc.vector.tensor_tensor_reduce(junk[:], same[:], g.before[:], 1.0, 0.0, ALU.mult, ALU.add,
                                                                       prev[:, u, d:d + 1]))
                chain.link(dve, nc.vector.tensor_scalar(later[:], prev[:], 0.0, None, ALU.is_gt))
                for d in range(2):
                    last = nc.vector.tensor_scalar(move[:, :, d], cols[h][:, :, 1 - d], -1.0, g.dump_row[:, 0:1], ALU.mult, ALU.add)
                chain.link(dve, last)
                chain.link(dve, nc.vector.tensor_tensor(move[:], move[:], later[:], ALU.mult))
                for d in range(2):
                    last = nc.vector.tensor_tensor(lead_f[:, :, d], cols[h][:, :, 1 - d], move[:, :, d], ALU.add)
                chain.link(dve, last)
                nc.vector.tensor_copy(lead_i[h][:], lead_f[:]).then_inc(s.ready.sem, 1)
                dve.wait_ge(s.ready.sem, s.ready.at(n + 1))
            pairs(dve, turn)

        @block.scalar
        def _(act):
            def turn(n, i, h):
                first = isinstance(i, int) and i == 0
                act.wait_ge(s.ready.sem, s.ready.at(n + 1))
                act.dma_start(g.lead[bass.ts(n, U * P), :].rearrange("(u p) c -> p u c", p=P), lead_i[h][:]).then_inc(s.stored[h].sem, 16)
            pairs(act, turn)
    s.ready.close(TURNS)
    chain.close(TURNS)
    s.loaded[0].close(32 * (TURNS // 2 + 1))
    s.loaded[1].close(32 * (TURNS // 2))
    s.stored[0].close(16 * (TURNS // 2 + 1))
    s.stored[1].close(16 * (TURNS // 2))


def fill_tables(nc, g, name, tables):
    with ExitStack() as ctx:
        filled = ctx.enter_context(nc.semaphore(f"{name}_filled"))
        block = ctx.enter_context(nc.Block())

        @block.sync
        def _(sp):
            for table in tables:
                width = G7 * table.shape[1]
                source = (g.lowest if table is g.high else g.zeros)[:, 0:width]
                with sp.Fori(0, NJ) as j:
                    sp.dma_start(table[bass.ts(j, SN), :].rearrange("(p q) d -> p (q d)", p=P), source).then_inc(filled, 16)
            sp.wait_ge(filled, 16 * NJ * len(tables))


def degrees(nc, g):
    with ExitStack() as ctx:
        QR = NT // 4
        rows = ctx.enter_context(nc.sbuf_tensor("dg_rows", [QR, 4, P], F32))
        t_ps = ctx.enter_context(nc.psum_tensor("dg_ps", [P, 4, QR], F32))
        read, turned = (ctx.enter_context(nc.semaphore(f"dg_{n}")) for n in ("read", "turned"))
        block = ctx.enter_context(nc.Block())

        @block.sync
        def _(sp):
            sp.dma_start(rows[:], g.count[0:NP, :].rearrange("(a b p) o -> b a (p o)", a=4, p=P)).then_inc(read, 16)

        @block.tensor
        def _(pe):
            pe.wait_ge(read, 16)
            for a in range(4):
                mm = nc.tensor.matmul(t_ps[:, a], rows[:, a], g.ident[0:QR, 0:QR], start=True, stop=True)
            mm.then_inc(turned, 1)

        @block.vector
        def _(v):
            v.wait_ge(turned, 1)
            nc.vector.tensor_copy(g.indegree[:], t_ps[:].rearrange("p a b -> p (a b)"))


def inverse_degrees(nc, g):
    with ExitStack() as ctx:
        most, root = (ctx.enter_context(nc.sbuf_tensor(f"dg_{n}", [P, NT], F32)) for n in ("most", "root"))
        rooted, dve = (ctx.enter_context(nc.semaphore(f"dg_{n}")) for n in ("rooted", "dve"))
        block = ctx.enter_context(nc.Block())

        @block.vector
        def _(v):
            nc.vector.tensor_scalar(most[:], g.indegree[:], 1.0, None, ALU.max).then_inc(dve, 1)
            v.wait_ge(dve, 1)
            nc.vector.reciprocal(g.rcount[:], most[:])
            v.wait_ge(rooted, 1)
            nc.vector.reciprocal(g.dinv[:], root[:])

        @block.scalar
        def _(act):
            nc.scalar.activation(root[:], g.indegree[:], ACT.Sqrt, bias=g.ones[:, 0:1]).then_inc(rooted, 1)


def all_engines(nc, g):
    with ExitStack() as ctx:
        block = ctx.enter_context(nc.Block())

        @block.sync
        def _(sp):
            sp.nop()

        @block.gpsimd
        def _(pool):
            pool.nop()

        @block.tensor
        def _(pe):
            pe.nop()

        @block.vector
        def _(v):
            v.nop()

        @block.scalar
        def _(act):
            act.nop()


def program(nc, inp, out):
    with ExitStack() as ctx:
        g = Env()
        sb = lambda n, s, d=F32: ctx.enter_context(nc.sbuf_tensor(n, s, d))
        dram = lambda n, s, d=F32: nc.dram_tensor(n, s, d, kind="Internal").ap()
        g.x, g.feat_t, g.out = inp["x"], inp["feat_t"], out
        g.T2 = dram("T2", [NP, 2 * D])
        g.T0, g.X, g.UT = dram("T0", [NP, D]), dram("X", [NP, D]), dram("UT", [P, NP])
        g.acc = dram("acc", [NR, D])
        g.back = [[dram(f"back{n}{k}", [NR, D]) for k in range(2)] for n in range(3)]
        g.win_edges, g.win_feat = dram("win_edges", [NC, 4, P], I32), dram("win_feat", [NJ * FE, WIN])
        g.win_idx, g.win_lead = dram("win_idx", [NJ * P, 3 * KC], I32), dram("win_lead", [NJ * P, KC], I32)
        g.win_dst, g.win_type, g.win_src, g.dst_back = (dram(n, [NC, P]) for n in ("win_dst", "win_type", "win_src", "dst_back"))
        g.win_mask, g.win_onehot = dram("win_mask", [NJ * P, KC * NPAIR * P], U8), dram("win_onehot", [NJ * R9, WIN])
        g.s_rows, g.m_rows = (dram(n, [2, NJ, KC, HEADS, P]) for n in ("s_rows", "m_rows"))
        g.place, g.src_m, g.dst_col, g.indegree = sb("place", [P, NC]), sb("src_m", [P, NC]), sb("dst_col", [P, NC]), sb("indegree", [P, NT])
        g.rising, g.fits = sb("rising", [P, 1]), sb("fits", [1, 1], I32)
        g.acc68, g.count, g.high = dram("acc68", [NR, D + HEADS]), dram("count", [NR, 1]), dram("high", [NR, HEADS])
        g.Q, g.KV = dram("Q", [NP, D]), dram("KV", [NP, 4 * D])
        g.KV2 = g.KV.rearrange("n (r c) -> (n r) c", r=2)
        g.edge_i, g.lead = dram("edge_i", [EP, 3], I32), dram("lead", [EP, 2], I32)
        g.edge_cols, g.edge_rows = dram("edge_cols", [EP, 4]), dram("edge_rows", [3, EP])
        g.pid_i, g.iota_i = sb("pid_i", [P, 1], I32), sb("iota_i", [P, 3 * P], I32)
        g.pid, g.iota_row, g.dump_row = sb("pid", [P, 1]), sb("iota_row", [P, 3 * P]), sb("dump_row", [P, 1])
        g.eps = sb("eps", [P, 1])
        g.ident, g.ones, g.before = sb("ident", [P, P]), sb("ones", [P, P]), sb("before", [P, P])
        g.zeros, g.lowest, g.type_of_row = sb("zeros", [P, G7 * (D + HEADS)]), sb("lowest", [P, G7 * HEADS]), sb("type_of_row", [P, NPAIR])
        g.w0, g.b0 = sb("w0", [P, 3, 2, NPAIR, D]), sb("b0", [R9, 3, 2, D])
        g.w1, g.w2, g.w3 = sb("w1", [D, P]), sb("w2", [P, D]), sb("w3", [D, D])
        g.cb1, g.gb1, g.cb2, g.gb2, g.cb3 = sb("cb1", [P, 1]), sb("gb1", [P, 2]), sb("cb2", [D, 1]), sb("gb2", [D, 2]), sb("cb3", [P, D])
        g.mv, g.bn = sb("mv", [P, 2]), sb("bn", [P, 4])
        g.wqkv, g.wa = sb("wqkv", [P, 5 * D]), sb("wa", [P, D])
        g.w31x, g.w31e, g.b31, g.w32, g.b32 = sb("w31x", [D, P]), sb("w31e", [FE, P]), sb("b31", [P, 1]), sb("w32", [P, D]), sb("b32", [P, D])
        g.w33, g.c3, g.w34, g.b34 = sb("w33", [P, D]), sb("c3", [D, 1]), sb("w34", [D, D]), sb("b34", [P, D])
        g.type1, g.alpha, g.beta, g.dinv, g.rcount = (sb(n, [P, NT]) for n in ("type1", "alpha", "beta", "dinv", "rcount"))
        g.sp_gate = ctx.enter_context(nc.semaphore("sp_gate"))
        g.pool_made = ctx.enter_context(nc.semaphore("pool_made"))
        g.ns, g.gs = Env(), Env()
        sg = lambda n: Signal(nc, ctx, n)
        n_, e_ = g.ns, g.gs
        n_.ready = sg("n_ready")
        n_.out = sg("n_out")
        n_.out2 = sg("n_out2")
        n_.turned = sg("n_turned")
        n_.half = sg("n_half")
        n_.product = sg("n_product")
        n_.chain = sg("n_chain")
        n_.stat = sg("n_stat")
        n_.squares = sg("n_squares")
        n_.root = sg("n_root")
        g.ns.loaded = [Signal(nc, ctx, f"n_loaded{h}") for h in range(2)]
        g.ns.stored = [Signal(nc, ctx, f"n_stored{h}") for h in range(2)]
        e_.loaded = sg("g_loaded")
        e_.gate = sg("g_gate")
        e_.summed = sg("g_summed")
        e_.turned = sg("g_turned")
        e_.masked = sg("g_masked")
        e_.product = sg("g_product")
        e_.msg = sg("g_msg")
        e_.joined = sg("g_joined")
        e_.chain = sg("g_chain")
        g.gs.gathered = [Signal(nc, ctx, f"g_gathered{d}") for d in range(3)]
        g.gs.scattered = [Signal(nc, ctx, f"g_scattered{d}") for d in range(2)]

        g.ls = Env()
        g.ls.ready, g.ls.chain = sg("l_ready"), sg("l_chain")
        g.ls.loaded, g.ls.stored = ([sg(f"l_{n}{h}") for h in range(2)] for n in ("loaded", "stored"))
        g.fs = f_ = Env()
        for_fast = lambda n: Signal(nc, ctx, f"f_{n}")
        f_.ready = for_fast("ready")
        f_.chain = for_fast("chain")
        f_.gate = for_fast("gate")
        f_.turned = for_fast("turned")
        f_.band = for_fast("band")
        f_.band_t = for_fast("band_t")
        f_.band_turned = for_fast("band_turned")
        f_.picked = for_fast("picked")
        f_.masked_f = for_fast("masked_f")
        f_.masked_r = for_fast("masked_r")
        f_.product_f = for_fast("product_f")
        f_.product_r = for_fast("product_r")
        f_.msg_f = for_fast("msg_f")
        f_.columns = for_fast("columns")
        f_.returned = for_fast("returned")
        f_.same = for_fast("same")
        f_.joined = for_fast("joined")
        f_.summed = for_fast("summed")
        f_.placed = for_fast("placed")
        f_.agg = for_fast("agg")
        f_.zeroed = for_fast("zeroed")
        f_.ones = for_fast("ones")
        f_.half = for_fast("half")
        f_.hidden = for_fast("hidden")
        f_.loaded, f_.stored, f_.indices = ([for_fast(f"{n}{h}") for h in range(2)] for n in ("loaded", "stored", "indices"))
        f_.gathered, f_.gathered_near, f_.scattered = ([for_fast(f"{n}{k}") for k in range(KC)] for n in ("gathered", "near", "scattered"))

        setup_constants(nc, g, inp)
        setup_windows(nc, g, inp)
        stage_norm(nc, g, "n0", True, [])
        fits = nc.values_load(g.fits[:], min_val=0, max_val=1)
        with nc.If(fits):
            all_engines(nc, g)
            fast_tables(nc, g)
            fast_transform_edges(nc, g, 0)
        with nc.Else():
            all_engines(nc, g)
            find_leaders(nc, g)
            fill_tables(nc, g, "z0", [g.acc, *g.back[0], g.count])
            general_sum_edges(nc, g, "gc", None, g.count, 1, count=True)
            general_transform_edges(nc, g, 0)
            degrees(nc, g)
        inverse_degrees(nc, g)
        for layer in (1, 2):
            stage_norm(nc, g, f"n1{layer}", False, [g.acc, *g.back[layer - 1]])
            with nc.If(fits):
                fast_transform_edges(nc, g, layer)
            with nc.Else():
                all_engines(nc, g)
                fill_tables(nc, g, f"z0{layer}", [g.acc, *g.back[layer]])
                general_transform_edges(nc, g, layer)
        stage_first_residual(nc, g)
        for n, channels, weight in ((1, P, g.w2[:]), (2, D, g.w3[:]), (3, None, None)):
            with nc.If(fits):
                fast_sum_edges(nc, g, f"f{n}", g.T0)
            with nc.Else():
                all_engines(nc, g)
                fill_tables(nc, g, f"z1{n}", [g.acc])
                general_sum_edges(nc, g, f"g{n}", g.T0, g.acc, D)
            if channels:
                stage_conv_stats(nc, g, f"s{n}", channels)
                stage_conv_next(nc, g, f"t{n}", channels, weight)
        stage_typed(nc, g)
        with nc.If(fits):
            all_engines(nc, g)
            with ExitStack() as c2:
                score = c2.enter_context(nc.sbuf_tensor("score", [P, NC * HEADS], F32))
                with ExitStack() as c3:
                    value = c2.enter_context(nc.sbuf_tensor("value", [P, NC * D], F32))
                    fast_scores(nc, g, score, value)
                    g.high_l, g.high_r = (c3.enter_context(nc.sbuf_tensor(n, [P, NC * HEADS], F32)) for n in ("high_l", "high_r"))
                    fast_weights(nc, g, score)
                fast_attend(nc, g, score, value)
        with nc.Else():
            all_engines(nc, g)
            fill_tables(nc, g, "z2", [g.acc68, g.high])
            general_scores(nc, g)
            general_attend(nc, g)
        stage_attended(nc, g)
        with nc.If(fits):
            fast_sum_edges(nc, g, "f4", g.T0, mlp=True)
        with nc.Else():
            all_engines(nc, g)
            fill_tables(nc, g, "z3", [g.acc])
            general_sum_edges(nc, g, "g4", g.T0, g.acc, D, mlp=True)
        stage_last(nc, g)


def kernel(**inputs):
    import numpy as np
    import concourse.bacc as bacc
    from concourse import mybir as mb
    from concourse.bass_utils import run_bass_kernel_spmd

    a = {k: np.asarray(v) for k, v in inputs.items()}
    pad = NP - N
    none = np.zeros(WIN, np.int32)
    own = np.arange(N, NP, dtype=np.int32)
    lay = {"x": np.concatenate([a["x"], np.zeros((pad, D), np.float32)]),
           "edges": np.stack([np.concatenate([a["src"], own, none]), np.concatenate([a["dst"], own, np.full(WIN, 1 << 20, np.int32)]),
                              np.concatenate([a["edge_type_9"], none[:pad], none]), np.concatenate([a["edge_type_2"], none[:pad], none])]),
           "feat_t": np.concatenate([a["edge_attr_32"], np.zeros((pad + WIN, FE), np.float32)]).T,
           "WkT": a["L2_gnn_Wk"].transpose(0, 2, 1), "WvT": a["L2_gnn_Wv"].transpose(0, 2, 1),
           "pri_rows": np.repeat(a["L2_gnn_pri"].T, HD, axis=1).reshape(-1)}
    lay["node_type_2"] = np.concatenate([a["node_type_2"], np.zeros(pad, np.int32)])
    for n, v in a.items():
        if n[:2] in ("L0", "L1", "L2", "L3") and n not in ("L2_gnn_Wk", "L2_gnn_Wv", "L2_gnn_pri"):
            lay[n] = v
    nc = bacc.Bacc("TRN2", target_bir_lowering=False, num_devices=1)
    arrays, inp = {}, {}
    for n, v in lay.items():
        arrays[f"in_{n}"] = np.ascontiguousarray(v)
        inp[n] = nc.dram_tensor(f"in_{n}", v.shape, mb.dt.from_np(v.dtype), kind="ExternalInput").ap()
    out = nc.dram_tensor("out", (NP, D), mb.dt.float32, kind="ExternalOutput").ap()
    program(nc, inp, out)
    r = run_bass_kernel_spmd(nc, [arrays], core_ids=[0])
    return r.results[0]["out"][:N]
```
